# Optimizing a Trainium2 kernel written in Bass

```python
import numpy as np
import jax
import jax.numpy as jnp

def _softmax(x, axis=-1):
    return jax.nn.softmax(x, axis=axis)

def _gelu(x):
    return jax.nn.gelu(x, approximate=True)

def _silu(x):
    return jax.nn.silu(x)

def _sigmoid(x):
    return jax.nn.sigmoid(x)

def _layernorm(x, axis=-1, eps=1e-05):
    m = jnp.mean(x, axis=axis, keepdims=True)
    v = jnp.var(x, axis=axis, keepdims=True)
    return (x - m) / jnp.sqrt(v + eps)

def _scatter_add(tgt, idx, src, axis=0):
    return tgt.at[idx].add(src)

def _segment_sum(src, seg, n):
    return jax.ops.segment_sum(src, seg, n)
kernel_name = 'mk_decoder_preln_d2_seqx_r4_ae78ef'

def setup_inputs(seed: int=0):
    np.random.seed(seed)
    _w = jnp.asarray

    def _rec_inputs():
        import jax
        import jax.numpy as jnp
        _rk = jax.random.key(seed)
        x = -0.0003929 + 0.9999 * jax.random.normal(jax.random.fold_in(_rk, 1), (64, 256, 256), jnp.float32)
        _lenS = 256 - jax.random.randint(jax.random.fold_in(_rk, 7), (64,), 0, max(1, 256 // 4) + 1, jnp.int32)
        _lenS2 = 77 - jax.random.randint(jax.random.fold_in(_rk, 8), (64,), 0, max(1, 77 // 4) + 1, jnp.int32)
        _ctx_1024P = jax.random.normal(jax.random.fold_in(_rk, 11), (64, 16, 256), jnp.float32)
        _ctx_1024c = jax.random.dirichlet(jax.random.fold_in(_rk, 511), 0.3 * jnp.ones((16,), jnp.float32), (64, 77))
        _ctx_1024t = jnp.einsum('bsk,bkd->bsd', _ctx_1024c, _ctx_1024P)
        _ctx_1024t = _ctx_1024t * jax.lax.rsqrt(jnp.mean(jnp.square(_ctx_1024t)) + 1e-12) * 0.953939
        ctx_1024 = 4.13588e-05 + 0.999923 * (_ctx_1024t + 0.3 * jax.random.normal(jax.random.fold_in(_rk, 611), (64, 77, 256), jnp.float32))
        return (x, ctx_1024)
    x, ctx_1024 = _rec_inputs()

    def _L0_attn_setup():
        import jax, jax.numpy as jnp
        import numpy as np
        DIM = 256
        C = 128
        B = 8
        T = 512
        key = jax.random.key(seed)
        ks = jax.random.split(key, 16)
        s = 0.02
        inp = {'x': jax.random.normal(ks[0], (B, T, DIM), dtype=jnp.float32), 'Wq': jax.random.normal(ks[1], (DIM, C), dtype=jnp.float32) * s, 'bq': jnp.zeros((C,), dtype=jnp.float32), 'Wk': jax.random.normal(ks[2], (DIM, C), dtype=jnp.float32) * s, 'bk': jnp.zeros((C,), dtype=jnp.float32), 'Wv': jax.random.normal(ks[3], (DIM, C), dtype=jnp.float32) * s, 'bv': jnp.zeros((C,), dtype=jnp.float32), 'Wa': jax.random.normal(ks[4], (DIM, 1), dtype=jnp.float32) * s, 'ba': jnp.zeros((1,), dtype=jnp.float32), 'Wb': jax.random.normal(ks[5], (DIM, 1), dtype=jnp.float32) * s, 'bb': jnp.zeros((1,), dtype=jnp.float32), 'Wg': jax.random.normal(ks[6], (DIM, C), dtype=jnp.float32) * s, 'bg': jnp.zeros((C,), dtype=jnp.float32), 'Wo': jax.random.normal(ks[7], (C, DIM), dtype=jnp.float32) * s, 'bo': jnp.zeros((DIM,), dtype=jnp.float32)}
        return inp
    _L0_attn_all = _L0_attn_setup()
    _L0_attn_in = {k: v for k, v in _L0_attn_all.items() if k in ('Wq', 'bq', 'Wk', 'bk', 'Wv', 'bv', 'Wa', 'ba', 'Wb', 'bb', 'Wg', 'bg', 'Wo', 'bo')}
    del _L0_attn_all

    def _L0_xattn_setup():
        import jax, jax.numpy as jnp
        import numpy as np
        key = jax.random.key(seed)
        k1, k2 = jax.random.split(key)
        B, L, V, D = (8, 512, 256, 256)
        hidden_states = jax.random.normal(k1, (B, L, D), dtype=jnp.float32)
        visual_hidden_state = jax.random.normal(k2, (B, V, D), dtype=jnp.float32)
        return {'hidden_states': hidden_states, 'visual_hidden_state': visual_hidden_state}
    _L0_xattn_all = _L0_xattn_setup()
    _L0_xattn_in = {k: v for k, v in _L0_xattn_all.items() if k in ()}
    del _L0_xattn_all

    def _L0_ffn_setup():
        import jax, jax.numpy as jnp
        import numpy as np
        QMAX = 127.0

        def _ste_round(v):
            return v + jax.lax.stop_gradient(jnp.round(v) - v)

        def _act_fake_quant(x, clip_factor):
            scale = jax.nn.sigmoid(clip_factor) * jnp.max(jnp.abs(x)) / QMAX
            return jnp.clip(_ste_round(x / scale), -QMAX - 1.0, QMAX) * scale

        def _weight_fake_quant(w):
            scale = jnp.max(jnp.abs(w), axis=1, keepdims=True) / QMAX
            return jnp.clip(_ste_round(w / scale), -QMAX - 1.0, QMAX) * scale
        key = jax.random.key(seed)
        k1, k2, k3, k4 = jax.random.split(key, 4)
        B, S, H, I = (8, 2048, 256, 704)
        return {'x': jax.random.normal(k1, (B, S, H), dtype=jnp.float32), 'clip_x': jnp.full((1,), 4.0, dtype=jnp.float32), 'clip_down': jnp.full((1,), 4.0, dtype=jnp.float32), 'w_gate': jax.random.normal(k2, (I, H), dtype=jnp.float32) * 0.02, 'w_up': jax.random.normal(k3, (I, H), dtype=jnp.float32) * 0.02, 'w_down': jax.random.normal(k4, (H, I), dtype=jnp.float32) * 0.02}
    _L0_ffn_all = _L0_ffn_setup()
    _L0_ffn_in = {k: v for k, v in _L0_ffn_all.items() if k in ('clip_x', 'clip_down', 'w_gate', 'w_up', 'w_down')}
    del _L0_ffn_all

    def _L1_attn_setup():
        import jax, jax.numpy as jnp
        import numpy as np
        B, S, D, H = (2, 512, 256, 16)
        HD = D // H
        key = jax.random.key(seed)
        ks = jax.random.split(key, 9)
        sd = 1.0 / np.sqrt(D)
        return {'x': jax.random.normal(ks[0], (B, S, D), dtype=jnp.float32), 'Wq': jax.random.normal(ks[1], (H, HD, D), dtype=jnp.float32) * sd, 'bq': jax.random.normal(ks[2], (H, HD), dtype=jnp.float32) * sd, 'Wk': jax.random.normal(ks[3], (H, HD, D), dtype=jnp.float32) * sd, 'bk': jax.random.normal(ks[4], (H, HD), dtype=jnp.float32) * sd, 'Wv': jax.random.normal(ks[5], (H, HD, D), dtype=jnp.float32) * sd, 'bv': jax.random.normal(ks[6], (H, HD), dtype=jnp.float32) * sd, 'Wp': jax.random.normal(ks[7], (D, D), dtype=jnp.float32) * sd, 'bp': jax.random.normal(ks[8], (D,), dtype=jnp.float32) * sd}
    _L1_attn_all = _L1_attn_setup()
    _L1_attn_in = {k: v for k, v in _L1_attn_all.items() if k in ('Wq', 'bq', 'Wk', 'bk', 'Wv', 'bv', 'Wp', 'bp')}
    del _L1_attn_all

    def _L1_xattn_setup():
        import jax, jax.numpy as jnp
        import numpy as np
        B, N, D = (4, 1024, 256)
        H = 16
        HD = D // H
        EPS = 1e-06
        BASE_SPARSITY = 0.3
        KEEP = max(int((1.0 - BASE_SPARSITY) * HD), 1)
        LEAKY_SLOPE = 0.01

        def _focus(x, focusing_factor):
            x = jnp.abs(jnp.where(x >= 0, x, LEAKY_SLOPE * x)) + EPS
            nrm = x.mean(axis=-1, keepdims=True)
            return jax.nn.softmax(jnp.log(x) * focusing_factor, axis=-1) * nrm

        def _to_heads(x):
            b, n, d = x.shape
            return x.reshape(b, n, H, HD).transpose(0, 2, 1, 3).reshape(b * H, n, HD)

        def _topk_sparsify(x):
            c = x.shape[-1]
            flat = x.reshape(-1, c)
            _, idx = jax.lax.top_k(jnp.abs(flat), KEEP)
            rows = jnp.arange(flat.shape[0])[:, None]
            mask = jnp.zeros(flat.shape, dtype=bool).at[rows, idx].set(True)
            return (flat * mask).reshape(x.shape)
        key = jax.random.key(seed)
        ks = jax.random.split(key, 8)
        mk = lambda k_, shp, s: jax.random.normal(k_, shp, dtype=jnp.float32) * s
        return {'q': mk(ks[0], (B, N, D), 1.0), 'k': mk(ks[1], (B, N, D), 1.0), 'v': mk(ks[2], (B, N, D), 1.0), 'Wq': mk(ks[3], (D, D), 0.02), 'Wk': mk(ks[4], (D, D), 0.02), 'Wv': mk(ks[5], (D, D), 0.02), 'Wp': mk(ks[6], (D, D), 0.02), 'focusing_factor': jnp.asarray(3.0, dtype=jnp.float32)}
    _L1_xattn_all = _L1_xattn_setup()
    _L1_xattn_in = {k: v for k, v in _L1_xattn_all.items() if k in ('Wq', 'Wk', 'Wv', 'Wp', 'focusing_factor')}
    del _L1_xattn_all

    def _L1_ffn_setup():
        import jax, jax.numpy as jnp
        import numpy as np
        B, N, D = (4, 512, 256)
        SPARSITY = 0.01
        key = jax.random.key(seed)
        k1, k2, k3 = jax.random.split(key, 3)
        x = jax.random.normal(k1, (B, N, D), dtype=jnp.float32)
        spatial = jax.random.normal(k2, (D, D), dtype=jnp.float32) * 0.02
        freq = jnp.fft.fft(spatial, axis=-1)
        k = int(D * SPARSITY)
        mag = jnp.abs(freq)
        kth = jax.lax.top_k(mag, k)[0][:, -1:]
        w_sparse = jnp.where(mag >= kth, freq, 0.0 + 0j)
        bias = jax.random.normal(k3, (D,), dtype=jnp.float32) * 0.01
        return {'x': x, 'w_freq_real': jnp.real(w_sparse).astype(jnp.float32), 'w_freq_imag': jnp.imag(w_sparse).astype(jnp.float32), 'bias': bias}
    _L1_ffn_all = _L1_ffn_setup()
    _L1_ffn_in = {k: v for k, v in _L1_ffn_all.items() if k in ('w_freq_real', 'w_freq_imag', 'bias')}
    del _L1_ffn_all
    return {'x': x, 'ctx_1024': ctx_1024, 'L0_attn_Wq': _L0_attn_in['Wq'], 'L0_attn_bq': _L0_attn_in['bq'], 'L0_attn_Wk': _L0_attn_in['Wk'], 'L0_attn_bk': _L0_attn_in['bk'], 'L0_attn_Wv': _L0_attn_in['Wv'], 'L0_attn_bv': _L0_attn_in['bv'], 'L0_attn_Wa': _L0_attn_in['Wa'], 'L0_attn_ba': _L0_attn_in['ba'], 'L0_attn_Wb': _L0_attn_in['Wb'], 'L0_attn_bb': _L0_attn_in['bb'], 'L0_attn_Wg': _L0_attn_in['Wg'], 'L0_attn_bg': _L0_attn_in['bg'], 'L0_attn_Wo': _L0_attn_in['Wo'], 'L0_attn_bo': _L0_attn_in['bo'], 'L0_ffn_clip_x': _L0_ffn_in['clip_x'], 'L0_ffn_clip_down': _L0_ffn_in['clip_down'], 'L0_ffn_w_gate': _L0_ffn_in['w_gate'], 'L0_ffn_w_up': _L0_ffn_in['w_up'], 'L0_ffn_w_down': _L0_ffn_in['w_down'], 'L1_attn_Wq': _L1_attn_in['Wq'], 'L1_attn_bq': _L1_attn_in['bq'], 'L1_attn_Wk': _L1_attn_in['Wk'], 'L1_attn_bk': _L1_attn_in['bk'], 'L1_attn_Wv': _L1_attn_in['Wv'], 'L1_attn_bv': _L1_attn_in['bv'], 'L1_attn_Wp': _L1_attn_in['Wp'], 'L1_attn_bp': _L1_attn_in['bp'], 'L1_xattn_Wq': _L1_xattn_in['Wq'], 'L1_xattn_Wk': _L1_xattn_in['Wk'], 'L1_xattn_Wv': _L1_xattn_in['Wv'], 'L1_xattn_Wp': _L1_xattn_in['Wp'], 'L1_xattn_focusing_factor': _L1_xattn_in['focusing_factor'], 'L1_ffn_w_freq_real': _L1_ffn_in['w_freq_real'], 'L1_ffn_w_freq_imag': _L1_ffn_in['w_freq_imag'], 'L1_ffn_bias': _L1_ffn_in['bias']}

def reference(x, ctx_1024, L0_attn_Wq, L0_attn_bq, L0_attn_Wk, L0_attn_bk, L0_attn_Wv, L0_attn_bv, L0_attn_Wa, L0_attn_ba, L0_attn_Wb, L0_attn_bb, L0_attn_Wg, L0_attn_bg, L0_attn_Wo, L0_attn_bo, L0_ffn_clip_x, L0_ffn_clip_down, L0_ffn_w_gate, L0_ffn_w_up, L0_ffn_w_down, L1_attn_Wq, L1_attn_bq, L1_attn_Wk, L1_attn_bk, L1_attn_Wv, L1_attn_bv, L1_attn_Wp, L1_attn_bp, L1_xattn_Wq, L1_xattn_Wk, L1_xattn_Wv, L1_xattn_Wp, L1_xattn_focusing_factor, L1_ffn_w_freq_real, L1_ffn_w_freq_imag, L1_ffn_bias):
    import jax
    import jax.numpy as jnp

    def _L0_attn_ref(x, Wq, bq, Wk, bk, Wv, bv, Wa, ba, Wb, bb, Wg, bg, Wo, bo):
        import jax, jax.numpy as jnp
        import numpy as np
        DIM = 256
        C = 128
        B = 8
        T = 512
        q = x @ Wq + bq
        kr = x @ Wk + bk
        k = kr / jnp.maximum(jnp.linalg.norm(kr, axis=-1, keepdims=True), 1e-12)
        v = x @ Wv + bv
        alpha = jax.nn.sigmoid(x @ Wa + ba)
        beta = jax.nn.sigmoid(x @ Wb + bb)
        gate = jax.nn.sigmoid(x @ Wg + bg)

        def step(S, inp):
            q_t, k_t, v_t, a_t, b_t, g_t = inp
            Sk = jnp.einsum('bij,bj->bi', S, k_t)
            a = a_t[:, :, None]
            b = b_t[:, :, None]
            S_new = a * (S - b * (Sk[:, :, None] * k_t[:, None, :])) + b * (v_t[:, :, None] * k_t[:, None, :])
            o = jnp.einsum('bi,bij->bj', q_t, S_new) * g_t
            return (S_new, o)
        seq = (jnp.swapaxes(q, 0, 1), jnp.swapaxes(k, 0, 1), jnp.swapaxes(v, 0, 1), jnp.swapaxes(alpha, 0, 1), jnp.swapaxes(beta, 0, 1), jnp.swapaxes(gate, 0, 1))
        S0 = jnp.zeros((x.shape[0], C, C), dtype=x.dtype)
        _, outs = jax.lax.scan(step, S0, seq)
        o = jnp.swapaxes(outs, 0, 1)
        return o @ Wo + bo

    def _L0_xattn_ref(hidden_states, visual_hidden_state):
        import jax, jax.numpy as jnp
        import numpy as np
        scores = jnp.einsum('bld,bvd->blv', hidden_states, visual_hidden_state)
        probs = jax.nn.softmax(scores, axis=-1)
        return jnp.einsum('blv,bvd->bld', probs, visual_hidden_state)

    def _L0_ffn_ref(x, clip_x, clip_down, w_gate, w_up, w_down):
        import jax, jax.numpy as jnp
        import numpy as np
        QMAX = 127.0

        def _ste_round(v):
            return v + jax.lax.stop_gradient(jnp.round(v) - v)

        def _act_fake_quant(x, clip_factor):
            scale = jax.nn.sigmoid(clip_factor) * jnp.max(jnp.abs(x)) / QMAX
            return jnp.clip(_ste_round(x / scale), -QMAX - 1.0, QMAX) * scale

        def _weight_fake_quant(w):
            scale = jnp.max(jnp.abs(w), axis=1, keepdims=True) / QMAX
            return jnp.clip(_ste_round(w / scale), -QMAX - 1.0, QMAX) * scale
        xq = _act_fake_quant(x, clip_x[0])
        gate = jnp.einsum('bsh,ih->bsi', xq, _weight_fake_quant(w_gate))
        up = jnp.einsum('bsh,ih->bsi', xq, _weight_fake_quant(w_up))
        h = _act_fake_quant(jax.nn.silu(gate) * up, clip_down[0])
        return jnp.einsum('bsi,hi->bsh', h, _weight_fake_quant(w_down))

    def _L1_attn_ref(x, Wq, bq, Wk, bk, Wv, bv, Wp, bp):
        import jax, jax.numpy as jnp
        import numpy as np
        B, S, D, H = (2, 512, 256, 16)
        HD = D // H
        q = jnp.einsum('bsd,hed->bhse', x, Wq) + bq[None, :, None, :]
        k = jnp.einsum('bsd,hed->bhse', x, Wk) + bk[None, :, None, :]
        v = jnp.einsum('bsd,hed->bhse', x, Wv) + bv[None, :, None, :]
        scale = 1.0 / np.sqrt(HD)
        scores = jnp.einsum('bhse,bhte->bhst', q, k) * scale
        attn = jax.nn.softmax(scores, axis=-1)
        out = jnp.einsum('bhst,bhte->bhse', attn, v)
        out = out.transpose(0, 2, 1, 3).reshape(x.shape[0], x.shape[1], -1)
        return out @ Wp.T + bp

    def _L1_xattn_ref(q, k, v, Wq, Wk, Wv, Wp, focusing_factor):
        import jax, jax.numpy as jnp
        import numpy as np
        B, N, D = (4, 1024, 256)
        H = 16
        HD = D // H
        EPS = 1e-06
        BASE_SPARSITY = 0.3
        KEEP = max(int((1.0 - BASE_SPARSITY) * HD), 1)
        LEAKY_SLOPE = 0.01

        def _focus(x, focusing_factor):
            x = jnp.abs(jnp.where(x >= 0, x, LEAKY_SLOPE * x)) + EPS
            nrm = x.mean(axis=-1, keepdims=True)
            return jax.nn.softmax(jnp.log(x) * focusing_factor, axis=-1) * nrm

        def _to_heads(x):
            b, n, d = x.shape
            return x.reshape(b, n, H, HD).transpose(0, 2, 1, 3).reshape(b * H, n, HD)

        def _topk_sparsify(x):
            c = x.shape[-1]
            flat = x.reshape(-1, c)
            _, idx = jax.lax.top_k(jnp.abs(flat), KEEP)
            rows = jnp.arange(flat.shape[0])[:, None]
            mask = jnp.zeros(flat.shape, dtype=bool).at[rows, idx].set(True)
            return (flat * mask).reshape(x.shape)
        b, n, d = q.shape
        q = q @ Wq.T
        k = k @ Wk.T
        v = v @ Wv.T
        q = _focus(q, focusing_factor)
        k = _focus(k, focusing_factor)
        qh, kh, vh = (_to_heads(q), _to_heads(k), _to_heads(v))
        qh = _topk_sparsify(qh)
        kh = _topk_sparsify(kh)
        length_k = float(n)
        sqrt_l = jnp.sqrt(jnp.asarray(length_k, dtype=q.dtype))
        k_mean = kh.mean(axis=1)
        z_inv = jnp.einsum('bnd,bd->bn', qh, k_mean) + EPS
        kv = jnp.einsum('bnc,bnd->bcd', kh / sqrt_l, vh / sqrt_l)
        y = jnp.einsum('bnc,bcd->bnd', qh, kv) / z_inv[..., None]
        y = y.reshape(b, H, n, HD).transpose(0, 2, 1, 3).reshape(b, n, d)
        return y @ Wp.T

    def _L1_ffn_ref(x, w_freq_real, w_freq_imag, bias):
        import jax, jax.numpy as jnp
        import numpy as np
        B, N, D = (4, 512, 256)
        SPARSITY = 0.01
        w = jax.lax.complex(w_freq_real, w_freq_imag)
        x_freq = jnp.fft.fft(x, axis=-1)
        y_freq = jnp.einsum('bnd,do->bno', x_freq, w)
        y = jnp.real(jnp.fft.ifft(y_freq, axis=-1))
        return y + bias
    x = x + _L0_attn_ref(_layernorm(x, axis=-1), L0_attn_Wq, L0_attn_bq, L0_attn_Wk, L0_attn_bk, L0_attn_Wv, L0_attn_bv, L0_attn_Wa, L0_attn_ba, L0_attn_Wb, L0_attn_bb, L0_attn_Wg, L0_attn_bg, L0_attn_Wo, L0_attn_bo)
    x = x + _L0_xattn_ref(_layernorm(x, axis=-1), ctx_1024)
    x = x + _L0_ffn_ref(_layernorm(x, axis=-1), L0_ffn_clip_x, L0_ffn_clip_down, L0_ffn_w_gate, L0_ffn_w_up, L0_ffn_w_down)
    x = x + _L1_attn_ref(_layernorm(x, axis=-1), L1_attn_Wq, L1_attn_bq, L1_attn_Wk, L1_attn_bk, L1_attn_Wv, L1_attn_bv, L1_attn_Wp, L1_attn_bp)
    x = x + _L1_xattn_ref(_layernorm(x, axis=-1), ctx_1024, ctx_1024, L1_xattn_Wq, L1_xattn_Wk, L1_xattn_Wv, L1_xattn_Wp, L1_xattn_focusing_factor)
    x = x + _L1_ffn_ref(_layernorm(x, axis=-1), L1_ffn_w_freq_real, L1_ffn_w_freq_imag, L1_ffn_bias)
    return x

_drawn_inputs = setup_inputs


def setup_inputs(seed=0):
    import zlib

    import numpy as np

    out = dict(_drawn_inputs(seed))
    spreads = {'L0_attn_bq': (0.0, 0.8),
     'L0_attn_bk': (0.0, 0.8),
     'L0_attn_bv': (0.0, 0.8),
     'L0_attn_bg': (0.0, 0.8),
     'L0_attn_bo': (0.0, 0.1)}
    factors = {'L0_attn_Wq': 3.974,
     'L0_attn_Wk': 3.916,
     'L0_attn_Wv': 3.983,
     'L0_attn_Wa': 8.0,
     'L0_attn_Wb': 8.0,
     'L0_attn_Wg': 8.0,
     'L0_attn_Wo': 3.749,
     'L0_ffn_w_gate': 3.228,
     'L0_ffn_w_up': 3.165,
     'L0_ffn_w_down': 3.151,
     'L1_attn_bq': 8.0,
     'L1_attn_bk': 8.0,
     'L1_xattn_Wq': 8.0,
     'L1_xattn_Wk': 8.0,
     'L1_xattn_Wv': 7.232,
     'L1_xattn_Wp': 7.219,
     'L1_ffn_bias': 8.0}
    for name, (base, spread) in spreads.items():
        noise = np.random.default_rng([zlib.crc32(name.encode()), seed]).standard_normal(out[name].shape)
        drawn = base * np.exp(spread * noise) if base else spread * noise
        out[name] = jnp.asarray(drawn.astype(out[name].dtype))
    for name, factor in factors.items():
        out[name] = (out[name] * factor).astype(out[name].dtype)
    return out
```

```python
from contextlib import ExitStack

import concourse.bass as bass
from concourse import mybir

F32 = mybir.dt.float32
BF16 = mybir.dt.bfloat16
I32 = mybir.dt.int32
ALU = mybir.AluOpType
ACT = mybir.ActivationFunctionType
AX_X = mybir.AxisListType.X
RMAX = bass.bass_isa.ReduceOp.max

B = 64
T = 256
D = 256
C = 128
V = 77
I = 704
H = 16
HD = D // H
P = 128
NT = T // P
ND = D // P
NI = -(-I // P)
LASTI = I - (NI - 1) * P
PAIRS = B // 2
LEVELS = 6
KEEP = max(int(0.7 * HD), 1)
QMAX = 127.0
LN_EPS = 1e-5
EPS = 1e-6
MAGIC = 12582912.0


def rows(dram, b):
    return dram[bass.ds(b, 1), :, :].rearrange("o (t p) d -> p (o t) d", p=P)


def phase_attention(nc, A, x2, xn3, ident, peak):
    with ExitStack() as ctx:
        def sb(name, shape, dt=F32):
            return ctx.enter_context(nc.sbuf_tensor("a_" + name, shape, dt))

        def sb2(name, shape, dt=F32):
            return [sb(f"{name}{p}", shape, dt) for p in range(2)]

        def sem(name):
            return ctx.enter_context(nc.semaphore("a_" + name))

        def sem2(name):
            return [sem(f"{name}{p}") for p in range(2)]

        Wkv = sb("Wkv", [P, ND, 2 * C])
        Wab = sb("Wab", [P, ND, 2])
        Wqg = sb("Wqg", [P, ND, 2 * C])
        Wo = sb("Wo", [C, D])
        bkv = sb("bkv", [P, 1, 2 * C])
        bab = sb("bab", [P, 1, 2])
        bq = sb("bq", [P, 1])
        bg = sb("bg", [P, 1])
        nbg = sb("nbg", [P, 1])
        bo = sb("bo", [P, 1, D])
        ones = sb("ones", [P, 3 * P])
        later = sb("later", [P, P])
        upto = sb("upto", [P, 3 * P])
        before = sb("before", [P, 3 * P])
        lmask = sb("lmask", [P, LEVELS, P])
        nmask = sb("nmask", [P, 2, P])
        half = sb("half", [P, NT])
        lneps = sb("lneps", [P, NT])
        x = sb2("x", [P, NT, D])
        cx = sb2("cx", [V, D])
        xbo = sb2("xbo", [P, NT, D])
        xn = sb2("xn", [P, NT, D])
        xT = sb2("xT", [P, ND, T])
        cT = sb2("cT", [P, ND, V])
        stats = sb2("stats", [P, NT, 6])
        mv = sb2("mv", [P, NT, 2])
        rstd = sb2("rstd", [P, NT])
        kv = sb2("kv", [P, NT, 2 * C])
        zab = sb2("zab", [P, NT, 2])
        tab = sb2("tab", [P, NT, 2])
        eab = sb2("eab", [P, NT, 2])
        lna = sb2("lna", [P, NT])
        la = sb2("la", [P, NT])
        beta = sb2("beta", [P, NT])
        sq = sb2("sq", [P, C])
        ss = sb2("ss", [P, NT])
        rk = sb2("rk", [P, NT])
        kn = sb2("kn", [P, NT, C])
        kT = sb2("kT", [C, T])
        qT = sb2("qT", [C, T])
        ge = sb2("ge", [C, T])
        gT = sb2("gT", [C, T])
        R = sb2("R", [P, 3 * P])
        Dx = sb2("Dx", [P, 3 * P])
        Di = sb2("Di", [P, 3 * P])
        Ds = sb2("Ds", [P, 3 * P])
        U = sb2("U", [P, 3 * P])
        L = sb2("L", [P, 2, P])
        Lm = sb2("Lm", [P, LEVELS, 2, P])
        N = sb2("N", [P, 4, P])
        Y = sb2("Y", [P, 2, P])
        W0 = sb2("W0", [P, P])
        WT = sb2("WT", [C, T])
        v1 = sb2("v1", [P, C])
        Pm = sb2("Pm", [P, 3 * P])
        oT = sb2("oT", [C, T])
        x1 = sb2("x1", [P, NT, D])
        nmx = sb2("nmx", [P, NT])
        es = sb2("es", [P, NT, V])
        sm = sb2("sm", [P, NT])
        rs = sb2("rs", [P, NT])
        eT = sb2("eT", [V, T])
        xo = sb2("xo", [P, NT, D])
        xno = sb2("xno", [P, NT, D])
        pk = sb2("pk", [P, 1])
        idle = sb2("idle", [P, 1])
        bank = [[ctx.enter_context(nc.psum_tensor(f"a_b{p}{k}", [P, 512], F32)) for k in range(4)]
                for p in range(2)]

        s_w = sem("weights")
        s_bg = sem("neg_gate_bias")
        s_c = sem("constants")
        s_x = sem2("x_in")
        s_cx = sem2("ctx_in")
        s_st = sem2("stats")
        s_mv = sem2("meanvar")
        s_ve = sem2("vareps")
        s_rs = sem2("rstd")
        s_xn = sem2("xn")
        s_xbo = sem2("xbo")
        s_tr = sem2("xn_transposed")
        s_xT = sem2("xT")
        s_cT = sem2("cT")
        s_ctr = sem2("ctx_transposed")
        s_pr = sem2("projected")
        s_kv = sem2("kv")
        s_zab = sem2("zab")
        s_tab = sem2("tab")
        s_eab = sem2("eab")
        s_e1 = sem2("eab1")
        s_lna = sem2("lna")
        s_la = sem2("la")
        s_be = sem2("beta")
        s_ss = sem2("ksq")
        s_sg = sem2("ksq_guarded")
        s_rk = sem2("rk")
        s_kn = sem2("kn")
        s_ktr = sem2("k_transposed")
        s_kT = sem2("kT")
        s_qT = sem2("qT")
        s_ge = sem2("gate_exp")
        s_gT = sem2("gate")
        s_R = sem2("R")
        s_G = sem2("gram")
        s_lD = sem2("logdecay")
        s_Dx = sem2("decay")
        s_Dm = sem2("decay_masked")
        s_U = sem2("U")
        s_utr = sem2("U_transposed")
        s_L = sem2("L")
        s_Lm = sem2("Lm")
        s_n0 = sem2("inverse_start")
        s_Yp = sem2("Yp")
        s_Y = sem2("Y")
        s_dN = sem2("dN")
        s_N = sem2("N")
        s_w0p = sem2("w0p")
        s_w0 = sem2("w0")
        s_v1p = sem2("v1p")
        s_v1 = sem2("v1")
        s_w1p = sem2("w1p")
        s_w1 = sem2("w1")
        s_Ap = sem2("Ap")
        s_P = sem2("P")
        s_op = sem2("op")
        s_og = sem2("og")
        s_wop = sem2("wop")
        s_x1 = sem2("x1")
        s_sc = sem2("scores")
        s_mx = sem2("rowmax")
        s_es = sem2("expscores")
        s_etr = sem2("es_transposed")
        s_eT = sem2("eT")
        s_co = sem2("ctx_out")
        s_rr = sem2("rsum")
        s_x2 = sem2("x2")
        s_pk = sem2("peak_part")
        s_pkm = sem2("peak")
        s_out = sem2("stored")
        WEIGHTS = 6 * ND + 8
        CONSTS = 12 + 4 * (LEVELS + 2) + 1
        block = ctx.enter_context(nc.Block())

        @block.sync
        def _(sp):
            for k in range(ND):
                r = slice(k * P, (k + 1) * P)
                sp.dma_start(Wkv[:, k, 0:C], A["L0_attn_Wk"][r, :]).then_inc(s_w, 16)
                sp.dma_start(Wkv[:, k, C:2 * C], A["L0_attn_Wv"][r, :]).then_inc(s_w, 16)
                sp.dma_start(Wab[:, k, 0:1], A["L0_attn_Wa"][r, :]).then_inc(s_w, 16)
                sp.dma_start(Wab[:, k, 1:2], A["L0_attn_Wb"][r, :]).then_inc(s_w, 16)
                sp.dma_start(Wqg[:, k, 0:C], A["L0_attn_Wq"][r, :]).then_inc(s_w, 16)
                sp.dma_start(Wqg[:, k, C:2 * C], A["L0_attn_Wg"][r, :]).then_inc(s_w, 16)
            sp.dma_start(Wo[:, :], A["L0_attn_Wo"][:, :]).then_inc(s_w, 16)
            sp.dma_start(bkv[:, 0, 0:C], A["L0_attn_bk"].partition_broadcast(P)).then_inc(s_w, 16)
            sp.dma_start(bkv[:, 0, C:2 * C], A["L0_attn_bv"].partition_broadcast(P)).then_inc(s_w, 16)
            sp.dma_start(bab[:, 0, 0:1], A["L0_attn_ba"].partition_broadcast(P)).then_inc(s_w, 16)
            sp.dma_start(bab[:, 0, 1:2], A["L0_attn_bb"].partition_broadcast(P)).then_inc(s_w, 16)
            sp.dma_start(bo[:, 0, :], A["L0_attn_bo"].partition_broadcast(P)).then_inc(s_w, 16)
            sp.dma_start(bq[:, :], A["L0_attn_bq"].unsqueeze(1)).then_inc(s_w, 16)
            sp.dma_start(bg[:, :], A["L0_attn_bg"].unsqueeze(1)).then_inc(s_w, 16)

            def load_x(p, b):
                sp.dma_start(x[p][:, :, :], rows(A["x"], b)).then_inc(s_x[p], 16)

            def load_ctx(p, b):
                sp.dma_start(cx[p][:, :], A["ctx_1024"][bass.ds(b, 1), :, :]
                             .rearrange("o v d -> v (o d)")).then_inc(s_cx[p], 16)

            for p in range(2):
                load_x(p, p)
                load_ctx(p, p)
            with sp.Fori(0, PAIRS - 1) as i:
                for p in range(2):
                    sp.wait_ge(s_xbo[p], i + 1)
                    sp.wait_ge(s_xn[p], 6 * i + 2)
                    load_x(p, 2 * i + 2 + p)
                for p in range(2):
                    sp.wait_ge(s_co[p], i + 1)
                    load_ctx(p, 2 * i + 2 + p)
            sp.wait_ge(s_w, 16)

        @block.gpsimd
        def _(pool):
            pool.memset(ones[:, :], 1.0).then_inc(s_c, 1)
            pool.memset(half[:, :], -0.5).then_inc(s_c, 1)
            pool.memset(lneps[:, :], LN_EPS).then_inc(s_c, 1)
            pool.memset(pk[0][:, :], 0.0).then_inc(s_c, 1)
            pool.memset(pk[1][:, :], 0.0).then_inc(s_c, 1)
            pool.wait_ge(s_c, 5)
            pool.affine_select(out=later[:, :], in_=ones[:, 0:P], compare_op=ALU.is_gt, fill=0.0, base=0,
                               pattern=[[-1, P]], channel_multiplier=1).then_inc(s_c, 1)
            for dst, op in ((upto, ALU.is_ge), (before, ALU.is_gt)):
                for c in (0, 2):
                    pool.affine_select(out=dst[:, c * P:(c + 1) * P], in_=ones[:, 0:P], compare_op=op,
                                       fill=0.0, base=0, pattern=[[1, P]],
                                       channel_multiplier=-1).then_inc(s_c, 1)
                pool.tensor_copy(dst[:, P:2 * P], ones[:, 0:P]).then_inc(s_c, 1)
            done = 5 + 1 + 6

            def half_blocks(out, h, flip):
                nonlocal done
                blocks = P // (2 * h)
                part = out.rearrange("p (b a c) -> p b a c", b=blocks, a=2)
                pool.memset(part[:, :, 0, :], 0.0 if flip else 1.0).then_inc(s_c, 1)
                pool.memset(part[:, :, 1, :], 1.0 if flip else 0.0).then_inc(s_c, 1)
                done += 2
                lo, hi = (0, h) if flip else (h, 2 * h)
                pool.wait_ge(s_c, done)
                pool.affine_select(out=part, in_=part, compare_op=ALU.is_ge, fill=0.0, base=-lo,
                                   pattern=[[-2 * h, blocks], [0, 2], [0, h]],
                                   channel_multiplier=1).then_inc(s_c, 1)
                done += 1
                pool.wait_ge(s_c, done)
                pool.affine_select(out=part, in_=part, compare_op=ALU.is_gt, fill=0.0, base=hi,
                                   pattern=[[2 * h, blocks], [0, 2], [0, h]],
                                   channel_multiplier=-1).then_inc(s_c, 1)
                done += 1

            for lv in range(LEVELS):
                half_blocks(lmask[:, lv, :], 2 << lv, False)
            half_blocks(nmask[:, 0, :], 1, True)
            half_blocks(nmask[:, 1, :], 1, False)
            pool.wait_ge(s_c, done)
            pool.tensor_scalar(nmask[:, :, :], nmask[:, :, :], -1.0, None, ALU.mult).then_inc(s_c, 1)
            done += 1
            assert done == CONSTS
            pool.wait_ge(s_w, 16 * WEIGHTS)
            pool.tensor_scalar(nbg[:, :], bg[:, :], -1.0, None, ALU.mult).then_inc(s_bg, 1)

            def rsqrt(p, n):
                pool.wait_ge(s_mv[p], 6 * i + 2 * n + 2)
                pool.wait_ge(s_xn[p], 6 * i + 2 * n)
                pool.tensor_tensor(rstd[p][:, :], mv[p][:, :, 1], lneps[:, :], ALU.add).then_inc(s_ve[p], 1)
                pool.wait_ge(s_ve[p], 3 * i + n + 1)
                pool.tensor_tensor(rstd[p][:, :], rstd[p][:, :], half[:, :], ALU.pow).then_inc(s_rs[p], 1)

            with pool.Fori(0, PAIRS) as i:
                for p in range(2):
                    rsqrt(p, 0)
                for p in range(2):
                    pool.wait_ge(s_x[p], 16 * i + 16)
                    pool.wait_ge(s_x1[p], i)
                    pool.tensor_tensor(xbo[p][:, :, :], x[p][:, :, :], bo[:, :, :].to_broadcast([P, NT, D]),
                                       ALU.add).then_inc(s_xbo[p], 1)
                for p in range(2):
                    pool.wait_ge(s_sg[p], i + 1)
                    pool.wait_ge(s_kn[p], 2 * i)
                    pool.tensor_tensor(rk[p][:, :], ss[p][:, :], half[:, :], ALU.pow).then_inc(s_rk[p], 1)
                for p in range(2):
                    pool.wait_ge(s_la[p], i + 1)
                    pool.tensor_tensor(R[p][:, 0:T], upto[:, 0:T], la[p][:, 0:1].to_broadcast([P, T]),
                                       ALU.mult).then_inc(s_R[p], 1)
                    pool.tensor_tensor(R[p][:, T:T + P], upto[:, 0:P], la[p][:, 1:2].to_broadcast([P, P]),
                                       ALU.mult).then_inc(s_R[p], 1)
                for p in range(2):
                    pool.wait_ge(s_Dx[p], i + 1)
                    pool.tensor_tensor(Ds[p][:, :], Dx[p][:, :], before[:, :], ALU.mult).then_inc(s_Dm[p], 1)
                    pool.tensor_tensor(Di[p][:, :], Dx[p][:, :], upto[:, :], ALU.mult).then_inc(s_Dm[p], 1)
                for p in range(2):
                    ud = U[p][:, :].rearrange("p (a c) -> p a c", a=3)[:, 0:3:2, :]
                    pool.wait_ge(s_U[p], 2 * i + 2)
                    pool.tensor_tensor(N[p][:, 0:2, :], ud, nmask[:, 0:1, :].to_broadcast([P, 2, P]),
                                       ALU.mult).then_inc(s_n0[p], 1)
                    pool.wait_ge(s_L[p], i + 1)
                    pool.tensor_tensor(N[p][:, 2:4, :], L[p][:, :, :], nmask[:, 1:2, :].to_broadcast([P, 2, P]),
                                       ALU.mult).then_inc(s_n0[p], 1)
                    pool.wait_ge(s_n0[p], 3 * i + 2)
                    pool.tensor_tensor(N[p][:, :, :], N[p][:, :, :],
                                       ident[:, :].unsqueeze(1).to_broadcast([P, 4, P]),
                                       ALU.add).then_inc(s_n0[p], 1)
                    for lv in range(LEVELS):
                        pool.tensor_tensor(Lm[p][:, lv, :, :], L[p][:, :, :],
                                           lmask[:, lv:lv + 1, :].to_broadcast([P, 2, P]),
                                           ALU.mult).then_inc(s_Lm[p], 1)
                for n in (1, 2):
                    for p in range(2):
                        rsqrt(p, n)

        @block.scalar
        def _(act):
            act.wait_ge(s_w, 16 * WEIGHTS)
            act.wait_ge(s_bg, 1)
            with act.Fori(0, PAIRS) as i:
                for p in range(2):
                    b0, b1, b2, b3 = bank[p]
                    act.wait_ge(s_ctr[p], i + 1)
                    act.copy(cT[p][:, :, :], b3[:, 0:ND * V]).then_inc(s_cT[p], 1)
                    act.wait_ge(s_tr[p], 2 * i + 1)
                    act.copy(xT[p][:, :, :], b0[:, :]).then_inc(s_xT[p], 1)
                for p in range(2):
                    b0, b1, b2, b3 = bank[p]
                    act.wait_ge(s_pr[p], i + 1)
                    act.activation(qT[p][:, :], b2[:, 0:T], ACT.Identity, bias=bq[:, :]).then_inc(s_qT[p], 1)
                    act.activation(ge[p][:, :], b2[:, T:2 * T], ACT.Exp, bias=nbg[:, :],
                                   scale=-1.0).then_inc(s_ge[p], 1)
                    act.wait_ge(s_kv[p], i + 1)
                    for t in range(NT):
                        act.activation(sq[p][:, :], kv[p][:, t, 0:C], ACT.Square,
                                       accum_out=ss[p][:, t:t + 1]).then_inc(s_ss[p], 1)
                        act.wait_ge(s_ss[p], 2 * i + t + 1)
                    act.wait_ge(s_tab[p], 2 * i + 2)
                    act.activation(eab[p][:, :, :], tab[p][:, :, :], ACT.Exp, scale=-1.0).then_inc(s_eab[p], 1)
                    act.wait_ge(s_e1[p], i + 1)
                    act.activation(lna[p][:, :], eab[p][:, :, 0], ACT.Ln).then_inc(s_lna[p], 1)
                for p in range(2):
                    act.wait_ge(s_lD[p], i + 1)
                    act.activation(Dx[p][:, :], bank[p][2][:, 0:3 * P], ACT.Exp).then_inc(s_Dx[p], 1)
                for p in range(2):
                    act.wait_ge(s_ktr[p], i + 1)
                    act.copy(kT[p][:, :], bank[p][0][:, 0:T]).then_inc(s_kT[p], 1)
                for p in range(2):
                    act.wait_ge(s_utr[p], i + 1)
                    act.copy(L[p][:, :, :], bank[p][3][:, 0:2 * P]).then_inc(s_L[p], 1)
                for lv in range(LEVELS):
                    for p in range(2):
                        act.wait_ge(s_Yp[p], LEVELS * i + lv + 1)
                        act.copy(Y[p][:, :, :], bank[p][0][:, 0:2 * P]).then_inc(s_Y[p], 1)
                for p in range(2):
                    act.wait_ge(s_w0p[p], i + 1)
                    act.copy(W0[p][:, :], bank[p][2][:, 0:P]).then_inc(s_w0[p], 1)
                    act.copy(WT[p][:, 0:P], bank[p][2][:, P:2 * P]).then_inc(s_w0[p], 1)
                for p in range(2):
                    act.wait_ge(s_w1p[p], i + 1)
                    act.copy(WT[p][:, P:2 * P], bank[p][2][:, 2 * P:3 * P]).then_inc(s_w1[p], 1)
                for p in range(2):
                    act.wait_ge(s_tr[p], 2 * i + 2)
                    act.copy(xT[p][:, :, :], bank[p][0][:, :]).then_inc(s_xT[p], 1)
                for p in range(2):
                    act.wait_ge(s_mx[p], i + 1)
                    for t in range(NT):
                        act.activation(es[p][:, t, :], bank[p][1][:, t * P:t * P + V], ACT.Exp,
                                       bias=nmx[p][:, t:t + 1], accum_out=sm[p][:, t:t + 1]).then_inc(s_es[p], 1)
                for p in range(2):
                    act.wait_ge(s_etr[p], i + 1)
                    act.copy(eT[p][:, :], bank[p][3][0:V, 0:T]).then_inc(s_eT[p], 1)
                for p in range(2):
                    act.wait_ge(s_x2[p], 2 * i + 2)
                    act.dma_start(rows(x2, 2 * i + p), xo[p][:, :, :]).then_inc(s_out[p], 16)
                    act.wait_ge(s_xn[p], 6 * i + 6)
                    act.dma_start(rows(xn3, 2 * i + p), xno[p][:, :, :]).then_inc(s_out[p], 16)
            for p in range(2):
                act.wait_ge(s_out[p], 32 * PAIRS)

        @block.vector
        def _(dve):
            def normed(dst, src, p, n):
                for t in range(NT):
                    dve.wait_ge(s_rs[p], 3 * i + n + 1)
                    dve.tensor_scalar(dst[:, t, :], src[:, t, :], mv[p][:, t, 0:1], rstd[p][:, t:t + 1],
                                      ALU.subtract, ALU.mult).then_inc(s_xn[p], 1)

            def stat(src, p, n):
                for t in range(NT):
                    dve.bn_stats(stats[p][:, t, :], src[:, t, :]).then_inc(s_st[p], 1)
                dve.wait_ge(s_st[p], 6 * i + 2 * n + 2)
                dve.memset(idle[p][:, :], 0.0)
                for t in range(NT):
                    dve.bn_aggr(mv[p][:, t, :], stats[p][:, t, :]).then_inc(s_mv[p], 1)

            dve.wait_ge(s_w, 16 * WEIGHTS)
            dve.wait_ge(s_c, CONSTS)
            with dve.Fori(0, PAIRS) as i:
                for p in range(2):
                    dve.wait_ge(s_x[p], 16 * i + 16)
                    stat(x[p], p, 0)
                for p in range(2):
                    normed(xn[p], x[p], p, 0)
                for p in range(2):
                    b0, b1, b2, b3 = bank[p]
                    dve.wait_ge(s_pr[p], i + 1)
                    dve.tensor_tensor(kv[p][:, :, :], b1[:, :].rearrange("p (t c) -> p t c", t=NT),
                                      bkv[:, :, :].to_broadcast([P, NT, 2 * C]), ALU.add).then_inc(s_kv[p], 1)
                    dve.tensor_tensor(zab[p][:, :, :], b3[:, 256:260].rearrange("p (t c) -> p t c", t=NT),
                                      bab[:, :, :].to_broadcast([P, NT, 2]), ALU.add).then_inc(s_zab[p], 1)
                    dve.wait_ge(s_zab[p], i + 1)
                    dve.scalar_tensor_tensor(tab[p][:, :, 0], zab[p][:, :, 0], -1.0, zab[p][:, :, 0],
                                             ALU.mult, ALU.max).then_inc(s_tab[p], 1)
                    dve.tensor_copy(tab[p][:, :, 1], zab[p][:, :, 1]).then_inc(s_tab[p], 1)
                for p in range(2):
                    dve.wait_ge(s_eab[p], i + 1)
                    dve.tensor_scalar(eab[p][:, :, :], eab[p][:, :, :], 1.0, None, ALU.add).then_inc(s_e1[p], 1)
                    dve.wait_ge(s_e1[p], i + 1)
                    dve.reciprocal(beta[p][:, :], eab[p][:, :, 1]).then_inc(s_be[p], 1)
                    dve.wait_ge(s_lna[p], i + 1)
                    dve.scalar_tensor_tensor(la[p][:, :], zab[p][:, :, 0], 0.0, lna[p][:, :],
                                             ALU.min, ALU.subtract).then_inc(s_la[p], 1)
                    dve.wait_ge(s_ss[p], 2 * i + 2)
                    dve.tensor_scalar(ss[p][:, :], ss[p][:, :], 1e-24, None, ALU.max).then_inc(s_sg[p], 1)
                for p in range(2):
                    dve.wait_ge(s_rk[p], i + 1)
                    for t in range(NT):
                        dve.tensor_scalar(kn[p][:, t, :], kv[p][:, t, 0:C], rk[p][:, t:t + 1], None,
                                          ALU.mult).then_inc(s_kn[p], 1)
                for p in range(2):
                    dve.wait_ge(s_ge[p], i + 1)
                    dve.tensor_scalar(ge[p][:, :], ge[p][:, :], 1.0, None, ALU.add).then_inc(s_gT[p], 1)
                    dve.wait_ge(s_gT[p], 2 * i + 1)
                    dve.reciprocal(gT[p][:, :], ge[p][:, :]).then_inc(s_gT[p], 1)
                for p in range(2):
                    dve.wait_ge(s_G[p], i + 1)
                    dve.wait_ge(s_Dm[p], 2 * i + 2)
                    dve.wait_ge(s_be[p], i + 1)
                    for t, c in ((0, slice(0, T)), (1, slice(T, T + P))):
                        dve.scalar_tensor_tensor(U[p][:, c], bank[p][1][:, c], beta[p][:, t:t + 1], Ds[p][:, c],
                                                 ALU.mult, ALU.mult).then_inc(s_U[p], 1)
                for lv in range(LEVELS):
                    w = 4 if lv < LEVELS - 1 else 2
                    for p in range(2):
                        dve.wait_ge(s_dN[p], LEVELS * i + lv + 1)
                        dve.tensor_tensor(N[p][:, 0:w, :], N[p][:, 0:w, :],
                                          bank[p][1][:, 0:w * P].rearrange("p (a c) -> p a c", a=w),
                                          ALU.subtract).then_inc(s_N[p], 1)
                for p in range(2):
                    dve.wait_ge(s_v1p[p], i + 1)
                    dve.tensor_tensor(v1[p][:, :], kv[p][:, 1, C:2 * C], bank[p][3][:, 256:384],
                                      ALU.subtract).then_inc(s_v1[p], 1)
                for p in range(2):
                    dve.wait_ge(s_Ap[p], i + 1)
                    for t, c in ((0, slice(0, T)), (1, slice(T, T + P))):
                        dve.scalar_tensor_tensor(Pm[p][:, c], bank[p][0][:, c], beta[p][:, t:t + 1], Di[p][:, c],
                                                 ALU.mult, ALU.mult).then_inc(s_P[p], 1)
                for p in range(2):
                    dve.wait_ge(s_op[p], i + 1)
                    dve.tensor_tensor(oT[p][:, :], bank[p][1][:, 0:T], gT[p][:, :], ALU.mult).then_inc(s_og[p], 1)
                for p in range(2):
                    dve.wait_ge(s_wop[p], i + 1)
                    dve.wait_ge(s_xbo[p], i + 1)
                    dve.tensor_tensor(x1[p][:, :, :], bank[p][2][:, :].rearrange("p (t c) -> p t c", t=NT),
                                      xbo[p][:, :, :], ALU.add).then_inc(s_x1[p], 1)
                    dve.wait_ge(s_x1[p], i + 1)
                    stat(x1[p], p, 1)
                for p in range(2):
                    normed(xn[p], x1[p], p, 1)
                for p in range(2):
                    dve.wait_ge(s_sc[p], i + 1)
                    dve.tensor_reduce(nmx[p][:, :],
                                      bank[p][1][:, 0:2 * P].rearrange("p (t c) -> p t c", t=NT)[:, :, 0:V],
                                      axis=AX_X, op=ALU.max, negate=True).then_inc(s_mx[p], 1)
                for p in range(2):
                    dve.wait_ge(s_es[p], 2 * i + 2)
                    dve.reciprocal(rs[p][:, :], sm[p][:, :]).then_inc(s_rr[p], 1)
                for p in range(2):
                    dve.wait_ge(s_co[p], i + 1)
                    dve.wait_ge(s_rr[p], i + 1)
                    dve.wait_ge(s_out[p], 32 * i)
                    for t in range(NT):
                        dve.scalar_tensor_tensor(xo[p][:, t, :], bank[p][2][:, t * D:(t + 1) * D],
                                                 rs[p][:, t:t + 1], x1[p][:, t, :],
                                                 ALU.mult, ALU.add).then_inc(s_x2[p], 1)
                    dve.wait_ge(s_x2[p], 2 * i + 2)
                    stat(xo[p], p, 2)
                for p in range(2):
                    normed(xno[p], xo[p], p, 2)
                    dve.wait_ge(s_xn[p], 6 * i + 6)
                    dve.tensor_reduce(rs[p][:, 0:1], xno[p][:, :, :], axis=mybir.AxisListType.XY, op=ALU.max,
                                      apply_absolute_value=True).then_inc(s_pk[p], 1)
                    dve.wait_ge(s_pk[p], i + 1)
                    dve.tensor_tensor(pk[p][:, :], pk[p][:, :], rs[p][:, 0:1], ALU.max).then_inc(s_pkm[p], 1)
            for p in range(2):
                dve.wait_ge(s_pkm[p], PAIRS)
            dve.tensor_tensor(peak[:, :], pk[0][:, :], pk[1][:, :], ALU.max).then_inc(s_pk[0], 1)
            dve.wait_ge(s_pk[0], PAIRS + 1)

        @block.tensor
        def _(pe):
            pe.wait_ge(s_w, 16 * WEIGHTS)
            pe.wait_ge(s_c, CONSTS)

            def turn(p, dst, src):
                for k in range(ND):
                    for t in range(NT):
                        last = pe.transpose(dst[:, k * T + t * P:k * T + (t + 1) * P],
                                            src[:, t, k * P:(k + 1) * P], ident[:, :])
                return last

            with pe.Fori(0, PAIRS) as i:
                for p in range(2):
                    b0, b1, b2, b3 = bank[p]
                    pe.wait_ge(s_cx[p], 16 * i + 16)
                    pe.wait_ge(s_eT[p], i)
                    for k in range(ND):
                        last = pe.transpose(b3[:, k * V:(k + 1) * V], cx[p][:, k * P:(k + 1) * P],
                                            ident[0:V, 0:V])
                    last.then_inc(s_ctr[p], 1)
                    pe.wait_ge(s_xn[p], 6 * i + 2)
                    turn(p, b0, xn[p]).then_inc(s_tr[p], 1)
                for p in range(2):
                    b0, b1, b2, b3 = bank[p]
                    pe.wait_ge(s_xT[p], 2 * i + 1)
                    pe.wait_ge(s_x2[p], 2 * i)
                    pe.wait_ge(s_cT[p], i + 1)
                    for k2 in range(NT):
                        for k in range(ND):
                            pe.matmul(b1[:, k2 * 2 * C:(k2 + 1) * 2 * C], xT[p][:, k, k2 * P:(k2 + 1) * P],
                                      Wkv[:, k, :], start=k == 0, stop=k == ND - 1)
                    for k2 in range(NT):
                        for k in range(ND):
                            pe.matmul(b3[:, 256 + 2 * k2:258 + 2 * k2], xT[p][:, k, k2 * P:(k2 + 1) * P],
                                      Wab[:, k, :], start=k == 0, stop=k == ND - 1)
                    for m in range(2):
                        for k in range(ND):
                            last = pe.matmul(b2[:, m * T:(m + 1) * T], Wqg[:, k, m * C:(m + 1) * C],
                                             xT[p][:, k, :], start=k == 0, stop=k == ND - 1)
                    last.then_inc(s_pr[p], 1)
                for p in range(2):
                    b2 = bank[p][2]
                    pe.wait_ge(s_R[p], 2 * i + 2)
                    pe.wait_ge(s_qT[p], i + 1)
                    pe.wait_ge(s_ge[p], i + 1)
                    pe.matmul(b2[:, 0:T], later[:, :], R[p][:, 0:T], start=True, stop=False)
                    pe.matmul(b2[:, P:T], ones[:, 0:P], R[p][:, T:T + P], start=False, stop=True)
                    pe.matmul(b2[:, T:T + P], later[:, :], R[p][:, T:T + P], start=True,
                              stop=True).then_inc(s_lD[p], 1)
                for p in range(2):
                    pe.wait_ge(s_kn[p], 2 * i + 2)
                    for t in range(NT):
                        last = pe.transpose(bank[p][0][:, t * P:(t + 1) * P], kn[p][:, t, :], ident[:, :])
                    last.then_inc(s_ktr[p], 1)
                for p in range(2):
                    pe.wait_ge(s_kT[p], i + 1)
                    pe.wait_ge(s_kv[p], i + 1)
                    pe.matmul(bank[p][1][:, 0:T], kT[p][:, 0:P], kT[p][:, :], start=True, stop=True)
                    pe.matmul(bank[p][1][:, T:T + P], kT[p][:, P:T], kT[p][:, P:T], start=True,
                              stop=True).then_inc(s_G[p], 1)
                for p in range(2):
                    pe.wait_ge(s_U[p], 2 * i + 2)
                    pe.wait_ge(s_zab[p], i + 1)
                    pe.transpose(bank[p][3][:, 0:P], U[p][:, 0:P], ident[:, :])
                    pe.transpose(bank[p][3][:, P:2 * P], U[p][:, 2 * P:3 * P], ident[:, :]).then_inc(s_utr[p], 1)
                for lv in range(LEVELS):
                    for p in range(2):
                        b0 = bank[p][0]
                        pe.wait_ge(s_Lm[p], LEVELS * i + lv + 1)
                        if lv == 0:
                            pe.wait_ge(s_n0[p], 3 * i + 3)
                        else:
                            pe.wait_ge(s_N[p], LEVELS * i + lv)
                        for j in range(2):
                            last = pe.matmul(b0[:, j * P:(j + 1) * P], Lm[p][:, lv, j, :], N[p][:, j, :],
                                             start=True, stop=True)
                        last.then_inc(s_Yp[p], 1)
                    for p in range(2):
                        b1 = bank[p][1]
                        pe.wait_ge(s_Y[p], LEVELS * i + lv + 1)
                        for j in range(2):
                            last = pe.matmul(b1[:, j * P:(j + 1) * P], N[p][:, 2 + j, :], Y[p][:, j, :],
                                             start=True, stop=True)
                        if lv < LEVELS - 1:
                            for j in range(2):
                                last = pe.matmul(b1[:, (2 + j) * P:(3 + j) * P], Y[p][:, j, :], N[p][:, 2 + j, :],
                                                 start=True, stop=True)
                        last.then_inc(s_dN[p], 1)
                for p in range(2):
                    b2 = bank[p][2]
                    pe.wait_ge(s_N[p], LEVELS * i + LEVELS)
                    pe.wait_ge(s_Dx[p], i + 1)
                    pe.matmul(b2[:, 0:P], N[p][:, 0, :], kv[p][:, 0, C:2 * C], start=True, stop=True)
                    pe.matmul(b2[:, P:2 * P], kv[p][:, 0, C:2 * C], N[p][:, 0, :], start=True,
                              stop=True).then_inc(s_w0p[p], 1)
                for p in range(2):
                    pe.wait_ge(s_w0[p], 2 * i + 2)
                    pe.wait_ge(s_L[p], i + 1)
                    pe.matmul(bank[p][3][:, 256:384], U[p][:, P:2 * P], W0[p][:, :], start=True,
                              stop=True).then_inc(s_v1p[p], 1)
                for p in range(2):
                    pe.wait_ge(s_v1[p], i + 1)
                    pe.matmul(bank[p][2][:, 2 * P:3 * P], v1[p][:, :], N[p][:, 1, :], start=True,
                              stop=True).then_inc(s_w1p[p], 1)
                for p in range(2):
                    b0 = bank[p][0]
                    pe.wait_ge(s_w1[p], i + 1)
                    pe.matmul(b0[:, 0:T], WT[p][:, 0:P], qT[p][:, :], start=True, stop=True)
                    pe.matmul(b0[:, T:T + P], WT[p][:, P:T], qT[p][:, P:T], start=True,
                              stop=True).then_inc(s_Ap[p], 1)
                for p in range(2):
                    b1 = bank[p][1]
                    pe.wait_ge(s_P[p], 2 * i + 2)
                    pe.matmul(b1[:, 0:T], kn[p][:, 0, :], Pm[p][:, 0:T], start=True, stop=False)
                    pe.matmul(b1[:, P:T], kn[p][:, 1, :], Pm[p][:, T:T + P], start=False,
                              stop=True).then_inc(s_op[p], 1)
                for p in range(2):
                    b2 = bank[p][2]
                    pe.wait_ge(s_og[p], i + 1)
                    for t in range(NT):
                        last = pe.matmul(b2[:, t * D:(t + 1) * D], oT[p][:, t * P:(t + 1) * P], Wo[:, :],
                                         start=True, stop=True)
                    last.then_inc(s_wop[p], 1)
                for p in range(2):
                    pe.wait_ge(s_xn[p], 6 * i + 4)
                    turn(p, bank[p][0], xn[p]).then_inc(s_tr[p], 1)
                for p in range(2):
                    b1 = bank[p][1]
                    pe.wait_ge(s_xT[p], 2 * i + 2)
                    for t in range(NT):
                        for k in range(ND):
                            last = pe.matmul(b1[:, t * P:t * P + V], xT[p][:, k, t * P:(t + 1) * P],
                                             cT[p][:, k, :], start=k == 0, stop=k == ND - 1)
                    last.then_inc(s_sc[p], 1)
                for p in range(2):
                    pe.wait_ge(s_es[p], 2 * i + 2)
                    for t in range(NT):
                        last = pe.transpose(bank[p][3][0:V, t * P:(t + 1) * P], es[p][:, t, :], ident[:, :])
                    last.then_inc(s_etr[p], 1)
                for p in range(2):
                    pe.wait_ge(s_eT[p], i + 1)
                    for t in range(NT):
                        last = pe.matmul(bank[p][2][:, t * D:(t + 1) * D], eT[p][:, t * P:(t + 1) * P],
                                         cx[p][:, :], start=True, stop=True)
                    last.then_inc(s_co[p], 1)


def phase_weights(nc, A, K):
    with ExitStack() as ctx:
        def sb(name, shape, dt=F32):
            return ctx.enter_context(nc.sbuf_tensor("w_" + name, shape, dt))

        def sem(name):
            return ctx.enter_context(nc.semaphore("w_" + name))

        square = {n: sb(n, [P, ND, D]) for n in ("wq", "wk", "wv", "wp", "xq", "xk", "xv", "xp", "wr", "wi")}
        dft = sb("dft", [P, 3, ND, D])
        gate = sb("gate", [P, NI, D])
        up = sb("up", [P, NI, D])
        down = sb("down", [P, ND, I])
        inv = sb("inv", [P, NI])
        t1 = sb("t1", [P, ND, D])
        t2 = sb("t2", [P, ND, D])
        bank = [ctx.enter_context(nc.psum_tensor(f"w_b{k}", [P, 512], F32)) for k in range(8)]
        s_in = sem("loaded")
        s_c = sem("cleared")
        s_q = sem("quantised")
        s_pe = sem("turned")
        s_ev = sem("evacuated")
        s_ch = sem("chain")
        block = ctx.enter_context(nc.Block())
        tiles = [(j, min(P, I - j * P)) for j in range(NI)]
        CLEARS = 5 + 4 + 5 + 4
        flat = {"wq": A["L1_attn_Wq"].rearrange("h e d -> (h e) d"), "wk": A["L1_attn_Wk"].rearrange("h e d -> (h e) d"),
                "wv": A["L1_attn_Wv"].rearrange("h e d -> (h e) d"), "wp": A["L1_attn_Wp"],
                "xq": A["L1_xattn_Wq"], "xk": A["L1_xattn_Wk"], "xv": A["L1_xattn_Wv"], "xp": A["L1_xattn_Wp"],
                "wr": A["L1_ffn_w_freq_real"], "wi": A["L1_ffn_w_freq_imag"]}

        @block.sync
        def _(sp):
            n = 0
            for name, w in flat.items():
                sp.dma_start(square[name][:, :, :], w.rearrange("(k p) d -> p k d", p=P)).then_inc(s_in, 16)
                n += 1
            for c in range(3):
                sp.dma_start(dft[:, c, :, :], A["dft"][c, :, :].rearrange("(k p) d -> p k d", p=P)).then_inc(s_in, 16)
            for dst, w in ((gate, A["L0_ffn_w_gate"]), (up, A["L0_ffn_w_up"])):
                sp.dma_start(dst[:, 0:NI - 1, :], w[0:(NI - 1) * P, :].rearrange("(k p) d -> p k d", p=P)).then_inc(s_in, 16)
                sp.dma_start(dst[0:LASTI, NI - 1, :], w[(NI - 1) * P:I, :]).then_inc(s_in, 16)
            sp.dma_start(down[:, :, :], A["L0_ffn_w_down"].rearrange("(k p) d -> p k d", p=P)).then_inc(s_in, 16)
            sp.wait_ge(s_c, 9)
            for name, dst in (("L1_attn_bq", K.bq), ("L1_attn_bk", K.bk)):
                for j in range(4):
                    sp.dma_start(dst[32 * j:32 * j + HD, :], A[name][j:H:4, :].rearrange("g e -> e g"),
                                 allow_slow_non_contiguous=True).then_inc(s_in, 16)
            for name, dst in (("L1_attn_bp", K.bp), ("L1_ffn_bias", K.bf)):
                sp.dma_start(dst[:, 0, :], A[name].partition_broadcast(P)).then_inc(s_in, 16)
            sp.dma_start(K.bv[:, 0, :], A["L1_attn_bv"].rearrange("h e -> (h e)").partition_broadcast(P)).then_inc(s_in, 16)
            sp.dma_start(K.clip[:, 0:1], A["L0_ffn_clip_x"].partition_broadcast(P)).then_inc(s_in, 16)
            sp.dma_start(K.clip[:, 1:2], A["L0_ffn_clip_down"].partition_broadcast(P)).then_inc(s_in, 16)
            sp.dma_start(K.focus[:, :], A["L1_xattn_focusing_factor"].partition_broadcast(P)).then_inc(s_in, 16)
            sp.dma_start(K.rank[:, 0, :], A["rank"].partition_broadcast(P)).then_inc(s_in, 16)

        LOADS = len(flat) + 3 + 4 + 1 + 8 + 7

        @block.gpsimd
        def _(pool):
            n = 0
            pool.memset(K.Wq[:, :, :], 0.0).then_inc(s_c, 1)
            pool.memset(K.Wk[:, :, :], 0.0).then_inc(s_c, 1)
            pool.memset(K.wd[:, :, :], 0.0).then_inc(s_c, 1)
            for t in (K.bq, K.bk):
                pool.memset(t[:, :], 0.0).then_inc(s_c, 1)
            n = 5
            for j in range(4):
                pool.wait_ge(s_c, n)
                pool.affine_select(out=K.bk[:, :], in_=K.bk[:, :], compare_op=ALU.not_equal, fill=1.0,
                                   base=-(32 * j + HD), pattern=[[0, 4]], channel_multiplier=1).then_inc(s_c, 1)
                n += 1
            pool.memset(K.magic[:, :], -MAGIC).then_inc(s_c, 1)
            pool.memset(K.eps[:, :], EPS).then_inc(s_c, 1)
            pool.memset(K.one77[:, :], 1.0 / V).then_inc(s_c, 1)
            pool.memset(K.heads[:, :, :], 1.0).then_inc(s_c, 1)
            pool.memset(K.blocks[:, :, :], 1.0 / T).then_inc(s_c, 1)
            n += 5
            pool.wait_ge(s_c, n)
            for out, w in ((K.heads, 1), (K.blocks, HD)):
                pool.affine_select(out=out[:, :, :], in_=out[:, :, :], compare_op=ALU.is_ge, fill=0.0, base=0,
                                   pattern=[[-HD, P // HD], [0, w]], channel_multiplier=1).then_inc(s_c, 1)
            pool.wait_ge(s_c, n + 2)
            for out, w in ((K.heads, 1), (K.blocks, HD)):
                pool.affine_select(out=out[:, :, :], in_=out[:, :, :], compare_op=ALU.is_gt, fill=0.0, base=HD,
                                   pattern=[[HD, P // HD], [0, w]], channel_multiplier=-1).then_inc(s_c, 1)

        @block.vector
        def _(dve):
            n = 0

            def link(ins):
                nonlocal n
                n += 1
                ins.then_inc(s_ch, 1)
                dve.wait_ge(s_ch, n)

            dve.wait_ge(s_in, 16 * LOADS)
            dve.wait_ge(s_c, CLEARS)
            link(dve.tensor_scalar(K.bq[:, :], K.bq[:, :], 0.25, None, ALU.mult))

            def quantise(part, scale, inv):
                link(dve.tensor_reduce(scale, part, axis=AX_X, op=ALU.max, apply_absolute_value=True))
                link(dve.tensor_scalar(scale, scale, 1.0 / QMAX, None, ALU.mult))
                link(dve.reciprocal(inv, scale))
                link(dve.tensor_scalar(part, part, inv, QMAX, ALU.mult, ALU.min))
                link(dve.tensor_scalar(part, part, -QMAX - 1.0, MAGIC, ALU.max, ALU.add))
                link(dve.tensor_scalar(part, part, -MAGIC, None, ALU.add))

            for w, scale in ((gate, K.sgate), (up, K.sup)):
                for j, m in tiles:
                    quantise(w[0:m, j, :], scale[0:m, j:j + 1], inv[0:m, 0:1])
            for k in range(ND):
                quantise(down[:, k, :], K.sdown[:, k:k + 1], inv[:, 0:1])
            for k in range(ND):
                link(dve.tensor_copy(K.srep[:, k, :], K.sdown[:, k:k + 1].to_broadcast([P, P])))
            dve.memset(inv[:, 0:1], 0.0).then_inc(s_q, 1)

        jobs = []

        def turn(name, out, scale=1.0):
            def go(pe, b):
                for k in range(ND):
                    for o in range(ND):
                        last = pe.transpose(b[:, k * D + o * P:k * D + (o + 1) * P],
                                            square[name][:, o, k * P:(k + 1) * P], K.ident[:, :])
                return last
            jobs.append((go, lambda act, b: act.activation(out, b[:, :], ACT.Copy, scale=scale)))

        def turn_padded(name, out, scale):
            def go(pe, b):
                for k in range(ND):
                    for o in range(ND):
                        last = pe.transpose(b[:, k * D + o * P:k * D + (o + 1) * P],
                                            square[name][:, o, k * P:(k + 1) * P], K.ident[:, :])
                return last
            jobs.append((go, lambda act, b: act.activation(
                out[:, :, :].rearrange("p k (h r) -> p (k h) r", r=32)[:, :, 0:HD],
                b[:, :].rearrange("p (h e) -> p h e", e=HD), ACT.Copy, scale=scale)))

        def mix(terms, out, scale):
            def go(pe, b):
                for m in range(ND):
                    for n, (x, y, k) in enumerate([(x, y, k) for x, y in terms for k in range(ND)]):
                        last = pe.matmul(b[:, m * D:(m + 1) * D], x[:, k, m * P:(m + 1) * P], y[:, k, :],
                                         start=n == 0, stop=n == 2 * ND - 1)
                return last
            jobs.append((go, lambda act, b: act.activation(out[:, :, :], b[:, :], ACT.Copy, scale=scale)))

        mix([(square["wr"], dft[:, 0]), (square["wi"], dft[:, 1])], t1, 1.0)
        mix([(square["wi"], dft[:, 0]), (square["wr"], dft[:, 2])], t2, 1.0)
        turn_padded("wq", K.Wq, 0.25)
        turn_padded("wk", K.Wk, 1.0)
        turn("wv", K.Wv[:, :, :])
        turn("wp", K.Wp[:, :, :])
        turn("xq", K.Xq[:, :, :])
        turn("xk", K.Xkv[:, :, 0:D])
        turn("xv", K.Xkv[:, :, D:2 * D])
        turn("xp", K.Xp[:, :, :])
        mix([(t1, dft[:, 0]), (t2, dft[:, 2])], K.M, 1.0 / D)
        PLAIN = len(jobs)
        for w, out in ((gate, K.wg), (up, K.wu)):
            for k in range(ND):
                for js in (range(0, 4), range(4, NI)):
                    def go(pe, b, w=w, k=k, js=js):
                        for j in js:
                            m = min(P, I - j * P)
                            last = pe.transpose(b[:, (j - js[0]) * P:(j - js[0]) * P + m],
                                                w[0:m, j, k * P:(k + 1) * P], K.ident[0:m, 0:m])
                        return last
                    lo, hi = js[0] * P, min(I, (js[-1] + 1) * P)
                    jobs.append((go, lambda act, b, out=out, k=k, lo=lo, hi=hi:
                                 act.activation(out[:, k, lo:hi], b[:, 0:hi - lo], ACT.Copy)))
        for j, m in tiles:
            def go(pe, b, j=j, m=m):
                for k in range(ND):
                    last = pe.transpose(b[0:m, k * P:(k + 1) * P], down[:, k, j * P:j * P + m], K.ident[:, :])
                return last
            jobs.append((go, lambda act, b, j=j, m=m: act.activation(K.wd[0:m, j, :], b[0:m, 0:D], ACT.Copy)))

        def scales(pe, b):
            for k in range(ND):
                last = pe.matmul(b[:, k * P:(k + 1) * P], K.srep[:, k, :], K.ident[:, :], start=True, stop=True)
            return last
        jobs.append((scales, lambda act, b: act.activation(K.srow[:, 0, :], b[:, 0:D], ACT.Copy)))

        @block.tensor
        def _(pe):
            pe.wait_ge(s_in, 16 * LOADS)
            for n, (go, _) in enumerate(jobs):
                if n >= 8:
                    pe.wait_ge(s_ev, n - 7)
                if n == PLAIN - 1:
                    pe.wait_ge(s_ev, 2)
                if n == PLAIN:
                    pe.wait_ge(s_q, 1)
                go(pe, bank[n % 8]).then_inc(s_pe, 1)

        @block.scalar
        def _(act):
            act.wait_ge(s_c, CLEARS)
            for n, (_, take) in enumerate(jobs):
                act.wait_ge(s_pe, n + 1)
                take(act, bank[n % 8]).then_inc(s_ev, 1)
            act.wait_ge(s_ev, len(jobs))


def phase_gate_up(nc, K, xn3, hs):
    with ExitStack() as ctx:
        def sb(name, shape, dt=F32):
            return ctx.enter_context(nc.sbuf_tensor("b_" + name, shape, dt))

        def sb2(name, shape, dt=F32):
            return [sb(f"{name}{p}", shape, dt) for p in range(2)]

        def sem(name):
            return ctx.enter_context(nc.semaphore("b_" + name))

        def sem2(name):
            return [sem(f"{name}{p}") for p in range(2)]

        BANKS = 3
        x = sb2("x", [P, NT, D])
        xq = sb2("xq", [P, NT, D])
        xT = sb2("xT", [P, ND, T], BF16)
        si = [sb2(f"si{r}", [P, T]) for r in range(BANKS)]
        h = sb2("h", [P, NI, T])
        part = sb2("part", [P, 1])
        pk = sb2("pk", [P, 1])
        sg = sb("sg", [P, NI])
        su = sb("su", [P, NI])
        g = sb("g", [P, 4])
        tr = [ctx.enter_context(nc.psum_tensor(f"b_t{p}", [P, 512], F32)) for p in range(2)]
        gu = [[ctx.enter_context(nc.psum_tensor(f"b_g{p}{r}", [P, 512], F32)) for r in range(BANKS)]
              for p in range(2)]
        s_g = sem("peak_all")
        s_e = sem("clip_exp")
        s_ch = sem("chain")
        s_sc = sem("scales")
        s_z = sem("zeroed")
        s_x = sem2("x_in")
        s_q1 = sem2("clipped")
        s_q2 = sem2("rounded")
        s_tr = sem2("turned")
        s_xT = sem2("xT")
        s_gu = [sem2(f"gate_up{r}") for r in range(BANKS)]
        s_si = [sem2(f"silu{r}") for r in range(BANKS)]
        s_h = [sem2(f"h{r}") for r in range(BANKS)]
        s_pp = sem2("part")
        s_pk = sem2("peak")
        s_out = sem2("stored")
        block = ctx.enter_context(nc.Block())
        tiles = [(j, min(P, I - j * P)) for j in range(NI)]

        @block.sync
        def _(sp):
            for p in range(2):
                sp.dma_start(x[p][:, :, :], rows(xn3, p)).then_inc(s_x[p], 16)
            with sp.Fori(0, PAIRS - 1) as i:
                for p in range(2):
                    sp.wait_ge(s_q1[p], i + 1)
                    sp.dma_start(x[p][:, :, :], rows(xn3, 2 * i + 2 + p)).then_inc(s_x[p], 16)

        @block.gpsimd
        def _(pool):
            pool.partition_all_reduce(g[:, 0:1], K.peak[:, :], P, RMAX).then_inc(s_g, 1)
            for p in range(2):
                pool.memset(h[p][:, :, :], 0.0).then_inc(s_z, 1)
                pool.memset(pk[p][:, :], 0.0).then_inc(s_z, 1)
            with pool.Fori(0, PAIRS) as i:
                for p in range(2):
                    for r in range(BANKS):
                        pool.wait_ge(s_h[r][p], 2 * i + 2)
                    pool.dma_start(hs[bass.ds(2 * i + p, 1), :, :].rearrange("o p c -> p (o c)"),
                                   h[p][:, :, :].rearrange("p j t -> p (j t)")).then_inc(s_out[p], 16)
            for p in range(2):
                pool.wait_ge(s_out[p], 16 * PAIRS)

        @block.scalar
        def _(act):
            act.activation(K.cexp[:, :], K.clip[:, :], ACT.Exp, scale=-1.0).then_inc(s_e, 1)
            act.wait_ge(s_sc, 1)
            with act.Fori(0, PAIRS) as i:
                for p in range(2):
                    act.wait_ge(s_tr[p], i + 1)
                    act.activation(xT[p][:, :, :], tr[p][:, :], ACT.Identity,
                                   bias=K.magic[:, :]).then_inc(s_xT[p], 1)
                for j, m in tiles:
                    r = j % BANKS
                    for p in range(2):
                        act.wait_ge(s_gu[r][p], 2 * i + 1 + j // BANKS)
                        act.activation(si[r][p][0:m, :], gu[p][r][0:m, 0:T], ACT.Silu,
                                       scale=sg[0:m, j:j + 1]).then_inc(s_si[r][p], 1)

        @block.vector
        def _(dve):
            n = 0

            def link(ins):
                nonlocal n
                n += 1
                ins.then_inc(s_ch, 1)
                dve.wait_ge(s_ch, n)

            dve.wait_ge(s_e, 1)
            link(dve.tensor_scalar(K.cexp[:, :], K.cexp[:, :], 1.0, None, ALU.add))
            link(dve.reciprocal(K.csig[:, :], K.cexp[:, :]))
            dve.wait_ge(s_g, 1)
            link(dve.tensor_tensor(g[:, 1:2], g[:, 0:1], K.csig[:, 0:1], ALU.mult))
            link(dve.tensor_scalar(g[:, 1:2], g[:, 1:2], 1.0 / QMAX, None, ALU.mult))
            link(dve.reciprocal(g[:, 2:3], g[:, 1:2]))
            link(dve.tensor_scalar(sg[:, 0:NI - 1], K.sgate[:, 0:NI - 1], g[:, 1:2], None, ALU.mult))
            link(dve.tensor_scalar(su[:, 0:NI - 1], K.sup[:, 0:NI - 1], g[:, 1:2], None, ALU.mult))
            link(dve.tensor_scalar(sg[0:LASTI, NI - 1:NI], K.sgate[0:LASTI, NI - 1:NI], g[0:LASTI, 1:2], None, ALU.mult))
            dve.tensor_scalar(su[0:LASTI, NI - 1:NI], K.sup[0:LASTI, NI - 1:NI], g[0:LASTI, 1:2], None,
                              ALU.mult).then_inc(s_sc, 1)
            dve.wait_ge(s_sc, 1)
            dve.wait_ge(s_z, 4)
            with dve.Fori(0, PAIRS) as i:
                for p in range(2):
                    dve.wait_ge(s_x[p], 16 * i + 16)
                    dve.wait_ge(s_tr[p], i)
                    dve.tensor_scalar(xq[p][:, :, :], x[p][:, :, :], g[:, 2:3], QMAX, ALU.mult,
                                      ALU.min).then_inc(s_q1[p], 1)
                for p in range(2):
                    dve.wait_ge(s_q1[p], i + 1)
                    dve.tensor_scalar(xq[p][:, :, :], xq[p][:, :, :], -QMAX - 1.0, MAGIC, ALU.max,
                                      ALU.add).then_inc(s_q2[p], 1)
                for p in range(2):
                    dve.wait_ge(s_out[p], 16 * i)
                for j, m in tiles:
                    r = j % BANKS
                    for p in range(2):
                        dve.wait_ge(s_si[r][p], 2 * i + 1 + j // BANKS)
                        dve.scalar_tensor_tensor(h[p][0:m, j, :], gu[p][r][0:m, T:2 * T], su[0:m, j:j + 1],
                                                 si[r][p][0:m, :], ALU.mult, ALU.mult).then_inc(s_h[r][p], 1)
                for p in range(2):
                    for r in range(BANKS):
                        dve.wait_ge(s_h[r][p], 2 * i + 2)
                    dve.tensor_reduce(part[p][:, :], h[p][:, :, :], axis=mybir.AxisListType.XY, op=ALU.max,
                                      apply_absolute_value=True).then_inc(s_pp[p], 1)
                for p in range(2):
                    dve.wait_ge(s_pp[p], i + 1)
                    dve.tensor_tensor(pk[p][:, :], pk[p][:, :], part[p][:, :], ALU.max).then_inc(s_pk[p], 1)
            for p in range(2):
                dve.wait_ge(s_pk[p], PAIRS)
            dve.tensor_tensor(K.hpeak[:, :], pk[0][:, :], pk[1][:, :], ALU.max).then_inc(s_sc, 1)
            dve.wait_ge(s_sc, 2)

        @block.tensor
        def _(pe):
            with pe.Fori(0, PAIRS) as i:
                for p in range(2):
                    pe.wait_ge(s_q2[p], i + 1)
                    for k in range(ND):
                        for t in range(NT):
                            last = pe.transpose(tr[p][:, k * T + t * P:k * T + (t + 1) * P],
                                                xq[p][:, t, k * P:(k + 1) * P], K.ident[:, :])
                    last.then_inc(s_tr[p], 1)
                for p in range(2):
                    pe.wait_ge(s_xT[p], i + 1)
                for j, m in tiles:
                    r = j % BANKS
                    for p in range(2):
                        pe.wait_ge(s_h[r][p], 2 * i + j // BANKS)
                        for c, w in enumerate((K.wg, K.wu)):
                            for k in range(ND):
                                last = pe.matmul(gu[p][r][0:m, c * T:(c + 1) * T], w[:, k, j * P:j * P + m],
                                                 xT[p][:, k, :], start=k == 0, stop=k == ND - 1)
                        last.then_inc(s_gu[r][p], 1)


def phase_tail(nc, A, K, x2, hs, out):
    with ExitStack() as ctx:
        def sb(name, shape, dt=F32):
            return ctx.enter_context(nc.sbuf_tensor("c_" + name, shape, dt))

        def sb2(name, shape, dt=F32):
            return [sb(f"{name}{p}", shape, dt) for p in range(2)]

        def sem(name):
            return ctx.enter_context(nc.semaphore("c_" + name))

        def sem2(name):
            return [sem(f"{name}{p}") for p in range(2)]

        STEPS = H // 2
        NE = 4
        KW = P + P // HD
        half = sb("half", [P, NT])
        lneps = sb("lneps", [P, NT])
        g = sb("g", [P, 4])
        srow = sb("srow", [P, 1, D])
        idle = sb2("idle", [P, 1])
        h = sb2("h", [P, NI, T])
        hq = sb2("hq", [P, NI, T], BF16)
        x = sb2("x", [P, NT, D])
        x3 = sb2("x3", [P, NT, D])
        xb = sb2("xb", [P, NT, D])
        x4 = sb2("x4", [P, NT, D])
        xn = sb2("xn", [P, NT, D])
        xT = sb2("xT", [P, ND, T])
        stats = sb2("stats", [P, NT, 6])
        mv = sb2("mv", [P, NT, 2])
        rstd = sb2("rstd", [P, NT])
        QT = sb2("QT", [P, 4, T])
        KT = sb2("KT", [P, 4, T])
        vs = sb2("vs", [P, NT, H, 32])
        mx = sb2("mx", [P, NT, H, 32])
        E = [sb(f"E{n}", [P, 2, NT, T]) for n in range(NE)]
        oT = sb2("oT", [P, 4, T])
        ro = sb2("ro", [P, NT, H])
        o = sb2("o", [P, NT, D])
        cx = sb2("cx", [V, D])
        cT = sb2("cT", [P, ND, V])
        kvc = sb2("kvc", [V, 2 * D])
        kl = sb2("kl", [V, 1, D])
        ke = sb2("ke", [V, 1, D])
        kk = sb2("kk", [V, 1, D], I32)
        kt = sb2("kt", [V, H, 8])
        ks = sb2("ks", [V, 4])
        KV = sb2("KV", [P, ND, KW])
        qe = sb2("qe", [P, NT, D])
        qk = sb2("qk", [P, NT, D], I32)
        qt = sb2("qt", [P, NT * H, 8])
        qs = sb2("qs", [P, 4, NT])
        rz = sb2("rz", [P, NT, ND, P // HD])
        xo = sb2("xo", [P, NT, D])
        S = [ctx.enter_context(nc.psum_tensor(f"c_s{r}", [P, 1024], F32)) for r in range(2)]
        m0 = [ctx.enter_context(nc.psum_tensor(f"c_m0{p}", [P, 512], F32)) for p in range(2)]
        m1 = [ctx.enter_context(nc.psum_tensor(f"c_m1{p}", [P, 512], F32)) for p in range(2)]

        s_g = sem("peak_all")
        s_ch = sem("chain")
        s_c = sem("constants")
        s_h = sem2("h_in")
        s_x = sem2("x_in")
        s_cx = sem2("ctx_in")
        s_h1 = sem2("h_clipped")
        s_h2 = sem2("h_rounded")
        s_hq = sem2("hq")
        s_dn = sem2("down")
        s_xs = sem2("down_scaled")
        s_x3 = sem2("x3")
        s_xb = sem2("residual_bias")
        s_st = sem2("stats")
        s_mv = sem2("meanvar")
        s_ve = sem2("vareps")
        s_rs = sem2("rstd")
        s_xn = sem2("xn")
        s_tr = sem2("turned")
        s_xT = sem2("xT")
        s_ctr = sem2("ctx_turned")
        s_cT = sem2("cT")
        s_ckv = sem2("ctx_kv_product")
        s_kvc = sem2("ctx_kv")
        s_kf = sem2("k_focus")
        s_kln = sem2("k_log")
        s_ke = sem2("k_exp")
        s_vp = sem2("v_product")
        s_vs = sem2("v")
        s_qp = sem2("q_product")
        s_q = sem2("q")
        s_kp = sem2("k_product")
        s_k = sem2("k")
        s_s1 = [sem(f"scores_st{r}") for r in range(2)]
        s_mx = [sem(f"maxima{r}") for r in range(2)]
        s_mt = sem2("maxima_turned")
        s_qm = sem2("q_with_maxima")
        s_s2 = [sem(f"scores_ts{r}") for r in range(2)]
        s_ex = [sem(f"exponentials{r}") for r in range(2)]
        s_av = [sem(f"weighted{n}") for n in range(NE)]
        s_ao = sem2("attention_out")
        s_oT = sem2("oT")
        s_ob = sem2("o_turned")
        s_ro = sem2("ro")
        s_o = sem2("o")
        s_pr = sem2("projected")
        s_x4 = sem2("x4")
        s_xq = sem2("q_pre")
        s_kv = sem2("kv_product")
        s_KV = sem2("KV")
        s_qf = sem2("q_focus")
        s_qln = sem2("q_log")
        s_qe = sem2("q_exp")
        s_y = sem2("y_product")
        s_z = sem2("z")
        s_yn = sem2("y")
        s_x5 = sem2("x5")
        s_x6 = sem2("x6")
        s_out = sem2("stored")
        block = ctx.enter_context(nc.Block())
        TURNS = 6
        PRE = 6

        @block.sync
        def _(sp):
            def load_h(p, b):
                sp.dma_start(h[p][:, :, :].rearrange("p j t -> p (j t)"),
                             hs[bass.ds(b, 1), :, :].rearrange("o p c -> p (o c)")).then_inc(s_h[p], 16)

            def load_x(p, b):
                sp.dma_start(x[p][:, :, :], rows(x2, b)).then_inc(s_x[p], 16)

            def load_ctx(p, b):
                sp.dma_start(cx[p][:, :], A["ctx_1024"][bass.ds(b, 1), :, :]
                             .rearrange("o v d -> v (o d)")).then_inc(s_cx[p], 16)

            for p in range(2):
                load_h(p, p)
                load_ctx(p, p)
                load_x(p, p)
            with sp.Fori(0, PAIRS - 1) as i:
                for p in range(2):
                    sp.wait_ge(s_hq[p], i + 1)
                    load_h(p, 2 * i + 2 + p)
                    sp.wait_ge(s_ctr[p], i + 1)
                    load_ctx(p, 2 * i + 2 + p)
                    sp.wait_ge(s_x3[p], i + 1)
                    load_x(p, 2 * i + 2 + p)
                for p in range(2):
                    sp.wait_ge(s_x6[p], i + 1)
                    sp.dma_start(rows(out, 2 * i + p), xo[p][:, :, :]).then_inc(s_out[p], 16)
            for p in range(2):
                sp.wait_ge(s_x6[p], PAIRS)
                sp.dma_start(rows(out, 2 * (PAIRS - 1) + p), xo[p][:, :, :]).then_inc(s_out[p], 16)
            for p in range(2):
                sp.wait_ge(s_out[p], 16 * PAIRS)

        @block.gpsimd
        def _(pool):
            pool.partition_all_reduce(g[:, 0:1], K.hpeak[:, :], P, RMAX).then_inc(s_g, 1)
            pool.memset(half[:, :], -0.5).then_inc(s_c, 1)
            pool.memset(lneps[:, :], LN_EPS).then_inc(s_c, 1)
            for p in range(2):
                pool.memset(mx[p][:, :, :, :], 0.0).then_inc(s_c, 1)
                pool.memset(vs[p][:, :, :, :], 0.0).then_inc(s_c, 1)
            pool.wait_ge(s_c, PRE)
            for p in range(2):
                pool.memset(vs[p][:, :, :, HD:HD + 1], 1.0).then_inc(s_c, 1)

            def rsqrt(p, n):
                pool.wait_ge(s_mv[p], 6 * i + 2 * n + 2)
                pool.wait_ge(s_xn[p], 6 * i + 2 * n)
                pool.tensor_tensor(rstd[p][:, :], mv[p][:, :, 1], lneps[:, :], ALU.add).then_inc(s_ve[p], 1)
                pool.wait_ge(s_ve[p], 3 * i + n + 1)
                pool.tensor_tensor(rstd[p][:, :], rstd[p][:, :], half[:, :], ALU.pow).then_inc(s_rs[p], 1)

            with pool.Fori(0, PAIRS) as i:
                for p in range(2):
                    rsqrt(p, 0)
                for p in range(2):
                    pool.wait_ge(s_x3[p], i + 1)
                    pool.wait_ge(s_x6[p], i)
                    pool.tensor_tensor(xb[p][:, :, :], x3[p][:, :, :], K.bp[:, :, :].to_broadcast([P, NT, D]),
                                       ALU.add).then_inc(s_xb[p], 1)
                for p in range(2):
                    rsqrt(p, 1)
                for p in range(2):
                    rsqrt(p, 2)
                    pool.wait_ge(s_x5[p], i + 1)
                    pool.tensor_tensor(xb[p][:, :, :], x3[p][:, :, :], K.bf[:, :, :].to_broadcast([P, NT, D]),
                                       ALU.add).then_inc(s_xb[p], 1)

        @block.scalar
        def _(act):
            with act.Fori(0, PAIRS) as i:
                for p in range(2):
                    act.wait_ge(s_ctr[p], i + 1)
                    act.copy(cT[p][:, :, :], m1[p][:, 0:ND * V]).then_inc(s_cT[p], 1)
                for p in range(2):
                    act.wait_ge(s_h2[p], i + 1)
                    act.activation(hq[p][:, :, :], h[p][:, :, :], ACT.Identity,
                                   bias=K.magic[:, :]).then_inc(s_hq[p], 1)
                for p in range(2):
                    act.wait_ge(s_ckv[p], i + 1)
                    act.copy(kvc[p][:, :], m1[p][0:V, :]).then_inc(s_kvc[p], 1)
                for p in range(2):
                    act.wait_ge(s_kf[p], 7 * i + 1)
                    act.activation(kl[p][:, 0, :], kl[p][:, 0, :], ACT.Ln, bias=K.eps[0:V, :]).then_inc(s_kln[p], 1)
                for p in range(2):
                    act.wait_ge(s_kf[p], 7 * i + 3)
                    act.activation(ke[p][:, 0, :], kl[p][:, 0, :], ACT.Exp, bias=ks[p][:, 1:2],
                                   accum_out=ks[p][:, 2:3]).then_inc(s_ke[p], 1)

                def turned(p, n, bank):
                    act.wait_ge(s_tr[p], TURNS * i + n + 1)
                    act.copy(xT[p][:, :, :], bank[p][:, :]).then_inc(s_xT[p], 1)

                for p in range(2):
                    turned(p, 0, m1)
                for p in range(2):
                    for c in range(2):
                        act.wait_ge(s_qp[p], 2 * i + c + 1)
                        for gg in (2 * c, 2 * c + 1):
                            act.activation(QT[p][:, gg, :], (m1, m0)[c][p][:, (gg % 2) * T:(gg % 2 + 1) * T],
                                           ACT.Identity, bias=K.bq[:, gg:gg + 1]).then_inc(s_q[p], 1)
                    for c in range(2):
                        act.wait_ge(s_kp[p], 2 * i + c + 1)
                        for gg in (2 * c, 2 * c + 1):
                            act.activation(KT[p][:, gg, :], (m1, m0)[c][p][:, (gg % 2) * T:(gg % 2 + 1) * T],
                                           ACT.Identity, bias=K.bk[:, gg:gg + 1]).then_inc(s_k[p], 1)
                for p in range(2):
                    for u in range(STEPS):
                        n = p * STEPS + u
                        act.wait_ge(s_s2[u % 2], STEPS * i + n // 2 + 1)
                        act.wait_ge(s_av[n % NE], 4 * i + n // NE)
                        act.activation(E[n % NE][:, :, :, :], S[u % 2][:, :], ACT.Exp).then_inc(s_ex[u % 2], 1)
                    act.wait_ge(s_ao[p], i + 1)
                    for c in range(2):
                        act.copy(oT[p][:, 2 * c:2 * c + 2, :], (m0, m1)[c][p][:, :]).then_inc(s_oT[p], 1)
                for p in range(2):
                    turned(p, 1, m0)
                for p in range(2):
                    turned(p, 2, m0)
                for p in range(2):
                    act.wait_ge(s_xq[p], i + 1)
                    act.copy(qe[p][:, :, :], m1[p][:, :]).then_inc(s_qe[p], 1)
                for p in range(2):
                    act.wait_ge(s_qf[p], 9 * i + 2)
                    act.activation(o[p][:, :, :], o[p][:, :, :], ACT.Ln, bias=K.eps[:, :]).then_inc(s_qln[p], 1)
                for p in range(2):
                    act.wait_ge(s_qf[p], 9 * i + 4)
                    for t in range(NT):
                        act.activation(qe[p][:, t, :], o[p][:, t, :], ACT.Exp, bias=qs[p][:, 1, t:t + 1],
                                       accum_out=qs[p][:, 2, t:t + 1]).then_inc(s_qe[p], 1)
                for n in (3, 4, 5):
                    for p in range(2):
                        turned(p, n, m0)

        @block.vector
        def _(dve):
            n = 0

            def link(ins):
                nonlocal n
                n += 1
                ins.then_inc(s_ch, 1)
                dve.wait_ge(s_ch, n)

            dve.wait_ge(s_g, 1)
            link(dve.tensor_tensor(g[:, 1:2], g[:, 0:1], K.csig[:, 1:2], ALU.mult))
            link(dve.tensor_scalar(g[:, 1:2], g[:, 1:2], 1.0 / QMAX, None, ALU.mult))
            link(dve.reciprocal(g[:, 2:3], g[:, 1:2]))
            link(dve.tensor_scalar(srow[:, 0, :], K.srow[:, 0, :], g[:, 1:2], None, ALU.mult))
            dve.wait_ge(s_c, PRE + 2)

            def stat(src, p, n):
                for t in range(NT):
                    dve.bn_stats(stats[p][:, t, :], src[:, t, :]).then_inc(s_st[p], 1)
                dve.wait_ge(s_st[p], 6 * i + 2 * n + 2)
                dve.memset(idle[p][:, :], 0.0)
                for t in range(NT):
                    dve.bn_aggr(mv[p][:, t, :], stats[p][:, t, :]).then_inc(s_mv[p], 1)

            def normed(src, p, n):
                for t in range(NT):
                    dve.wait_ge(s_rs[p], 3 * i + n + 1)
                    dve.tensor_scalar(xn[p][:, t, :], src[:, t, :], mv[p][:, t, 0:1], rstd[p][:, t:t + 1],
                                      ALU.subtract, ALU.mult).then_inc(s_xn[p], 1)

            SMALL = HD - KEEP
            with dve.Fori(0, PAIRS) as i:
                for p in range(2):
                    dve.wait_ge(s_h[p], 16 * i + 16)
                    dve.tensor_scalar(h[p][:, :, :], h[p][:, :, :], g[:, 2:3], QMAX, ALU.mult,
                                      ALU.min).then_inc(s_h1[p], 1)
                for p in range(2):
                    dve.wait_ge(s_h1[p], i + 1)
                    dve.tensor_scalar(h[p][:, :, :], h[p][:, :, :], -QMAX - 1.0, MAGIC, ALU.max,
                                      ALU.add).then_inc(s_h2[p], 1)
                for p in range(2):
                    dve.wait_ge(s_kvc[p], i + 1)
                    dve.scalar_tensor_tensor(kl[p][:, 0, :], kvc[p][:, 0:D], -0.01, kvc[p][:, 0:D],
                                             ALU.mult, ALU.max, accum_out=ks[p][:, 0:1]).then_inc(s_kf[p], 1)
                for p in range(2):
                    dve.wait_ge(s_dn[p], i + 1)
                    dve.tensor_tensor(x3[p][:, :, :], m0[p][:, :].rearrange("p (t d) -> p t d", t=NT),
                                      srow[:, :, :].to_broadcast([P, NT, D]), ALU.mult).then_inc(s_xs[p], 1)
                    dve.wait_ge(s_xs[p], i + 1)
                    dve.wait_ge(s_x[p], 16 * i + 16)
                    dve.tensor_tensor(x3[p][:, :, :], x3[p][:, :, :], x[p][:, :, :], ALU.add).then_inc(s_x3[p], 1)
                    dve.wait_ge(s_x3[p], i + 1)
                    stat(x3[p], p, 0)
                for p in range(2):
                    normed(x3[p], p, 0)
                for p in range(2):
                    dve.wait_ge(s_kln[p], i + 1)
                    dve.tensor_scalar(kl[p][:, 0, :], kl[p][:, 0, :], K.focus[0:V, :], None,
                                      ALU.mult).then_inc(s_kf[p], 1)
                    dve.wait_ge(s_kf[p], 7 * i + 2)
                    dve.tensor_reduce(ks[p][:, 1:2], kl[p][:, 0, :], axis=AX_X, op=ALU.max,
                                      negate=True).then_inc(s_kf[p], 1)
                for p in range(2):
                    dve.wait_ge(s_vp[p], i + 1)
                    dve.tensor_tensor(vs[p][:, :, :, 0:HD],
                                      m0[p][:, :].rearrange("p (t h e) -> p t h e", t=NT, h=H),
                                      K.bv[:, :, :].rearrange("p o (h e) -> p o h e", h=H)
                                      .to_broadcast([P, NT, H, HD]), ALU.add).then_inc(s_vs[p], 1)
                for p in range(2):
                    dve.wait_ge(s_ke[p], i + 1)
                    dve.scalar_tensor_tensor(kk[p][:, :, :], ke[p][:, :, :].bitcast(I32), -16,
                                             K.rank[0:V, :, :], ALU.bitwise_and,
                                             ALU.bitwise_or).then_inc(s_kf[p], 1)
                    dve.reciprocal(ks[p][:, 2:3], ks[p][:, 2:3]).then_inc(s_kf[p], 1)
                    dve.tensor_scalar(ks[p][:, 0:1], ks[p][:, 0:1], 1.0 / D, EPS, ALU.mult,
                                      ALU.add).then_inc(s_kf[p], 1)
                for p in range(2):
                    dve.wait_ge(s_kf[p], 7 * i + 6)
                    dve.memset(idle[p][:, :], 0.0)
                    for hh in range(H):
                        last = dve.max(kt[p][:, hh, :], kk[p][:, 0, hh * HD:(hh + 1) * HD].bitcast(F32))
                    last.then_inc(s_kf[p], 1)
                for p in range(2):
                    dve.wait_ge(s_kf[p], 7 * i + 7)
                    dve.tensor_tensor(kl[p][:, 0, :].rearrange("p (h e) -> p h e", h=H),
                                      kk[p][:, 0, :].bitcast(F32).rearrange("p (h e) -> p h e", h=H),
                                      kt[p][:, :, SMALL - 1:SMALL].to_broadcast([V, H, HD]),
                                      ALU.is_lt).then_inc(s_KV[p], 1)
                    dve.tensor_scalar(ks[p][:, 3:4], ks[p][:, 2:3], ks[p][:, 0:1], None, ALU.mult).then_inc(s_KV[p], 1)
                for p in range(2):
                    dve.wait_ge(s_KV[p], 5 * i + 2)
                    dve.scalar_tensor_tensor(ke[p][:, 0, :], kl[p][:, 0, :], ks[p][:, 3:4], ke[p][:, 0, :],
                                             ALU.mult, ALU.mult).then_inc(s_KV[p], 1)
                for p in range(2):
                    for u in range(STEPS):
                        n = p * STEPS + u
                        dve.wait_ge(s_s1[u % 2], STEPS * i + n // 2 + 1)
                        dve.tensor_reduce(mx[p][:, :, 2 * u:2 * u + 2, HD].rearrange("p t h -> p h t"),
                                          S[u % 2][:, :].rearrange("p (h t s) -> p h t s", h=2, t=NT),
                                          axis=AX_X, op=ALU.max, negate=True).then_inc(s_mx[u % 2], 1)
                for p in range(2):
                    for c in range(2):
                        dve.wait_ge(s_mt[p], 2 * i + c + 1)
                        dve.tensor_tensor(QT[p][:, 2 * c:2 * c + 2, :], QT[p][:, 2 * c:2 * c + 2, :],
                                          (m0, m1)[c][p][:, :].rearrange("p (g s) -> p g s", g=2),
                                          ALU.add).then_inc(s_qm[p], 1)
                for p in range(2):
                    dve.wait_ge(s_ob[p], i + 1)
                    ob = [b[p][:, :].rearrange("p (h r) -> p h r", r=32) for b in (m0, m1)]
                    for t in range(NT):
                        dve.reciprocal(ro[p][:, t, :], ob[t][:, :, HD]).then_inc(s_ro[p], 1)
                    dve.wait_ge(s_ro[p], 2 * i + 2)
                    for t in range(NT):
                        dve.tensor_tensor(o[p][:, t, :].rearrange("p (h e) -> p h e", h=H), ob[t][:, :, 0:HD],
                                          ro[p][:, t, :].unsqueeze(2).to_broadcast([P, H, HD]),
                                          ALU.mult).then_inc(s_o[p], 1)
                for p in range(2):
                    dve.wait_ge(s_pr[p], 3 * i + 1)
                    dve.wait_ge(s_xb[p], 2 * i + 1)
                    dve.tensor_tensor(x4[p][:, :, :], m1[p][:, :].rearrange("p (t d) -> p t d", t=NT),
                                      xb[p][:, :, :], ALU.add).then_inc(s_x4[p], 1)
                    dve.wait_ge(s_x4[p], i + 1)
                    stat(x4[p], p, 1)
                for p in range(2):
                    normed(x4[p], p, 1)
                for p in range(2):
                    dve.wait_ge(s_qe[p], 3 * i + 1)
                    for t in range(NT):
                        dve.scalar_tensor_tensor(o[p][:, t, :], qe[p][:, t, :], -0.01, qe[p][:, t, :],
                                                 ALU.mult, ALU.max, accum_out=qs[p][:, 0, t:t + 1]).then_inc(s_qf[p], 1)
                for p in range(2):
                    dve.wait_ge(s_kv[p], i + 1)
                    for k in range(ND):
                        dve.tensor_tensor(KV[p][:, k, 0:P].rearrange("p (h e) -> p h e", e=HD),
                                          m0[p][:, k * 256:k * 256 + P].rearrange("p (h e) -> p h e", e=HD),
                                          K.blocks[:, :, :], ALU.mult)
                        last = dve.tensor_tensor(KV[p][:, k, P:KW],
                                                 m0[p][:, k * 256 + P:k * 256 + P + 1].to_broadcast([P, P // HD]),
                                                 K.heads[:, :, 0], ALU.mult)
                    last.then_inc(s_KV[p], 2)
                for p in range(2):
                    dve.wait_ge(s_qln[p], i + 1)
                    dve.tensor_scalar(o[p][:, :, :], o[p][:, :, :], K.focus[:, :], None, ALU.mult).then_inc(s_qf[p], 1)
                    dve.wait_ge(s_qf[p], 9 * i + 3)
                    dve.tensor_reduce(qs[p][:, 1, :], o[p][:, :, :], axis=AX_X, op=ALU.max,
                                      negate=True).then_inc(s_qf[p], 1)
                for p in range(2):
                    dve.wait_ge(s_qe[p], 3 * i + 3)
                    dve.scalar_tensor_tensor(qk[p][:, :, :], qe[p][:, :, :].bitcast(I32), -16,
                                             K.rank[:, :, :].to_broadcast([P, NT, D]), ALU.bitwise_and,
                                             ALU.bitwise_or).then_inc(s_qf[p], 1)
                    dve.reciprocal(qs[p][:, 2, :], qs[p][:, 2, :]).then_inc(s_qf[p], 1)
                    dve.tensor_scalar(qs[p][:, 0, :], qs[p][:, 0, :], 1.0 / D, EPS, ALU.mult,
                                      ALU.add).then_inc(s_qf[p], 1)
                for p in range(2):
                    dve.wait_ge(s_qf[p], 9 * i + 7)
                    dve.memset(idle[p][:, :], 0.0)
                    for t in range(NT):
                        for hh in range(H):
                            dve.max(qt[p][:, t * H + hh, :], qk[p][:, t, hh * HD:(hh + 1) * HD].bitcast(F32))
                    dve.tensor_tensor(qs[p][:, 3, :], qs[p][:, 2, :], qs[p][:, 0, :], ALU.mult).then_inc(s_qf[p], 1)
                for p in range(2):
                    dve.wait_ge(s_qf[p], 9 * i + 8)
                    dve.tensor_tensor(o[p][:, :, :].rearrange("p t (h e) -> p (t h) e", h=H),
                                      qk[p][:, :, :].bitcast(F32).rearrange("p t (h e) -> p (t h) e", h=H),
                                      qt[p][:, :, SMALL - 1:SMALL].to_broadcast([P, NT * H, HD]),
                                      ALU.is_lt).then_inc(s_qf[p], 1)
                    dve.wait_ge(s_qf[p], 9 * i + 9)
                    for t in range(NT):
                        dve.scalar_tensor_tensor(qe[p][:, t, :], o[p][:, t, :], qs[p][:, 3, t:t + 1],
                                                 qe[p][:, t, :], ALU.mult, ALU.mult).then_inc(s_o[p], 1)
                for p in range(2):
                    dve.wait_ge(s_y[p], i + 1)
                    yb = [b[p][:, :].rearrange("p (k c) -> p k c", k=ND) for b in (m1, m0)]
                    for t in range(NT):
                        dve.tensor_scalar(rz[p][:, t, :, :], yb[t][:, :, P:KW], EPS, None,
                                          ALU.add).then_inc(s_z[p], 1)
                    dve.wait_ge(s_z[p], 3 * i + 2)
                    dve.reciprocal(rz[p][:, :, :, :], rz[p][:, :, :, :]).then_inc(s_z[p], 1)
                    dve.wait_ge(s_z[p], 3 * i + 3)
                    for t in range(NT):
                        dve.tensor_tensor(o[p][:, t, :].rearrange("p (k h e) -> p k h e", k=ND, e=HD),
                                          yb[t][:, :, 0:P].rearrange("p k (h e) -> p k h e", e=HD),
                                          rz[p][:, t, :, :].unsqueeze(3).to_broadcast([P, ND, P // HD, HD]),
                                          ALU.mult).then_inc(s_yn[p], 1)
                for p in range(2):
                    dve.wait_ge(s_pr[p], 3 * i + 2)
                    dve.wait_ge(s_xb[p], 2 * i + 1)
                    dve.tensor_tensor(x3[p][:, :, :], m1[p][:, :].rearrange("p (t d) -> p t d", t=NT),
                                      x4[p][:, :, :], ALU.add).then_inc(s_x5[p], 1)
                    dve.wait_ge(s_x5[p], i + 1)
                    stat(x3[p], p, 2)
                for p in range(2):
                    normed(x3[p], p, 2)
                for p in range(2):
                    dve.wait_ge(s_pr[p], 3 * i + 3)
                    dve.wait_ge(s_xb[p], 2 * i + 2)
                    dve.wait_ge(s_out[p], 16 * i)
                    dve.tensor_tensor(xo[p][:, :, :], m1[p][:, :].rearrange("p (t d) -> p t d", t=NT),
                                      xb[p][:, :, :], ALU.add).then_inc(s_x6[p], 1)

        @block.tensor
        def _(pe):
            def turn(p, bank, src):
                for k in range(ND):
                    for t in range(NT):
                        last = pe.transpose(bank[p][:, k * T + t * P:k * T + (t + 1) * P],
                                            src[p][:, t, k * P:(k + 1) * P], K.ident[:, :])
                last.then_inc(s_tr[p], 1)

            def project(bank, p, w):
                for t in range(NT):
                    for k in range(ND):
                        last = pe.matmul(bank[p][:, t * D:(t + 1) * D], xT[p][:, k, t * P:(t + 1) * P],
                                         w[:, k, :], start=k == 0, stop=k == ND - 1)
                return last

            def heads(bank, p, w, c):
                for gg in range(2):
                    for k in range(ND):
                        last = pe.matmul(bank[p][:, gg * T:(gg + 1) * T],
                                         w[:, k, (2 * c + gg) * P:(2 * c + gg + 1) * P], xT[p][:, k, :],
                                         start=k == 0, stop=k == ND - 1)
                return last

            with pe.Fori(0, PAIRS) as i:
                for p in range(2):
                    pe.wait_ge(s_cx[p], 16 * i + 16)
                    pe.wait_ge(s_x6[p], i)
                    for k in range(ND):
                        last = pe.transpose(m1[p][:, k * V:(k + 1) * V], cx[p][:, k * P:(k + 1) * P],
                                            K.ident[0:V, 0:V])
                    last.then_inc(s_ctr[p], 1)
                for p in range(2):
                    pe.wait_ge(s_cT[p], i + 1)
                    for k in range(ND):
                        last = pe.matmul(m1[p][0:V, :], cT[p][:, k, :], K.Xkv[:, k, :], start=k == 0,
                                         stop=k == ND - 1)
                    last.then_inc(s_ckv[p], 1)
                for p in range(2):
                    pe.wait_ge(s_hq[p], i + 1)
                    for t in range(NT):
                        for j in range(NI):
                            last = pe.matmul(m0[p][:, t * D:(t + 1) * D], hq[p][:, j, t * P:(t + 1) * P],
                                             K.wd[:, j, :], start=j == 0, stop=j == NI - 1)
                    last.then_inc(s_dn[p], 1)
                for p in range(2):
                    pe.wait_ge(s_xn[p], 6 * i + 2)
                    pe.wait_ge(s_kvc[p], i + 1)
                    turn(p, m1, xn)
                for p in range(2):
                    pe.wait_ge(s_xT[p], TURNS * i + 1)
                    project(m0, p, K.Wv).then_inc(s_vp[p], 1)
                    heads(m1, p, K.Wq, 0).then_inc(s_qp[p], 1)
                for p in range(2):
                    pe.wait_ge(s_vs[p], i + 1)
                    heads(m0, p, K.Wq, 1).then_inc(s_qp[p], 1)
                    pe.wait_ge(s_q[p], 4 * i + 2)
                    heads(m1, p, K.Wk, 0).then_inc(s_kp[p], 1)
                    pe.wait_ge(s_q[p], 4 * i + 4)
                    heads(m0, p, K.Wk, 1).then_inc(s_kp[p], 1)
                for p in range(2):
                    pe.wait_ge(s_k[p], 4 * i + 4)
                    for u in range(STEPS):
                        n = p * STEPS + u
                        gg, r = u // 2, u % 2
                        if n < 2:
                            pe.wait_ge(s_ex[r], STEPS * i)
                        else:
                            pe.wait_ge(s_mx[r], STEPS * i + n // 2)
                        for t in range(NT):
                            for a in range(2):
                                j = 2 * r + a
                                rr = slice(32 * j, 32 * j + 32)
                                last = pe.matmul(S[r][:, a * 512 + t * T:a * 512 + (t + 1) * T],
                                                 QT[p][rr, gg, t * P:(t + 1) * P], KT[p][rr, gg, :],
                                                 start=True, stop=True)
                        last.then_inc(s_s1[r], 1)
                for p in range(2):
                    for r in range(2):
                        pe.wait_ge(s_mx[r], STEPS * i + 4 * p + 4)
                    for c in range(2):
                        for gg in (2 * c, 2 * c + 1):
                            for t in range(NT):
                                at = (gg % 2) * T + t * P
                                last = pe.transpose((m0, m1)[c][p][:, at:at + P],
                                                    mx[p][:, t, 4 * gg:4 * gg + 4, :].rearrange("p h r -> p (h r)"),
                                                    K.ident[:, :])
                        last.then_inc(s_mt[p], 1)

                def weigh(n):
                    p, u = n // STEPS, n % STEPS
                    gg, r = u // 2, u % 2
                    pe.wait_ge(s_ex[r], STEPS * i + n // 2 + 1)
                    for a in range(2):
                        j = 2 * r + a
                        for t in range(NT):
                            last = pe.matmul((m0, m1)[gg // 2][p][32 * j:32 * j + 32, (gg % 2) * T:(gg % 2 + 1) * T],
                                             vs[p][:, t, 4 * gg + j, :], E[n % NE][:, a, t, :],
                                             start=t == 0, stop=t == NT - 1, skip_group_check=True)
                    last.then_inc(s_av[n % NE], 1)
                    if u == STEPS - 1:
                        pe.wait_ge(s_av[n % NE], 4 * i + n // NE + 1)
                        pe.nop().then_inc(s_ao[p], 1)

                for n in range(2 * STEPS + 1):
                    if n < 2 * STEPS:
                        p, u = n // STEPS, n % STEPS
                        gg, r = u // 2, u % 2
                        if u == 0:
                            pe.wait_ge(s_qm[p], 2 * i + 2)
                        if n < 2:
                            pe.wait_ge(s_mx[r], STEPS * i + STEPS)
                        else:
                            pe.wait_ge(s_ex[r], STEPS * i + n // 2)
                        for t in range(NT):
                            for a in range(2):
                                j = 2 * r + a
                                rr = slice(32 * j, 32 * j + 32)
                                last = pe.matmul(S[r][:, a * 512 + t * T:a * 512 + (t + 1) * T],
                                                 KT[p][rr, gg, t * P:(t + 1) * P], QT[p][rr, gg, :],
                                                 start=True, stop=True)
                        last.then_inc(s_s2[r], 1)
                    if n >= 1:
                        weigh(n - 1)
                for p in range(2):
                    pe.wait_ge(s_oT[p], 2 * i + 2)
                    for t in range(NT):
                        for gg in range(4):
                            last = pe.transpose((m0, m1)[t][p][:, gg * P:(gg + 1) * P],
                                                oT[p][:, gg, t * P:(t + 1) * P], K.ident[:, :])
                    last.then_inc(s_ob[p], 1)
                for p in range(2):
                    pe.wait_ge(s_o[p], 4 * i + 2)
                    turn(p, m0, o)
                for p in range(2):
                    pe.wait_ge(s_xT[p], TURNS * i + 2)
                    project(m1, p, K.Wp).then_inc(s_pr[p], 1)
                for p in range(2):
                    pe.wait_ge(s_xn[p], 6 * i + 4)
                    turn(p, m0, xn)
                for p in range(2):
                    pe.wait_ge(s_xT[p], TURNS * i + 3)
                    project(m1, p, K.Xq).then_inc(s_xq[p], 1)
                    pe.wait_ge(s_KV[p], 5 * i + 3)
                    for k in range(ND):
                        pe.matmul(m0[p][:, k * 256:k * 256 + P], ke[p][:, 0, k * P:(k + 1) * P],
                                  kvc[p][:, D + k * P:D + (k + 1) * P], start=True, stop=True)
                        last = pe.matmul(m0[p][:, k * 256 + P:k * 256 + P + 1], ke[p][:, 0, k * P:(k + 1) * P],
                                         K.one77[0:V, :], start=True, stop=True)
                    last.then_inc(s_kv[p], 1)
                for p in range(2):
                    pe.wait_ge(s_o[p], 4 * i + 4)
                    pe.wait_ge(s_KV[p], 5 * i + 5)
                    turn(p, m0, qe)
                for p in range(2):
                    pe.wait_ge(s_xT[p], TURNS * i + 4)
                    for t in range(NT):
                        for k in range(ND):
                            last = pe.matmul((m1, m0)[t][p][:, k * 256:k * 256 + KW],
                                             xT[p][:, k, t * P:(t + 1) * P], KV[p][:, k, :], start=True, stop=True)
                    last.then_inc(s_y[p], 1)
                for p in range(2):
                    pe.wait_ge(s_yn[p], 2 * i + 2)
                    turn(p, m0, o)
                for p in range(2):
                    pe.wait_ge(s_xT[p], TURNS * i + 5)
                    project(m1, p, K.Xp).then_inc(s_pr[p], 1)
                for p in range(2):
                    pe.wait_ge(s_xn[p], 6 * i + 6)
                    turn(p, m0, xn)
                for p in range(2):
                    pe.wait_ge(s_xT[p], TURNS * i + 6)
                    project(m1, p, K.M).then_inc(s_pr[p], 1)


def clear_semaphores(nc, numbers):
    with nc.Block() as block:
        @block.gpsimd
        def _(pool):
            pool.sem_clear(numbers)


class Kept:
    pass


def build(nc, A, out):
    x2 = nc.dram_tensor("x2_scratch", (B, T, D), F32, kind="Internal").ap()
    xn3 = nc.dram_tensor("xn3_scratch", (B, T, D), F32, kind="Internal").ap()
    hs = nc.dram_tensor("h_scratch", (B, P, NI * T), F32, kind="Internal").ap()
    numbers = range(min(nc.free_semaphores), max(nc.free_semaphores) + 1)
    with ExitStack() as ctx:
        def sb(name, shape, dt=F32):
            return ctx.enter_context(nc.sbuf_tensor("k_" + name, shape, dt))

        K = Kept()
        K.ident = sb("ident", [P, P])
        K.peak = sb("peak", [P, 1])
        K.hpeak = sb("hpeak", [P, 1])
        K.Wq = sb("Wq", [P, ND, 4 * P])
        K.Wk = sb("Wk", [P, ND, 4 * P])
        K.Wv = sb("Wv", [P, ND, D])
        K.Wp = sb("Wp", [P, ND, D])
        K.bq = sb("bq", [P, 4])
        K.bk = sb("bk", [P, 4])
        K.bv = sb("bv", [P, 1, D])
        K.bp = sb("bp", [P, 1, D])
        K.bf = sb("bf", [P, 1, D])
        K.Xq = sb("Xq", [P, ND, D])
        K.Xkv = sb("Xkv", [P, ND, 2 * D])
        K.Xp = sb("Xp", [P, ND, D])
        K.M = sb("M", [P, ND, D])
        K.wg = sb("wg", [P, ND, I], BF16)
        K.wu = sb("wu", [P, ND, I], BF16)
        K.wd = sb("wd", [P, NI, D], BF16)
        K.sgate = sb("sgate", [P, NI])
        K.sup = sb("sup", [P, NI])
        K.sdown = sb("sdown", [P, ND])
        K.srep = sb("srep", [P, ND, P])
        K.srow = sb("srow", [P, 1, D])
        K.clip = sb("clip", [P, 2])
        K.cexp = sb("cexp", [P, 2])
        K.csig = sb("csig", [P, 2])
        K.focus = sb("focus", [P, 1])
        K.rank = sb("rank", [P, 1, D], I32)
        K.magic = sb("magic", [P, 1])
        K.eps = sb("eps", [P, 1])
        K.one77 = sb("one77", [P, 1])
        K.heads = sb("heads", [P, P // HD, 1])
        K.blocks = sb("blocks", [P, P // HD, HD])
        with nc.semaphore("ident_made") as s_id, nc.Block() as block:
            @block.gpsimd
            def _(pool):
                pool.memset(K.ident[:, :], 0.0).then_inc(s_id, 1)
                pool.wait_ge(s_id, 1)
                pool.affine_select(out=K.ident[:, :], in_=K.ident[:, :], compare_op=ALU.not_equal, fill=1.0,
                                   base=0, pattern=[[-1, P]], channel_multiplier=1).then_inc(s_id, 1)
                pool.wait_ge(s_id, 2)
        clear_semaphores(nc, numbers)
        phase_weights(nc, A, K)
        clear_semaphores(nc, numbers)
        phase_attention(nc, A, x2, xn3, K.ident, K.peak)
        clear_semaphores(nc, numbers)
        phase_gate_up(nc, K, xn3, hs)
        clear_semaphores(nc, numbers)
        phase_tail(nc, A, K, x2, hs, out)


def kernel(**inputs):
    import numpy as np
    import concourse.bacc as bacc
    from concourse.bass_utils import run_bass_kernel_spmd

    nc = bacc.Bacc("TRN2", target_bir_lowering=False, num_devices=1)
    arrays, A = {}, {}
    for name, a in inputs.items():
        a = np.ascontiguousarray(a)
        if a.ndim == 0:
            a = a.reshape(1)
        arrays["in_" + name] = a
        A[name] = nc.dram_tensor("in_" + name, a.shape, mybir.dt.from_np(a.dtype), kind="ExternalInput").ap()
    turns = np.outer(np.arange(D), np.arange(D)) % D * (2 * np.pi / D)
    arrays["in_dft"] = np.stack([np.cos(turns), np.sin(turns), -np.sin(turns)]).astype(np.float32)
    A["dft"] = nc.dram_tensor("in_dft", (3, D, D), F32, kind="ExternalInput").ap()
    rank = (HD - 1 - np.arange(D) % HD).astype(np.int64) - 2 ** 31
    arrays["in_rank"] = rank.astype(np.int32)
    A["rank"] = nc.dram_tensor("in_rank", (D,), I32, kind="ExternalInput").ap()
    out = nc.dram_tensor("out_0", (B, T, D), F32, kind="ExternalOutput").ap()
    build(nc, A, out)
    r = run_bass_kernel_spmd(nc, [arrays], core_ids=[0])
    return r.results[0]["out_0"]
```

```python
from contextlib import ExitStack

import concourse.bass as bass
from concourse import mybir

F32 = mybir.dt.float32
BF16 = mybir.dt.bfloat16
I32 = mybir.dt.int32
ALU = mybir.AluOpType
ACT = mybir.ActivationFunctionType
AX_X = mybir.AxisListType.X
RMAX = bass.bass_isa.ReduceOp.max

B = 64
T = 256
D = 256
C = 128
V = 77
I = 704
H = 16
HD = D // H
P = 128
NT = T // P
ND = D // P
NI = -(-I // P)
LASTI = I - (NI - 1) * P
PAIRS = B // 2
LEVELS = 6
KEEP = max(int(0.7 * HD), 1)
QMAX = 127.0
LN_EPS = 1e-5
EPS = 1e-6
MAGIC = 12582912.0


def rows(dram, b):
    return dram[bass.ds(b, 1), :, :].rearrange("o (t p) d -> p (o t) d", p=P)


def phase_attention(nc, A, x2, xn3, ident, peak):
    CHAINS = 4
    ROUNDS = 2 * PAIRS // CHAINS
    with ExitStack() as ctx:
        def sb(name, shape, dt=F32):
            return ctx.enter_context(nc.sbuf_tensor("a_" + name, shape, dt))

        def each(name, shape, dt=F32):
            return [sb(f"{name}{p}", shape, dt) for p in range(CHAINS)]

        def sem(name):
            return ctx.enter_context(nc.semaphore("a_" + name))

        def count(i, p, k=1, stage=0, stages=1):
            return k * CHAINS * stages * i + k * (CHAINS * stage + p + 1)

        Wkv = sb("Wkv", [P, ND, 2 * C])
        Wab = sb("Wab", [P, ND, 2])
        Wqg = sb("Wqg", [P, ND, 2 * C])
        Wo = sb("Wo", [C, D])
        bkv = sb("bkv", [P, 1, 2 * C])
        bab = sb("bab", [P, 1, 2])
        bq = sb("bq", [P, 1])
        bg = sb("bg", [P, 1])
        nbg = sb("nbg", [P, 1])
        bo = sb("bo", [P, 1, D])
        ones = sb("ones", [P, 3 * P])
        later = sb("later", [P, P])
        upto = sb("upto", [P, 3 * P])
        before = sb("before", [P, 3 * P])
        lmask = sb("lmask", [P, LEVELS, P])
        nmask = sb("nmask", [P, 2, P])
        half = sb("half", [P, NT])
        lneps = sb("lneps", [P, NT])
        x = each("x", [P, NT, D])
        cx = each("cx", [V, D])
        xbo = each("xbo", [P, NT, D])
        xn = each("xn", [P, NT, D])
        xT = each("xT", [P, ND, T])
        cT = each("cT", [P, ND, V])
        stats = each("stats", [P, NT, 6])
        mv = each("mv", [P, NT, 2])
        rstd = each("rstd", [P, NT])
        kv = each("kv", [P, NT, 2 * C])
        zab = each("zab", [P, NT, 2])
        tab = each("tab", [P, NT, 2])
        eab = each("eab", [P, NT, 2])
        lna = each("lna", [P, NT])
        la = each("la", [P, NT])
        beta = each("beta", [P, NT])
        sq = each("sq", [P, C])
        ss = each("ss", [P, NT])
        rk = each("rk", [P, NT])
        kn = each("kn", [P, NT, C])
        kT = each("kT", [C, T])
        qT = each("qT", [C, T])
        ge = each("ge", [C, T])
        gT = each("gT", [C, T])
        R = each("R", [P, 3 * P])
        Dx = each("Dx", [P, 3 * P])
        Di = each("Di", [P, 3 * P])
        Ds = each("Ds", [P, 3 * P])
        U = each("U", [P, 3 * P])
        L = each("L", [P, 2, P])
        Lm = each("Lm", [P, LEVELS, 2, P])
        N = each("N", [P, 4, P])
        Y = each("Y", [P, 2, P])
        W0 = each("W0", [P, P])
        WT = each("WT", [C, T])
        v1 = each("v1", [P, C])
        Pm = each("Pm", [P, 3 * P])
        oT = each("oT", [C, T])
        x1 = each("x1", [P, NT, D])
        nmx = each("nmx", [P, NT])
        es = each("es", [P, NT, V])
        sm = each("sm", [P, NT])
        rs = each("rs", [P, NT])
        eT = each("eT", [V, T])
        xo = each("xo", [P, NT, D])
        xno = each("xno", [P, NT, D])
        pk = each("pk", [P, 1])
        idle = each("idle", [P, 1])
        bank = [[ctx.enter_context(nc.psum_tensor(f"a_b{p}{k}", [P, 512], F32)) for k in range(2)]
                for p in range(CHAINS)]

        s_w = sem("weights")
        s_bg = sem("neg_gate_bias")
        s_c = sem("constants")
        s_x = [sem(f"x_in{p}") for p in range(CHAINS)]
        s_cx = [sem(f"ctx_in{p}") for p in range(CHAINS)]
        s_st = sem("stats")
        s_mv = sem("meanvar")
        s_ve = sem("vareps")
        s_rs = sem("rstd")
        s_xn = sem("xn")
        s_xbo = sem("xbo")
        s_tr = sem("xn_transposed")
        s_xT = sem("xT")
        s_cT = sem("cT")
        s_ctr = sem("ctx_transposed")
        s_pr = sem("projected")
        s_ab = sem("ab_product")
        s_kvp = sem("kv_product")
        s_kv = sem("kv")
        s_zab = sem("zab")
        s_tab = sem("tab")
        s_eab = sem("eab")
        s_e1 = sem("eab1")
        s_lna = sem("lna")
        s_la = sem("la")
        s_be = sem("beta")
        s_ss = sem("ksq")
        s_sg = sem("ksq_guarded")
        s_rk = sem("rk")
        s_kn = sem("kn")
        s_ktr = sem("k_transposed")
        s_kT = sem("kT")
        s_qT = sem("qT")
        s_ge = sem("gate_exp")
        s_gT = sem("gate")
        s_R = sem("R")
        s_G = sem("gram")
        s_lD = sem("logdecay")
        s_Dx = sem("decay")
        s_Dm = sem("decay_masked")
        s_U = sem("U")
        s_utr = sem("U_transposed")
        s_L = sem("L")
        s_Lm = sem("Lm")
        s_n0 = sem("inverse_start")
        s_Yp = sem("Yp")
        s_Y = sem("Y")
        s_dN = sem("dN")
        s_N = sem("N")
        s_w0p = sem("w0p")
        s_w0 = sem("w0")
        s_v1p = sem("v1p")
        s_v1 = sem("v1")
        s_w1p = sem("w1p")
        s_w1 = sem("w1")
        s_Ap = sem("Ap")
        s_P = sem("P")
        s_op = sem("op")
        s_og = sem("og")
        s_wop = sem("wop")
        s_x1 = sem("x1")
        s_sc = sem("scores")
        s_mx = sem("rowmax")
        s_es = sem("expscores")
        s_etr = sem("es_transposed")
        s_eT = sem("eT")
        s_co = sem("ctx_out")
        s_rr = sem("rsum")
        s_x2 = sem("x2")
        s_pk = sem("peak_part")
        s_pkm = sem("peak")
        s_out = [sem(f"stored{p}") for p in range(CHAINS)]
        WEIGHTS = 6 * ND + 8
        CONSTS = 10 + CHAINS + 4 * (LEVELS + 2) + 1
        block = ctx.enter_context(nc.Block())

        @block.sync
        def _(sp):
            for k in range(ND):
                r = slice(k * P, (k + 1) * P)
                sp.dma_start(Wkv[:, k, 0:C], A["L0_attn_Wk"][r, :]).then_inc(s_w, 16)
                sp.dma_start(Wkv[:, k, C:2 * C], A["L0_attn_Wv"][r, :]).then_inc(s_w, 16)
                sp.dma_start(Wab[:, k, 0:1], A["L0_attn_Wa"][r, :]).then_inc(s_w, 16)
                sp.dma_start(Wab[:, k, 1:2], A["L0_attn_Wb"][r, :]).then_inc(s_w, 16)
                sp.dma_start(Wqg[:, k, 0:C], A["L0_attn_Wq"][r, :]).then_inc(s_w, 16)
                sp.dma_start(Wqg[:, k, C:2 * C], A["L0_attn_Wg"][r, :]).then_inc(s_w, 16)
            sp.dma_start(Wo[:, :], A["L0_attn_Wo"][:, :]).then_inc(s_w, 16)
            sp.dma_start(bkv[:, 0, 0:C], A["L0_attn_bk"].partition_broadcast(P)).then_inc(s_w, 16)
            sp.dma_start(bkv[:, 0, C:2 * C], A["L0_attn_bv"].partition_broadcast(P)).then_inc(s_w, 16)
            sp.dma_start(bab[:, 0, 0:1], A["L0_attn_ba"].partition_broadcast(P)).then_inc(s_w, 16)
            sp.dma_start(bab[:, 0, 1:2], A["L0_attn_bb"].partition_broadcast(P)).then_inc(s_w, 16)
            sp.dma_start(bo[:, 0, :], A["L0_attn_bo"].partition_broadcast(P)).then_inc(s_w, 16)
            sp.dma_start(bq[:, :], A["L0_attn_bq"].unsqueeze(1)).then_inc(s_w, 16)
            sp.dma_start(bg[:, :], A["L0_attn_bg"].unsqueeze(1)).then_inc(s_w, 16)

            def load_x(p, b):
                sp.dma_start(x[p][:, :, :], rows(A["x"], b)).then_inc(s_x[p], 16)

            def load_ctx(p, b):
                sp.dma_start(cx[p][:, :], A["ctx_1024"][bass.ds(b, 1), :, :]
                             .rearrange("o v d -> v (o d)")).then_inc(s_cx[p], 16)

            def store(p, b):
                sp.dma_start(rows(x2, b), xo[p][:, :, :]).then_inc(s_out[p], 16)
                sp.dma_start(rows(xn3, b), xno[p][:, :, :]).then_inc(s_out[p], 16)

            for p in range(CHAINS):
                load_x(p, p)
                load_ctx(p, p)
            with sp.Fori(0, ROUNDS - 1) as i:
                for p in range(CHAINS):
                    sp.wait_ge(s_x1, count(i, p))
                    load_x(p, CHAINS * (i + 1) + p)
                for p in range(CHAINS):
                    sp.wait_ge(s_co, count(i, p))
                    load_ctx(p, CHAINS * (i + 1) + p)
                for p in range(CHAINS):
                    sp.wait_ge(s_xn, count(i, p, 2, 2, 3))
                    store(p, CHAINS * i + p)
            for p in range(CHAINS):
                sp.wait_ge(s_xn, count(ROUNDS - 1, p, 2, 2, 3))
                store(p, CHAINS * (ROUNDS - 1) + p)
            for p in range(CHAINS):
                sp.wait_ge(s_out[p], 32 * (ROUNDS + 1))

        @block.gpsimd
        def _(pool):
            pool.memset(ones[:, :], 1.0).then_inc(s_c, 1)
            pool.memset(half[:, :], -0.5).then_inc(s_c, 1)
            pool.memset(lneps[:, :], LN_EPS).then_inc(s_c, 1)
            for p in range(CHAINS):
                pool.memset(pk[p][:, :], 0.0).then_inc(s_c, 1)
                pool.sem_inc(s_out[p], 32)
            pool.wait_ge(s_c, 3 + CHAINS)
            pool.affine_select(out=later[:, :], in_=ones[:, 0:P], compare_op=ALU.is_gt, fill=0.0, base=0,
                               pattern=[[-1, P]], channel_multiplier=1).then_inc(s_c, 1)
            for dst, op in ((upto, ALU.is_ge), (before, ALU.is_gt)):
                for c in (0, 2):
                    pool.affine_select(out=dst[:, c * P:(c + 1) * P], in_=ones[:, 0:P], compare_op=op,
                                       fill=0.0, base=0, pattern=[[1, P]],
                                       channel_multiplier=-1).then_inc(s_c, 1)
                pool.tensor_copy(dst[:, P:2 * P], ones[:, 0:P]).then_inc(s_c, 1)
            done = 3 + CHAINS + 1 + 6

            def half_blocks(out, h, flip):
                nonlocal done
                blocks = P // (2 * h)
                part = out.rearrange("p (b a c) -> p b a c", b=blocks, a=2)
                pool.memset(part[:, :, 0, :], 0.0 if flip else 1.0).then_inc(s_c, 1)
                pool.memset(part[:, :, 1, :], 1.0 if flip else 0.0).then_inc(s_c, 1)
                done += 2
                lo, hi = (0, h) if flip else (h, 2 * h)
                pool.wait_ge(s_c, done)
                pool.affine_select(out=part, in_=part, compare_op=ALU.is_ge, fill=0.0, base=-lo,
                                   pattern=[[-2 * h, blocks], [0, 2], [0, h]],
                                   channel_multiplier=1).then_inc(s_c, 1)
                done += 1
                pool.wait_ge(s_c, done)
                pool.affine_select(out=part, in_=part, compare_op=ALU.is_gt, fill=0.0, base=hi,
                                   pattern=[[2 * h, blocks], [0, 2], [0, h]],
                                   channel_multiplier=-1).then_inc(s_c, 1)
                done += 1

            for lv in range(LEVELS):
                half_blocks(lmask[:, lv, :], 2 << lv, False)
            half_blocks(nmask[:, 0, :], 1, True)
            half_blocks(nmask[:, 1, :], 1, False)
            pool.wait_ge(s_c, done)
            pool.tensor_scalar(nmask[:, :, :], nmask[:, :, :], -1.0, None, ALU.mult).then_inc(s_c, 1)
            done += 1
            assert done == CONSTS
            pool.wait_ge(s_w, 16 * WEIGHTS)
            pool.tensor_scalar(nbg[:, :], bg[:, :], -1.0, None, ALU.mult).then_inc(s_bg, 1)

            def rsqrt(p, n):
                pool.wait_ge(s_mv, count(i, p, 2, n, 3))
                if n:
                    pool.wait_ge(s_xn, count(i, p, 2, n - 1, 3))
                pool.tensor_tensor(rstd[p][:, :], mv[p][:, :, 1], lneps[:, :], ALU.add).then_inc(s_ve, 1)
                pool.wait_ge(s_ve, count(i, p, 1, n, 3))
                pool.tensor_tensor(rstd[p][:, :], rstd[p][:, :], half[:, :], ALU.pow).then_inc(s_rs, 1)

            with pool.Fori(0, ROUNDS) as i:
                for p in range(CHAINS):
                    rsqrt(p, 0)
                for p in range(CHAINS):
                    pool.wait_ge(s_x[p], 16 * i + 16)
                    pool.tensor_tensor(xbo[p][:, :, :], x[p][:, :, :], bo[:, :, :].to_broadcast([P, NT, D]),
                                       ALU.add).then_inc(s_xbo, 1)
                for p in range(CHAINS):
                    pool.wait_ge(s_sg, count(i, p))
                    pool.tensor_tensor(rk[p][:, :], ss[p][:, :], half[:, :], ALU.pow).then_inc(s_rk, 1)
                for p in range(CHAINS):
                    pool.wait_ge(s_la, count(i, p))
                    pool.tensor_tensor(R[p][:, 0:T], upto[:, 0:T], la[p][:, 0:1].to_broadcast([P, T]),
                                       ALU.mult).then_inc(s_R, 1)
                    pool.tensor_tensor(R[p][:, T:T + P], upto[:, 0:P], la[p][:, 1:2].to_broadcast([P, P]),
                                       ALU.mult).then_inc(s_R, 1)
                for p in range(CHAINS):
                    pool.wait_ge(s_Dx, count(i, p))
                    pool.tensor_tensor(Ds[p][:, :], Dx[p][:, :], before[:, :], ALU.mult).then_inc(s_Dm, 1)
                    pool.tensor_tensor(Di[p][:, :], Dx[p][:, :], upto[:, :], ALU.mult).then_inc(s_Dm, 1)
                for p in range(CHAINS):
                    ud = U[p][:, :].rearrange("p (a c) -> p a c", a=3)[:, 0:3:2, :]
                    pool.wait_ge(s_U, count(i, p, 2))
                    pool.tensor_tensor(N[p][:, 0:2, :], ud, nmask[:, 0:1, :].to_broadcast([P, 2, P]),
                                       ALU.mult).then_inc(s_n0, 1)
                    pool.wait_ge(s_L, count(i, p))
                    pool.tensor_tensor(N[p][:, 2:4, :], L[p][:, :, :], nmask[:, 1:2, :].to_broadcast([P, 2, P]),
                                       ALU.mult).then_inc(s_n0, 1)
                    pool.wait_ge(s_n0, count(i, p, 3) - 1)
                    pool.tensor_tensor(N[p][:, :, :], N[p][:, :, :],
                                       ident[:, :].unsqueeze(1).to_broadcast([P, 4, P]),
                                       ALU.add).then_inc(s_n0, 1)
                    for lv in range(LEVELS):
                        pool.tensor_tensor(Lm[p][:, lv, :, :], L[p][:, :, :],
                                           lmask[:, lv:lv + 1, :].to_broadcast([P, 2, P]),
                                           ALU.mult).then_inc(s_Lm, 1)
                for n in (1, 2):
                    for p in range(CHAINS):
                        rsqrt(p, n)

        @block.scalar
        def _(act):
            act.wait_ge(s_w, 16 * WEIGHTS)
            act.wait_ge(s_bg, 1)
            act.preload_act_table_set("natural_log_exp_and_others")
            with act.Fori(0, ROUNDS) as i:
                for p in range(CHAINS):
                    act.wait_ge(s_ctr, count(i, p))
                    act.copy(cT[p][:, :, :], bank[p][1][:, 0:ND * V]).then_inc(s_cT, 1)
                    act.wait_ge(s_tr, count(i, p, 1, 0, 2))
                    act.copy(xT[p][:, :, :], bank[p][0][:, :]).then_inc(s_xT, 1)
                for p in range(CHAINS):
                    act.wait_ge(s_pr, count(i, p))
                    act.activation(qT[p][:, :], bank[p][0][:, 0:T], ACT.Identity, bias=bq[:, :]).then_inc(s_qT, 1)
                    act.activation(ge[p][:, :], bank[p][0][:, T:2 * T], ACT.Exp, bias=nbg[:, :],
                                   scale=-1.0).then_inc(s_ge, 1)
                    act.wait_ge(s_kv, count(i, p))
                    for t in range(NT):
                        act.activation(sq[p][:, :], kv[p][:, t, 0:C], ACT.Square,
                                       accum_out=ss[p][:, t:t + 1]).then_inc(s_ss, 1)
                        act.wait_ge(s_ss, count(i, p, 2) - 1 + t)
                    act.wait_ge(s_tab, count(i, p, 2))
                    act.activation(eab[p][:, :, :], tab[p][:, :, :], ACT.Exp, scale=-1.0).then_inc(s_eab, 1)
                    act.wait_ge(s_e1, count(i, p))
                    act.activation(lna[p][:, :], eab[p][:, :, 0], ACT.Ln).then_inc(s_lna, 1)
                for p in range(CHAINS):
                    act.wait_ge(s_lD, count(i, p))
                    act.activation(Dx[p][:, :], bank[p][0][:, 0:3 * P], ACT.Exp).then_inc(s_Dx, 1)
                for p in range(CHAINS):
                    act.wait_ge(s_ktr, count(i, p))
                    act.copy(kT[p][:, :], bank[p][1][:, 0:T]).then_inc(s_kT, 1)
                for p in range(CHAINS):
                    act.wait_ge(s_utr, count(i, p))
                    act.copy(L[p][:, :, :], bank[p][0][:, 0:2 * P]).then_inc(s_L, 1)
                for lv in range(LEVELS):
                    for p in range(CHAINS):
                        act.wait_ge(s_Yp, count(i, p, 1, lv, LEVELS))
                        act.copy(Y[p][:, :, :], bank[p][0][:, 0:2 * P]).then_inc(s_Y, 1)
                for p in range(CHAINS):
                    act.wait_ge(s_w0p, count(i, p))
                    act.copy(W0[p][:, :], bank[p][0][:, 0:P]).then_inc(s_w0, 1)
                    act.copy(WT[p][:, 0:P], bank[p][0][:, P:2 * P]).then_inc(s_w0, 1)
                for p in range(CHAINS):
                    act.wait_ge(s_w1p, count(i, p))
                    act.copy(WT[p][:, P:2 * P], bank[p][1][:, 0:P]).then_inc(s_w1, 1)
                for p in range(CHAINS):
                    act.wait_ge(s_tr, count(i, p, 1, 1, 2))
                    act.copy(xT[p][:, :, :], bank[p][1][:, :]).then_inc(s_xT, 1)
                for p in range(CHAINS):
                    act.wait_ge(s_mx, count(i, p))
                    for t in range(NT):
                        act.activation(es[p][:, t, :], bank[p][0][:, t * P:t * P + V], ACT.Exp,
                                       bias=nmx[p][:, t:t + 1], accum_out=sm[p][:, t:t + 1]).then_inc(s_es, 1)
                for p in range(CHAINS):
                    act.wait_ge(s_etr, count(i, p))
                    act.copy(eT[p][:, :], bank[p][1][0:V, 0:T]).then_inc(s_eT, 1)

        @block.vector
        def _(dve):
            def normed(dst, src, p, n):
                for t in range(NT):
                    dve.wait_ge(s_rs, count(i, p, 1, n, 3))
                    dve.tensor_scalar(dst[:, t, :], src[:, t, :], mv[p][:, t, 0:1], rstd[p][:, t:t + 1],
                                      ALU.subtract, ALU.mult).then_inc(s_xn, 1)

            def stat(src, p, n):
                for t in range(NT):
                    dve.bn_stats(stats[p][:, t, :], src[:, t, :]).then_inc(s_st, 1)
                dve.wait_ge(s_st, count(i, p, 2, n, 3))
                dve.memset(idle[p][:, :], 0.0)
                for t in range(NT):
                    dve.bn_aggr(mv[p][:, t, :], stats[p][:, t, :]).then_inc(s_mv, 1)

            dve.wait_ge(s_w, 16 * WEIGHTS)
            dve.wait_ge(s_c, CONSTS)
            with dve.Fori(0, ROUNDS) as i:
                for p in range(CHAINS):
                    dve.wait_ge(s_x[p], 16 * i + 16)
                    stat(x[p], p, 0)
                for p in range(CHAINS):
                    normed(xn[p], x[p], p, 0)
                for p in range(CHAINS):
                    dve.wait_ge(s_ab, count(i, p))
                    dve.tensor_tensor(zab[p][:, :, :], bank[p][1][:, 256:260].rearrange("p (t c) -> p t c", t=NT),
                                      bab[:, :, :].to_broadcast([P, NT, 2]), ALU.add).then_inc(s_zab, 1)
                    dve.wait_ge(s_zab, count(i, p))
                    dve.scalar_tensor_tensor(tab[p][:, :, 0], zab[p][:, :, 0], -1.0, zab[p][:, :, 0],
                                             ALU.mult, ALU.max).then_inc(s_tab, 1)
                    dve.tensor_copy(tab[p][:, :, 1], zab[p][:, :, 1]).then_inc(s_tab, 1)
                for p in range(CHAINS):
                    dve.wait_ge(s_kvp, count(i, p))
                    dve.tensor_tensor(kv[p][:, :, :], bank[p][1][:, :].rearrange("p (t c) -> p t c", t=NT),
                                      bkv[:, :, :].to_broadcast([P, NT, 2 * C]), ALU.add).then_inc(s_kv, 1)
                for p in range(CHAINS):
                    dve.wait_ge(s_eab, count(i, p))
                    dve.tensor_scalar(eab[p][:, :, :], eab[p][:, :, :], 1.0, None, ALU.add).then_inc(s_e1, 1)
                    dve.wait_ge(s_e1, count(i, p))
                    dve.reciprocal(beta[p][:, :], eab[p][:, :, 1]).then_inc(s_be, 1)
                    dve.wait_ge(s_lna, count(i, p))
                    dve.scalar_tensor_tensor(la[p][:, :], zab[p][:, :, 0], 0.0, lna[p][:, :],
                                             ALU.min, ALU.subtract).then_inc(s_la, 1)
                    dve.wait_ge(s_ss, count(i, p, 2))
                    dve.tensor_scalar(ss[p][:, :], ss[p][:, :], 1e-24, None, ALU.max).then_inc(s_sg, 1)
                for p in range(CHAINS):
                    dve.wait_ge(s_rk, count(i, p))
                    for t in range(NT):
                        dve.tensor_scalar(kn[p][:, t, :], kv[p][:, t, 0:C], rk[p][:, t:t + 1], None,
                                          ALU.mult).then_inc(s_kn, 1)
                for p in range(CHAINS):
                    dve.wait_ge(s_ge, count(i, p))
                    dve.tensor_scalar(ge[p][:, :], ge[p][:, :], 1.0, None, ALU.add).then_inc(s_gT, 1)
                    dve.wait_ge(s_gT, count(i, p, 2) - 1)
                    dve.reciprocal(gT[p][:, :], ge[p][:, :]).then_inc(s_gT, 1)
                for p in range(CHAINS):
                    dve.wait_ge(s_G, count(i, p))
                    dve.wait_ge(s_Dm, count(i, p, 2))
                    dve.wait_ge(s_be, count(i, p))
                    for t, c in ((0, slice(0, T)), (1, slice(T, T + P))):
                        dve.scalar_tensor_tensor(U[p][:, c], bank[p][1][:, c], beta[p][:, t:t + 1], Ds[p][:, c],
                                                 ALU.mult, ALU.mult).then_inc(s_U, 1)
                for lv in range(LEVELS):
                    w = 4 if lv < LEVELS - 1 else 2
                    for p in range(CHAINS):
                        dve.wait_ge(s_dN, count(i, p, 1, lv, LEVELS))
                        dve.tensor_tensor(N[p][:, 0:w, :], N[p][:, 0:w, :],
                                          bank[p][1][:, 0:w * P].rearrange("p (a c) -> p a c", a=w),
                                          ALU.subtract).then_inc(s_N, 1)
                for p in range(CHAINS):
                    dve.wait_ge(s_v1p, count(i, p))
                    dve.tensor_tensor(v1[p][:, :], kv[p][:, 1, C:2 * C], bank[p][0][:, 256:384],
                                      ALU.subtract).then_inc(s_v1, 1)
                for p in range(CHAINS):
                    dve.wait_ge(s_Ap, count(i, p))
                    for t, c in ((0, slice(0, T)), (1, slice(T, T + P))):
                        dve.scalar_tensor_tensor(Pm[p][:, c], bank[p][0][:, c], beta[p][:, t:t + 1], Di[p][:, c],
                                                 ALU.mult, ALU.mult).then_inc(s_P, 1)
                for p in range(CHAINS):
                    dve.wait_ge(s_op, count(i, p))
                    dve.tensor_tensor(oT[p][:, :], bank[p][1][:, 0:T], gT[p][:, :], ALU.mult).then_inc(s_og, 1)
                for p in range(CHAINS):
                    dve.wait_ge(s_wop, count(i, p))
                    dve.wait_ge(s_xbo, count(i, p))
                    dve.tensor_tensor(x1[p][:, :, :], bank[p][0][:, :].rearrange("p (t c) -> p t c", t=NT),
                                      xbo[p][:, :, :], ALU.add).then_inc(s_x1, 1)
                    dve.wait_ge(s_x1, count(i, p))
                    stat(x1[p], p, 1)
                for p in range(CHAINS):
                    normed(xn[p], x1[p], p, 1)
                for p in range(CHAINS):
                    dve.wait_ge(s_sc, count(i, p))
                    dve.tensor_reduce(nmx[p][:, :],
                                      bank[p][0][:, 0:2 * P].rearrange("p (t c) -> p t c", t=NT)[:, :, 0:V],
                                      axis=AX_X, op=ALU.max, negate=True).then_inc(s_mx, 1)
                for p in range(CHAINS):
                    dve.wait_ge(s_es, count(i, p, 2))
                    dve.reciprocal(rs[p][:, :], sm[p][:, :]).then_inc(s_rr, 1)
                for p in range(CHAINS):
                    dve.wait_ge(s_co, count(i, p))
                    dve.wait_ge(s_rr, count(i, p))
                    dve.wait_ge(s_out[p], 32 * i + 32)
                    for t in range(NT):
                        dve.scalar_tensor_tensor(xo[p][:, t, :], bank[p][0][:, t * D:(t + 1) * D],
                                                 rs[p][:, t:t + 1], x1[p][:, t, :],
                                                 ALU.mult, ALU.add).then_inc(s_x2, 1)
                    dve.wait_ge(s_x2, count(i, p, 2))
                    stat(xo[p], p, 2)
                for p in range(CHAINS):
                    normed(xno[p], xo[p], p, 2)
                    dve.wait_ge(s_xn, count(i, p, 2, 2, 3))
                    dve.tensor_reduce(rs[p][:, 0:1], xno[p][:, :, :], axis=mybir.AxisListType.XY, op=ALU.max,
                                      apply_absolute_value=True).then_inc(s_pk, 1)
                    dve.wait_ge(s_pk, count(i, p))
                    dve.tensor_tensor(pk[p][:, :], pk[p][:, :], rs[p][:, 0:1], ALU.max).then_inc(s_pkm, 1)
            dve.wait_ge(s_pkm, CHAINS * ROUNDS)
            for n, p in enumerate(range(1, CHAINS)):
                dve.tensor_tensor(peak[:, :] if p == CHAINS - 1 else pk[0][:, :], pk[0][:, :], pk[p][:, :],
                                  ALU.max).then_inc(s_pkm, 1)
                dve.wait_ge(s_pkm, CHAINS * ROUNDS + n + 1)

        @block.tensor
        def _(pe):
            pe.wait_ge(s_w, 16 * WEIGHTS)
            pe.wait_ge(s_c, CONSTS)

            def turn(p, dst, src):
                for k in range(ND):
                    for t in range(NT):
                        last = pe.transpose(dst[:, k * T + t * P:k * T + (t + 1) * P],
                                            src[:, t, k * P:(k + 1) * P], ident[:, :])
                return last

            with pe.Fori(0, ROUNDS) as i:
                for p in range(CHAINS):
                    pe.wait_ge(s_xn, count(i, p, 2, 0, 3))
                    turn(p, bank[p][0], xn[p]).then_inc(s_tr, 1)
                    pe.wait_ge(s_cx[p], 16 * i + 16)
                    for k in range(ND):
                        last = pe.transpose(bank[p][1][:, k * V:(k + 1) * V], cx[p][:, k * P:(k + 1) * P],
                                            ident[0:V, 0:V])
                    last.then_inc(s_ctr, 1)
                for p in range(CHAINS):
                    b0, b1 = bank[p]
                    pe.wait_ge(s_xT, count(i, p, 1, 0, 2))
                    for t in range(NT):
                        for k in range(ND):
                            last = pe.matmul(b1[:, 256 + 2 * t:258 + 2 * t], xT[p][:, k, t * P:(t + 1) * P],
                                             Wab[:, k, :], start=k == 0, stop=k == ND - 1)
                    last.then_inc(s_ab, 1)
                    for m in range(2):
                        for k in range(ND):
                            last = pe.matmul(b0[:, m * T:(m + 1) * T], Wqg[:, k, m * C:(m + 1) * C],
                                             xT[p][:, k, :], start=k == 0, stop=k == ND - 1)
                    last.then_inc(s_pr, 1)
                for p in range(CHAINS):
                    pe.wait_ge(s_zab, count(i, p))
                    pe.wait_ge(s_cT, count(i, p))
                    for t in range(NT):
                        for k in range(ND):
                            last = pe.matmul(bank[p][1][:, t * 2 * C:(t + 1) * 2 * C],
                                             xT[p][:, k, t * P:(t + 1) * P], Wkv[:, k, :], start=k == 0,
                                             stop=k == ND - 1)
                    last.then_inc(s_kvp, 1)
                for p in range(CHAINS):
                    b0 = bank[p][0]
                    pe.wait_ge(s_R, count(i, p, 2))
                    pe.wait_ge(s_qT, count(i, p))
                    pe.wait_ge(s_ge, count(i, p))
                    pe.matmul(b0[:, 0:T], later[:, :], R[p][:, 0:T], start=True, stop=False)
                    pe.matmul(b0[:, P:T], ones[:, 0:P], R[p][:, T:T + P], start=False, stop=True)
                    pe.matmul(b0[:, T:T + P], later[:, :], R[p][:, T:T + P], start=True,
                              stop=True).then_inc(s_lD, 1)
                for p in range(CHAINS):
                    pe.wait_ge(s_kn, count(i, p, 2))
                    for t in range(NT):
                        last = pe.transpose(bank[p][1][:, t * P:(t + 1) * P], kn[p][:, t, :], ident[:, :])
                    last.then_inc(s_ktr, 1)
                for p in range(CHAINS):
                    pe.wait_ge(s_kT, count(i, p))
                    pe.wait_ge(s_kv, count(i, p))
                    pe.matmul(bank[p][1][:, 0:T], kT[p][:, 0:P], kT[p][:, :], start=True, stop=True)
                    pe.matmul(bank[p][1][:, T:T + P], kT[p][:, P:T], kT[p][:, P:T], start=True,
                              stop=True).then_inc(s_G, 1)
                for p in range(CHAINS):
                    pe.wait_ge(s_U, count(i, p, 2))
                    pe.wait_ge(s_Dx, count(i, p))
                    pe.transpose(bank[p][0][:, 0:P], U[p][:, 0:P], ident[:, :])
                    pe.transpose(bank[p][0][:, P:2 * P], U[p][:, 2 * P:3 * P], ident[:, :]).then_inc(s_utr, 1)
                for lv in range(LEVELS):
                    for p in range(CHAINS):
                        b0 = bank[p][0]
                        pe.wait_ge(s_Lm, count(i, p, LEVELS) - LEVELS + lv + 1)
                        if lv == 0:
                            pe.wait_ge(s_n0, count(i, p, 3))
                        else:
                            pe.wait_ge(s_N, count(i, p, 1, lv - 1, LEVELS))
                        for j in range(2):
                            last = pe.matmul(b0[:, j * P:(j + 1) * P], Lm[p][:, lv, j, :], N[p][:, j, :],
                                             start=True, stop=True)
                        last.then_inc(s_Yp, 1)
                    for p in range(CHAINS):
                        b1 = bank[p][1]
                        pe.wait_ge(s_Y, count(i, p, 1, lv, LEVELS))
                        for j in range(2):
                            last = pe.matmul(b1[:, j * P:(j + 1) * P], N[p][:, 2 + j, :], Y[p][:, j, :],
                                             start=True, stop=True)
                        if lv < LEVELS - 1:
                            for j in range(2):
                                last = pe.matmul(b1[:, (2 + j) * P:(3 + j) * P], Y[p][:, j, :], N[p][:, 2 + j, :],
                                                 start=True, stop=True)
                        last.then_inc(s_dN, 1)
                for p in range(CHAINS):
                    b0 = bank[p][0]
                    pe.wait_ge(s_N, count(i, p, 1, LEVELS - 1, LEVELS))
                    pe.wait_ge(s_Dx, count(i, p))
                    pe.matmul(b0[:, 0:P], N[p][:, 0, :], kv[p][:, 0, C:2 * C], start=True, stop=True)
                    pe.matmul(b0[:, P:2 * P], kv[p][:, 0, C:2 * C], N[p][:, 0, :], start=True,
                              stop=True).then_inc(s_w0p, 1)
                for p in range(CHAINS):
                    pe.wait_ge(s_w0, count(i, p, 2))
                    pe.matmul(bank[p][0][:, 256:384], U[p][:, P:2 * P], W0[p][:, :], start=True,
                              stop=True).then_inc(s_v1p, 1)
                for p in range(CHAINS):
                    pe.wait_ge(s_v1, count(i, p))
                    pe.matmul(bank[p][1][:, 0:P], v1[p][:, :], N[p][:, 1, :], start=True,
                              stop=True).then_inc(s_w1p, 1)
                for p in range(CHAINS):
                    b0 = bank[p][0]
                    pe.wait_ge(s_w1, count(i, p))
                    pe.matmul(b0[:, 0:T], WT[p][:, 0:P], qT[p][:, :], start=True, stop=True)
                    pe.matmul(b0[:, T:T + P], WT[p][:, P:T], qT[p][:, P:T], start=True,
                              stop=True).then_inc(s_Ap, 1)
                for p in range(CHAINS):
                    b1 = bank[p][1]
                    pe.wait_ge(s_P, count(i, p, 2))
                    pe.matmul(b1[:, 0:T], kn[p][:, 0, :], Pm[p][:, 0:T], start=True, stop=False)
                    pe.matmul(b1[:, P:T], kn[p][:, 1, :], Pm[p][:, T:T + P], start=False,
                              stop=True).then_inc(s_op, 1)
                for p in range(CHAINS):
                    b0 = bank[p][0]
                    pe.wait_ge(s_og, count(i, p))
                    for t in range(NT):
                        last = pe.matmul(b0[:, t * D:(t + 1) * D], oT[p][:, t * P:(t + 1) * P], Wo[:, :],
                                         start=True, stop=True)
                    last.then_inc(s_wop, 1)
                for p in range(CHAINS):
                    pe.wait_ge(s_xn, count(i, p, 2, 1, 3))
                    turn(p, bank[p][1], xn[p]).then_inc(s_tr, 1)
                for p in range(CHAINS):
                    b1 = bank[p][0]
                    pe.wait_ge(s_xT, count(i, p, 1, 1, 2))
                    for t in range(NT):
                        for k in range(ND):
                            last = pe.matmul(b1[:, t * P:t * P + V], xT[p][:, k, t * P:(t + 1) * P],
                                             cT[p][:, k, :], start=k == 0, stop=k == ND - 1)
                    last.then_inc(s_sc, 1)
                for p in range(CHAINS):
                    pe.wait_ge(s_es, count(i, p, 2))
                    for t in range(NT):
                        last = pe.transpose(bank[p][1][0:V, t * P:(t + 1) * P], es[p][:, t, :], ident[:, :])
                    last.then_inc(s_etr, 1)
                for p in range(CHAINS):
                    pe.wait_ge(s_eT, count(i, p))
                    for t in range(NT):
                        last = pe.matmul(bank[p][0][:, t * D:(t + 1) * D], eT[p][:, t * P:(t + 1) * P],
                                         cx[p][:, :], start=True, stop=True)
                    last.then_inc(s_co, 1)


def phase_weights(nc, A, K):
    with ExitStack() as ctx:
        def sb(name, shape, dt=F32):
            return ctx.enter_context(nc.sbuf_tensor("w_" + name, shape, dt))

        def sem(name):
            return ctx.enter_context(nc.semaphore("w_" + name))

        square = {n: sb(n, [P, ND, D]) for n in ("wq", "wk", "wv", "wp", "xq", "xk", "xv", "xp", "wr", "wi")}
        dft = sb("dft", [P, 3, ND, D])
        gate = sb("gate", [P, NI, D])
        up = sb("up", [P, NI, D])
        down = sb("down", [P, ND, I])
        inv = sb("inv", [P, NI])
        t1 = sb("t1", [P, ND, D])
        t2 = sb("t2", [P, ND, D])
        bank = [ctx.enter_context(nc.psum_tensor(f"w_b{k}", [P, 512], F32)) for k in range(8)]
        s_in = sem("loaded")
        s_c = sem("cleared")
        s_q = sem("quantised")
        s_pe = sem("turned")
        s_ev = sem("evacuated")
        s_ch = sem("chain")
        block = ctx.enter_context(nc.Block())
        tiles = [(j, min(P, I - j * P)) for j in range(NI)]
        CLEARS = 1 + 5 + 4
        flat = {"wq": A["L1_attn_Wq"].rearrange("h e d -> (h e) d"), "wk": A["L1_attn_Wk"].rearrange("h e d -> (h e) d"),
                "wv": A["L1_attn_Wv"].rearrange("h e d -> (h e) d"), "wp": A["L1_attn_Wp"],
                "xq": A["L1_xattn_Wq"], "xk": A["L1_xattn_Wk"], "xv": A["L1_xattn_Wv"], "xp": A["L1_xattn_Wp"],
                "wr": A["L1_ffn_w_freq_real"], "wi": A["L1_ffn_w_freq_imag"]}

        @block.sync
        def _(sp):
            n = 0
            for name, w in flat.items():
                sp.dma_start(square[name][:, :, :], w.rearrange("(k p) d -> p k d", p=P)).then_inc(s_in, 16)
                n += 1
            for c in range(3):
                sp.dma_start(dft[:, c, :, :], A["dft"][c, :, :].rearrange("(k p) d -> p k d", p=P)).then_inc(s_in, 16)
            for dst, w in ((gate, A["L0_ffn_w_gate"]), (up, A["L0_ffn_w_up"])):
                sp.dma_start(dst[:, 0:NI - 1, :], w[0:(NI - 1) * P, :].rearrange("(k p) d -> p k d", p=P)).then_inc(s_in, 16)
                sp.dma_start(dst[0:LASTI, NI - 1, :], w[(NI - 1) * P:I, :]).then_inc(s_in, 16)
            sp.dma_start(down[:, :, :], A["L0_ffn_w_down"].rearrange("(k p) d -> p k d", p=P)).then_inc(s_in, 16)
            for name, dst in (("L1_attn_bp", K.bp), ("L1_ffn_bias", K.bf)):
                sp.dma_start(dst[:, 0, :], A[name].partition_broadcast(P)).then_inc(s_in, 16)
            for name, dst in (("L1_attn_bq", K.bq), ("L1_attn_bk", K.bk), ("L1_attn_bv", K.bv)):
                sp.dma_start(dst[:, 0, :], A[name].rearrange("h e -> (h e)").partition_broadcast(P)).then_inc(s_in, 16)
            sp.dma_start(K.clip[:, 0:1], A["L0_ffn_clip_x"].partition_broadcast(P)).then_inc(s_in, 16)
            sp.dma_start(K.clip[:, 1:2], A["L0_ffn_clip_down"].partition_broadcast(P)).then_inc(s_in, 16)
            sp.dma_start(K.focus[:, :], A["L1_xattn_focusing_factor"].partition_broadcast(P)).then_inc(s_in, 16)
            sp.dma_start(K.rank[:, 0, :], A["rank"].partition_broadcast(P)).then_inc(s_in, 16)

        LOADS = len(flat) + 3 + 4 + 1 + 9

        @block.gpsimd
        def _(pool):
            n = 0
            pool.memset(K.wd[:, :, :], 0.0).then_inc(s_c, 1)
            n = 1
            pool.memset(K.magic[:, :], -MAGIC).then_inc(s_c, 1)
            pool.memset(K.eps[:, :], EPS).then_inc(s_c, 1)
            pool.memset(K.one77[:, :], 1.0 / V).then_inc(s_c, 1)
            pool.memset(K.heads[:, :, :], 1.0).then_inc(s_c, 1)
            pool.memset(K.blocks[:, :, :], 1.0 / T).then_inc(s_c, 1)
            n += 5
            pool.wait_ge(s_c, n)
            for out, w in ((K.heads, 1), (K.blocks, HD)):
                pool.affine_select(out=out[:, :, :], in_=out[:, :, :], compare_op=ALU.is_ge, fill=0.0, base=0,
                                   pattern=[[-HD, P // HD], [0, w]], channel_multiplier=1).then_inc(s_c, 1)
            pool.wait_ge(s_c, n + 2)
            for out, w in ((K.heads, 1), (K.blocks, HD)):
                pool.affine_select(out=out[:, :, :], in_=out[:, :, :], compare_op=ALU.is_gt, fill=0.0, base=HD,
                                   pattern=[[HD, P // HD], [0, w]], channel_multiplier=-1).then_inc(s_c, 1)

        @block.vector
        def _(dve):
            n = 0

            def link(ins):
                nonlocal n
                n += 1
                ins.then_inc(s_ch, 1)
                dve.wait_ge(s_ch, n)

            dve.wait_ge(s_in, 16 * LOADS)
            dve.wait_ge(s_c, CLEARS)
            link(dve.tensor_scalar(K.bq[:, :, :], K.bq[:, :, :], 0.25, None, ALU.mult))

            def quantise(part, scale, inv):
                link(dve.tensor_reduce(scale, part, axis=AX_X, op=ALU.max, apply_absolute_value=True))
                link(dve.tensor_scalar(scale, scale, 1.0 / QMAX, None, ALU.mult))
                link(dve.reciprocal(inv, scale))
                link(dve.tensor_scalar(part, part, inv, QMAX, ALU.mult, ALU.min))
                link(dve.tensor_scalar(part, part, -QMAX - 1.0, MAGIC, ALU.max, ALU.add))
                link(dve.tensor_scalar(part, part, -MAGIC, None, ALU.add))

            for w, scale in ((gate, K.sgate), (up, K.sup)):
                for j, m in tiles:
                    quantise(w[0:m, j, :], scale[0:m, j:j + 1], inv[0:m, 0:1])
            for k in range(ND):
                quantise(down[:, k, :], K.sdown[:, k:k + 1], inv[:, 0:1])
            for k in range(ND):
                link(dve.tensor_copy(K.srep[:, k, :], K.sdown[:, k:k + 1].to_broadcast([P, P])))
            dve.memset(inv[:, 0:1], 0.0).then_inc(s_q, 1)

        jobs = []

        def turn(name, out, scale=1.0):
            def go(pe, b):
                for k in range(ND):
                    for o in range(ND):
                        last = pe.transpose(b[:, k * D + o * P:k * D + (o + 1) * P],
                                            square[name][:, o, k * P:(k + 1) * P], K.ident[:, :])
                return last
            jobs.append((go, lambda act, b: act.activation(out, b[:, :], ACT.Copy, scale=scale)))

        def mix(terms, out, scale):
            def go(pe, b):
                for m in range(ND):
                    for n, (x, y, k) in enumerate([(x, y, k) for x, y in terms for k in range(ND)]):
                        last = pe.matmul(b[:, m * D:(m + 1) * D], x[:, k, m * P:(m + 1) * P], y[:, k, :],
                                         start=n == 0, stop=n == 2 * ND - 1)
                return last
            jobs.append((go, lambda act, b: act.activation(out[:, :, :], b[:, :], ACT.Copy, scale=scale)))

        mix([(square["wr"], dft[:, 0]), (square["wi"], dft[:, 1])], t1, 1.0)
        mix([(square["wi"], dft[:, 0]), (square["wr"], dft[:, 2])], t2, 1.0)
        turn("wq", K.Wq[:, :, :], 0.25)
        turn("wk", K.Wk[:, :, :])
        turn("wv", K.Wv[:, :, :])
        turn("wp", K.Wp[:, :, :])
        turn("xq", K.Xq[:, :, :])
        turn("xk", K.Xkv[:, :, 0:D])
        turn("xv", K.Xkv[:, :, D:2 * D])
        turn("xp", K.Xp[:, :, :])
        mix([(t1, dft[:, 0]), (t2, dft[:, 2])], K.M, 1.0 / D)
        PLAIN = len(jobs)
        for w, out in ((gate, K.wg), (up, K.wu)):
            for k in range(ND):
                for js in (range(0, 4), range(4, NI)):
                    def go(pe, b, w=w, k=k, js=js):
                        for j in js:
                            m = min(P, I - j * P)
                            last = pe.transpose(b[:, (j - js[0]) * P:(j - js[0]) * P + m],
                                                w[0:m, j, k * P:(k + 1) * P], K.ident[0:m, 0:m])
                        return last
                    lo, hi = js[0] * P, min(I, (js[-1] + 1) * P)
                    jobs.append((go, lambda act, b, out=out, k=k, lo=lo, hi=hi:
                                 act.activation(out[:, k, lo:hi], b[:, 0:hi - lo], ACT.Copy)))
        for j, m in tiles:
            def go(pe, b, j=j, m=m):
                for k in range(ND):
                    last = pe.transpose(b[0:m, k * P:(k + 1) * P], down[:, k, j * P:j * P + m], K.ident[:, :])
                return last
            jobs.append((go, lambda act, b, j=j, m=m: act.activation(K.wd[0:m, j, :], b[0:m, 0:D], ACT.Copy)))

        def scales(pe, b):
            for k in range(ND):
                last = pe.matmul(b[:, k * P:(k + 1) * P], K.srep[:, k, :], K.ident[:, :], start=True, stop=True)
            return last
        jobs.append((scales, lambda act, b: act.activation(K.srow[:, 0, :], b[:, 0:D], ACT.Copy)))

        @block.tensor
        def _(pe):
            pe.wait_ge(s_in, 16 * LOADS)
            for n, (go, _) in enumerate(jobs):
                if n >= 8:
                    pe.wait_ge(s_ev, n - 7)
                if n == PLAIN - 1:
                    pe.wait_ge(s_ev, 2)
                if n == PLAIN:
                    pe.wait_ge(s_q, 1)
                go(pe, bank[n % 8]).then_inc(s_pe, 1)

        @block.scalar
        def _(act):
            act.wait_ge(s_c, CLEARS)
            for n, (_, take) in enumerate(jobs):
                act.wait_ge(s_pe, n + 1)
                take(act, bank[n % 8]).then_inc(s_ev, 1)
            act.wait_ge(s_ev, len(jobs))


def phase_gate_up(nc, K, xn3, hs):
    with ExitStack() as ctx:
        def sb(name, shape, dt=F32):
            return ctx.enter_context(nc.sbuf_tensor("b_" + name, shape, dt))

        def sb2(name, shape, dt=F32):
            return [sb(f"{name}{p}", shape, dt) for p in range(2)]

        def sem(name):
            return ctx.enter_context(nc.semaphore("b_" + name))

        def sem2(name):
            return [sem(f"{name}{p}") for p in range(2)]

        BANKS = 3
        x = sb2("x", [P, NT, D])
        xq = sb2("xq", [P, NT, D])
        xT = sb2("xT", [P, ND, T], BF16)
        si = [sb2(f"si{r}", [P, T]) for r in range(BANKS)]
        h = sb2("h", [P, NI, T])
        part = sb2("part", [P, 1])
        pk = sb2("pk", [P, 1])
        sg = sb("sg", [P, NI])
        su = sb("su", [P, NI])
        g = sb("g", [P, 4])
        tr = [ctx.enter_context(nc.psum_tensor(f"b_t{p}", [P, 512], F32)) for p in range(2)]
        gu = [[ctx.enter_context(nc.psum_tensor(f"b_g{p}{r}", [P, 512], F32)) for r in range(BANKS)]
              for p in range(2)]
        s_g = sem("peak_all")
        s_e = sem("clip_exp")
        s_ch = sem("chain")
        s_sc = sem("scales")
        s_z = sem("zeroed")
        s_x = sem2("x_in")
        s_q1 = sem2("clipped")
        s_q2 = sem2("rounded")
        s_tr = sem2("turned")
        s_xT = sem2("xT")
        s_gu = [sem2(f"gate_up{r}") for r in range(BANKS)]
        s_si = [sem2(f"silu{r}") for r in range(BANKS)]
        s_h = [sem2(f"h{r}") for r in range(BANKS)]
        s_pp = sem2("part")
        s_pk = sem2("peak")
        s_out = sem2("stored")
        block = ctx.enter_context(nc.Block())
        tiles = [(j, min(P, I - j * P)) for j in range(NI)]

        @block.sync
        def _(sp):
            for p in range(2):
                sp.dma_start(x[p][:, :, :], rows(xn3, p)).then_inc(s_x[p], 16)
            with sp.Fori(0, PAIRS - 1) as i:
                for p in range(2):
                    sp.wait_ge(s_q1[p], i + 1)
                    sp.dma_start(x[p][:, :, :], rows(xn3, 2 * i + 2 + p)).then_inc(s_x[p], 16)
                for p in range(2):
                    for r in range(BANKS):
                        sp.wait_ge(s_h[r][p], 2 * i + 2)
                    sp.dma_start(hs[bass.ds(2 * i + p, 1), :, :].rearrange("o p c -> p (o c)"),
                                 h[p][:, :, :].rearrange("p j t -> p (j t)")).then_inc(s_out[p], 16)
            for p in range(2):
                for r in range(BANKS):
                    sp.wait_ge(s_h[r][p], 2 * PAIRS)
                sp.dma_start(hs[2 * PAIRS - 2 + p, :, :], h[p][:, :, :].rearrange("p j t -> p (j t)")).then_inc(s_out[p], 16)
            for p in range(2):
                sp.wait_ge(s_out[p], 16 * PAIRS)

        @block.gpsimd
        def _(pool):
            pool.partition_all_reduce(g[:, 0:1], K.peak[:, :], P, RMAX).then_inc(s_g, 1)
            for p in range(2):
                pool.memset(h[p][:, :, :], 0.0).then_inc(s_z, 1)
                pool.memset(pk[p][:, :], 0.0).then_inc(s_z, 1)

        @block.scalar
        def _(act):
            act.activation(K.cexp[:, :], K.clip[:, :], ACT.Exp, scale=-1.0).then_inc(s_e, 1)
            act.wait_ge(s_sc, 1)
            with act.Fori(0, PAIRS) as i:
                for p in range(2):
                    act.wait_ge(s_tr[p], i + 1)
                    act.activation(xT[p][:, :, :], tr[p][:, :], ACT.Identity,
                                   bias=K.magic[:, :]).then_inc(s_xT[p], 1)
                for j, m in tiles:
                    r = j % BANKS
                    for p in range(2):
                        act.wait_ge(s_gu[r][p], 2 * i + 1 + j // BANKS)
                        act.activation(si[r][p][0:m, :], gu[p][r][0:m, 0:T], ACT.Silu,
                                       scale=sg[0:m, j:j + 1]).then_inc(s_si[r][p], 1)

        @block.vector
        def _(dve):
            n = 0

            def link(ins):
                nonlocal n
                n += 1
                ins.then_inc(s_ch, 1)
                dve.wait_ge(s_ch, n)

            dve.wait_ge(s_e, 1)
            link(dve.tensor_scalar(K.cexp[:, :], K.cexp[:, :], 1.0, None, ALU.add))
            link(dve.reciprocal(K.csig[:, :], K.cexp[:, :]))
            dve.wait_ge(s_g, 1)
            link(dve.tensor_tensor(g[:, 1:2], g[:, 0:1], K.csig[:, 0:1], ALU.mult))
            link(dve.tensor_scalar(g[:, 1:2], g[:, 1:2], 1.0 / QMAX, None, ALU.mult))
            link(dve.reciprocal(g[:, 2:3], g[:, 1:2]))
            link(dve.tensor_scalar(sg[:, 0:NI - 1], K.sgate[:, 0:NI - 1], g[:, 1:2], None, ALU.mult))
            link(dve.tensor_scalar(su[:, 0:NI - 1], K.sup[:, 0:NI - 1], g[:, 1:2], None, ALU.mult))
            link(dve.tensor_scalar(sg[0:LASTI, NI - 1:NI], K.sgate[0:LASTI, NI - 1:NI], g[0:LASTI, 1:2], None, ALU.mult))
            dve.tensor_scalar(su[0:LASTI, NI - 1:NI], K.sup[0:LASTI, NI - 1:NI], g[0:LASTI, 1:2], None,
                              ALU.mult).then_inc(s_sc, 1)
            dve.wait_ge(s_sc, 1)
            dve.wait_ge(s_z, 4)
            with dve.Fori(0, PAIRS) as i:
                for p in range(2):
                    dve.wait_ge(s_x[p], 16 * i + 16)
                    dve.wait_ge(s_tr[p], i)
                    dve.tensor_scalar(xq[p][:, :, :], x[p][:, :, :], g[:, 2:3], QMAX, ALU.mult,
                                      ALU.min).then_inc(s_q1[p], 1)
                for p in range(2):
                    dve.wait_ge(s_q1[p], i + 1)
                    dve.tensor_scalar(xq[p][:, :, :], xq[p][:, :, :], -QMAX - 1.0, MAGIC, ALU.max,
                                      ALU.add).then_inc(s_q2[p], 1)
                for p in range(2):
                    dve.wait_ge(s_out[p], 16 * i)
                for j, m in tiles:
                    r = j % BANKS
                    for p in range(2):
                        dve.wait_ge(s_si[r][p], 2 * i + 1 + j // BANKS)
                        dve.scalar_tensor_tensor(h[p][0:m, j, :], gu[p][r][0:m, T:2 * T], su[0:m, j:j + 1],
                                                 si[r][p][0:m, :], ALU.mult, ALU.mult).then_inc(s_h[r][p], 1)
                for p in range(2):
                    for r in range(BANKS):
                        dve.wait_ge(s_h[r][p], 2 * i + 2)
                    dve.tensor_reduce(part[p][:, :], h[p][:, :, :], axis=mybir.AxisListType.XY, op=ALU.max,
                                      apply_absolute_value=True).then_inc(s_pp[p], 1)
                for p in range(2):
                    dve.wait_ge(s_pp[p], i + 1)
                    dve.tensor_tensor(pk[p][:, :], pk[p][:, :], part[p][:, :], ALU.max).then_inc(s_pk[p], 1)
            for p in range(2):
                dve.wait_ge(s_pk[p], PAIRS)
            dve.tensor_tensor(K.hpeak[:, :], pk[0][:, :], pk[1][:, :], ALU.max).then_inc(s_sc, 1)
            dve.wait_ge(s_sc, 2)

        @block.tensor
        def _(pe):
            with pe.Fori(0, PAIRS) as i:
                for p in range(2):
                    pe.wait_ge(s_q2[p], i + 1)
                    for k in range(ND):
                        for t in range(NT):
                            last = pe.transpose(tr[p][:, k * T + t * P:k * T + (t + 1) * P],
                                                xq[p][:, t, k * P:(k + 1) * P], K.ident[:, :])
                    last.then_inc(s_tr[p], 1)
                for p in range(2):
                    pe.wait_ge(s_xT[p], i + 1)
                for j, m in tiles:
                    r = j % BANKS
                    for p in range(2):
                        pe.wait_ge(s_h[r][p], 2 * i + j // BANKS)
                        for c, w in enumerate((K.wg, K.wu)):
                            for k in range(ND):
                                last = pe.matmul(gu[p][r][0:m, c * T:(c + 1) * T], w[:, k, j * P:j * P + m],
                                                 xT[p][:, k, :], start=k == 0, stop=k == ND - 1)
                        last.then_inc(s_gu[r][p], 1)


def phase_tail(nc, A, K, x2, hs, out):
    with ExitStack() as ctx:
        def sb(name, shape, dt=F32):
            return ctx.enter_context(nc.sbuf_tensor("c_" + name, shape, dt))

        def sb2(name, shape, dt=F32):
            return [sb(f"{name}{p}", shape, dt) for p in range(2)]

        def sem(name):
            return ctx.enter_context(nc.semaphore("c_" + name))

        def sem2(name):
            return [sem(f"{name}{p}") for p in range(2)]

        STEPS = H // 2
        NE = 4
        KW = P + P // HD
        half = sb("half", [P, NT])
        lneps = sb("lneps", [P, NT])
        g = sb("g", [P, 4])
        srow = sb("srow", [P, 1, D])
        zero = sb("zero", [P, 1])
        idle = sb2("idle", [P, 1])
        h = sb2("h", [P, NI, T])
        hq = sb2("hq", [P, NI, T], BF16)
        x = sb2("x", [P, NT, D])
        x3 = sb2("x3", [P, NT, D])
        xb = sb2("xb", [P, NT, D])
        x4 = sb2("x4", [P, NT, D])
        xn = sb2("xn", [P, NT, D])
        xT = sb2("xT", [P, ND, T])
        stats = sb2("stats", [P, NT, 6])
        mv = sb2("mv", [P, NT, 2])
        rstd = sb2("rstd", [P, NT])
        qf = sb2("qf", [P, NT, D])
        Qs = sb2("Qs", [P, NT, H, P], BF16)
        Ks = sb("Ks", [P, NT, H, P], BF16)
        QS = sb2("QS", [P, H, T], BF16)
        KS = sb2("KS", [P, H, T], BF16)
        mr = sb2("mr", [P, NT, H])
        vs = sb2("vs", [P, NT, H, 32])
        E = [sb(f"E{n}", [P, 2, NT, T]) for n in range(NE)]
        MR = 6 * HD
        oT = sb2("oT", [P, 4, T])
        ro = sb2("ro", [P, NT, H])
        o = sb2("o", [P, NT, D])
        cx = sb2("cx", [V, D])
        cT = sb2("cT", [P, ND, V])
        kvc = sb2("kvc", [V, 2 * D])
        kl = sb2("kl", [V, 1, D])
        ke = sb2("ke", [V, 1, D])
        kk = sb2("kk", [V, 1, D], I32)
        kt = sb2("kt", [V, H, 8])
        ks = sb2("ks", [V, 4])
        KV = sb2("KV", [P, ND, KW])
        qe = sb2("qe", [P, NT, D])
        qk = sb2("qk", [P, NT, D], I32)
        qt = sb2("qt", [P, NT * H, 8])
        qs = sb2("qs", [P, 4, NT])
        rz = sb2("rz", [P, NT, ND, P // HD])
        xo = sb2("xo", [P, NT, D])
        S = [ctx.enter_context(nc.psum_tensor(f"c_s{r}", [P, 1024], F32)) for r in range(2)]
        m0 = [ctx.enter_context(nc.psum_tensor(f"c_m0{p}", [P, 512], F32)) for p in range(2)]
        m1 = [ctx.enter_context(nc.psum_tensor(f"c_m1{p}", [P, 512], F32)) for p in range(2)]

        s_g = sem("peak_all")
        s_ch = sem("chain")
        s_c = sem("constants")
        s_h = sem2("h_in")
        s_x = sem2("x_in")
        s_cx = sem2("ctx_in")
        s_h1 = sem2("h_clipped")
        s_h2 = sem2("h_rounded")
        s_hq = sem2("hq")
        s_dn = sem2("down")
        s_xs = sem2("down_scaled")
        s_x3 = sem2("x3")
        s_xb = sem2("residual_bias")
        s_bs = sem2("stats")
        s_mv = sem2("meanvar")
        s_ve = sem2("vareps")
        s_rs = sem2("rstd")
        s_xn = sem2("xn")
        s_tr = sem2("turned")
        s_xT = sem2("xT")
        s_ctr = sem2("ctx_turned")
        s_cT = sem2("cT")
        s_ckv = sem2("ctx_kv_product")
        s_kvc = sem2("ctx_kv")
        s_kf = sem2("k_focus")
        s_kln = sem2("k_log")
        s_ke = sem2("k_exp")
        s_vp = sem2("v_product")
        s_vs = sem2("v")
        s_qp = sem2("q_product")
        s_kp = sem2("k_product")
        s_qb = sem2("qk_biased")
        s_p1 = sem2("part1")
        s_r1 = sem2("rest1")
        s_p2 = sem2("part2")
        s_p3 = sem2("part3")
        s_sk = sem2("stacked")
        s_st = sem2("stack_turned")
        s_qe0 = sem2("stack_out_dve")
        s_qe1 = sem2("stack_out_act")
        s_mr = sem2("maxima_parts")
        s_s1 = [sem(f"scores_st{r}") for r in range(2)]
        s_mx = [sem(f"maxima{r}") for r in range(2)]
        s_mt = sem2("maxima_turned")
        s_qm = sem2("maxima_rows")
        s_s2 = [sem(f"scores_ts{r}") for r in range(2)]
        s_ex = [sem(f"exponentials{r}") for r in range(2)]
        s_av = [sem(f"weighted{n}") for n in range(NE)]
        s_ao = sem2("attention_out")
        s_oT = sem2("oT")
        s_ob = sem2("o_turned")
        s_ro = sem2("ro")
        s_o = sem2("o")
        s_pr = sem2("projected")
        s_x4 = sem2("x4")
        s_xq = sem2("q_pre")
        s_kv = sem2("kv_product")
        s_KV = sem2("KV")
        s_qf = sem2("q_focus")
        s_qln = sem2("q_log")
        s_qe = sem2("q_exp")
        s_y = sem2("y_product")
        s_z = sem2("z")
        s_yn = sem2("y")
        s_x5 = sem2("x5")
        s_x6 = sem2("x6")
        s_out = sem2("stored")
        block = ctx.enter_context(nc.Block())
        TURNS = 6
        PRE = 8

        @block.sync
        def _(sp):
            def load_h(p, b):
                sp.dma_start(h[p][:, :, :].rearrange("p j t -> p (j t)"),
                             hs[bass.ds(b, 1), :, :].rearrange("o p c -> p (o c)")).then_inc(s_h[p], 16)

            def load_x(p, b):
                sp.dma_start(x[p][:, :, :], rows(x2, b)).then_inc(s_x[p], 16)

            def load_ctx(p, b):
                sp.dma_start(cx[p][:, :], A["ctx_1024"][bass.ds(b, 1), :, :]
                             .rearrange("o v d -> v (o d)")).then_inc(s_cx[p], 16)

            for p in range(2):
                load_h(p, p)
                load_ctx(p, p)
                load_x(p, p)
            with sp.Fori(0, PAIRS - 1) as i:
                for p in range(2):
                    sp.wait_ge(s_hq[p], i + 1)
                    load_h(p, 2 * i + 2 + p)
                    sp.wait_ge(s_ctr[p], i + 1)
                    load_ctx(p, 2 * i + 2 + p)
                    sp.wait_ge(s_x3[p], i + 1)
                    load_x(p, 2 * i + 2 + p)
                for p in range(2):
                    sp.wait_ge(s_x6[p], i + 1)
                    sp.dma_start(rows(out, 2 * i + p), xo[p][:, :, :]).then_inc(s_out[p], 16)
            for p in range(2):
                sp.wait_ge(s_x6[p], PAIRS)
                sp.dma_start(rows(out, 2 * (PAIRS - 1) + p), xo[p][:, :, :]).then_inc(s_out[p], 16)
            for p in range(2):
                sp.wait_ge(s_out[p], 16 * PAIRS)

        @block.gpsimd
        def _(pool):
            pool.partition_all_reduce(g[:, 0:1], K.hpeak[:, :], P, RMAX).then_inc(s_g, 1)
            pool.memset(half[:, :], -0.5).then_inc(s_c, 1)
            pool.memset(lneps[:, :], LN_EPS).then_inc(s_c, 1)
            for p in range(2):
                pool.memset(Qs[p][:, :, :, :], 0.0).then_inc(s_c, 1)
                pool.memset(vs[p][:, :, :, :], 0.0).then_inc(s_c, 1)
            pool.memset(Ks[:, :, :, :], 0.0).then_inc(s_c, 1)
            pool.memset(zero[:, :], 0.0).then_inc(s_c, 1)
            pool.wait_ge(s_c, PRE)
            pool.memset(Ks[:, :, :, MR:MR + 3], 1.0).then_inc(s_c, 1)
            for p in range(2):
                pool.memset(vs[p][:, :, :, HD:HD + 1], 1.0).then_inc(s_c, 1)

            def rsqrt(p, n):
                pool.wait_ge(s_mv[p], 6 * i + 2 * n + 2)
                pool.wait_ge(s_xn[p], 6 * i + 2 * n)
                pool.tensor_tensor(rstd[p][:, :], mv[p][:, :, 1], lneps[:, :], ALU.add).then_inc(s_ve[p], 1)
                pool.wait_ge(s_ve[p], 3 * i + n + 1)
                pool.tensor_tensor(rstd[p][:, :], rstd[p][:, :], half[:, :], ALU.pow).then_inc(s_rs[p], 1)

            def parts(p, stack, n, a, b, c):
                qh = qf[p][:, :, :].rearrange("p t (h e) -> p (t h) e", h=H)
                slot = [stack[:, :, :, s * HD:(s + 1) * HD].rearrange("p t h e -> p (t h) e") for s in (a, b, c)]
                pool.wait_ge(s_p1[p], 2 * i + n + 1)
                pool.tensor_tensor(qh, qh, slot[0], ALU.subtract).then_inc(s_r1[p], 1)
                pool.wait_ge(s_r1[p], 2 * i + n + 1)
                pool.tensor_tensor(slot[1], qh, zero[:, :].unsqueeze(2).to_broadcast([P, NT * H, HD]),
                                   ALU.add).then_inc(s_p2[p], 1)
                pool.wait_ge(s_p2[p], 2 * i + n + 1)
                pool.tensor_tensor(slot[2], qh, slot[1], ALU.subtract).then_inc(s_p3[p], 1)

            with pool.Fori(0, PAIRS) as i:
                for p in range(2):
                    rsqrt(p, 0)
                for p in range(2):
                    parts(p, Qs[p], 0, 0, 3, 5)
                for p in range(2):
                    parts(p, Ks, 1, 0, 1, 2)
                for p in range(2):
                    pool.wait_ge(s_x3[p], i + 1)
                    pool.wait_ge(s_x6[p], i)
                    pool.tensor_tensor(xb[p][:, :, :], x3[p][:, :, :], K.bp[:, :, :].to_broadcast([P, NT, D]),
                                       ALU.add).then_inc(s_xb[p], 1)
                for p in range(2):
                    rsqrt(p, 1)
                for p in range(2):
                    rsqrt(p, 2)
                    pool.wait_ge(s_x5[p], i + 1)
                    pool.tensor_tensor(xb[p][:, :, :], x3[p][:, :, :], K.bf[:, :, :].to_broadcast([P, NT, D]),
                                       ALU.add).then_inc(s_xb[p], 1)

        @block.scalar
        def _(act):
            act.preload_act_table_set("natural_log_exp_and_others")
            with act.Fori(0, PAIRS) as i:
                for p in range(2):
                    act.wait_ge(s_ctr[p], i + 1)
                    act.copy(cT[p][:, :, :], m1[p][:, 0:ND * V]).then_inc(s_cT[p], 1)
                for p in range(2):
                    act.wait_ge(s_h2[p], i + 1)
                    act.activation(hq[p][:, :, :], h[p][:, :, :], ACT.Identity,
                                   bias=K.magic[:, :]).then_inc(s_hq[p], 1)
                for p in range(2):
                    act.wait_ge(s_ckv[p], i + 1)
                    act.copy(kvc[p][:, :], m1[p][0:V, :]).then_inc(s_kvc[p], 1)
                for p in range(2):
                    act.wait_ge(s_kf[p], 7 * i + 1)
                    act.activation(kl[p][:, 0, :], kl[p][:, 0, :], ACT.Ln, bias=K.eps[0:V, :]).then_inc(s_kln[p], 1)
                for p in range(2):
                    act.wait_ge(s_kf[p], 7 * i + 3)
                    act.activation(ke[p][:, 0, :], kl[p][:, 0, :], ACT.Exp, bias=ks[p][:, 1:2],
                                   accum_out=ks[p][:, 2:3]).then_inc(s_ke[p], 1)

                def turned(p, n, bank):
                    act.wait_ge(s_tr[p], TURNS * i + n + 1)
                    act.copy(xT[p][:, :, :], bank[p][:, :]).then_inc(s_xT[p], 1)

                for p in range(2):
                    turned(p, 0, m1)
                def part1(p, stack, n):
                    act.wait_ge(s_qb[p], 2 * i + n + 1)
                    act.copy(stack[:, :, :, 0:HD].rearrange("p t h e -> p (t h) e"),
                             qf[p][:, :, :].rearrange("p t (h e) -> p (t h) e", h=H)).then_inc(s_p1[p], 1)

                def stack_out(p, n, dst):
                    for c in (1, 3):
                        act.wait_ge(s_st[p], 8 * i + 4 * n + c + 1)
                        act.copy(dst[p][:, 4 * c:4 * c + 4, :], m1[p][:, :].bitcast(BF16)).then_inc(s_qe1[p], 1)

                for p in range(2):
                    part1(p, Qs[p], 0)
                stack_out(0, 0, QS)
                part1(0, Ks, 1)
                stack_out(1, 0, QS)
                stack_out(0, 1, KS)
                act.wait_ge(s_st[0], 8 * i + 8)
                act.wait_ge(s_sk[0], 4 * i + 4)
                part1(1, Ks, 1)
                stack_out(1, 1, KS)
                for p in range(2):
                    for c in range(4):
                        act.wait_ge(s_mt[p], 4 * i + c + 1)
                        act.copy(QS[p][MR:P, 4 * c:4 * c + 4, :],
                                 (m0, m1)[c % 2][p][MR:P, :].bitcast(BF16)).then_inc(s_qm[p], 1)
                for p in range(2):
                    for u in range(STEPS):
                        n = p * STEPS + u
                        act.wait_ge(s_s2[u % 2], STEPS * i + n // 2 + 1)
                        act.wait_ge(s_av[n % NE], 4 * i + n // NE)
                        act.activation(E[n % NE][:, :, :, :], S[u % 2][:, :], ACT.Exp).then_inc(s_ex[u % 2], 1)
                    act.wait_ge(s_ao[p], i + 1)
                    for c in range(2):
                        act.copy(oT[p][:, 2 * c:2 * c + 2, :], (m0, m1)[c][p][:, :]).then_inc(s_oT[p], 1)
                for p in range(2):
                    turned(p, 1, m0)
                for p in range(2):
                    turned(p, 2, m0)
                for p in range(2):
                    act.wait_ge(s_xq[p], i + 1)
                    act.copy(qe[p][:, :, :], m1[p][:, :]).then_inc(s_qe[p], 1)
                for p in range(2):
                    act.wait_ge(s_qf[p], 9 * i + 2)
                    act.activation(o[p][:, :, :], o[p][:, :, :], ACT.Ln, bias=K.eps[:, :]).then_inc(s_qln[p], 1)
                for p in range(2):
                    act.wait_ge(s_qf[p], 9 * i + 4)
                    for t in range(NT):
                        act.activation(qe[p][:, t, :], o[p][:, t, :], ACT.Exp, bias=qs[p][:, 1, t:t + 1],
                                       accum_out=qs[p][:, 2, t:t + 1]).then_inc(s_qe[p], 1)
                for n in (3, 4, 5):
                    for p in range(2):
                        turned(p, n, m0)

        @block.vector
        def _(dve):
            n = 0

            def link(ins):
                nonlocal n
                n += 1
                ins.then_inc(s_ch, 1)
                dve.wait_ge(s_ch, n)

            dve.wait_ge(s_g, 1)
            link(dve.tensor_tensor(g[:, 1:2], g[:, 0:1], K.csig[:, 1:2], ALU.mult))
            link(dve.tensor_scalar(g[:, 1:2], g[:, 1:2], 1.0 / QMAX, None, ALU.mult))
            link(dve.reciprocal(g[:, 2:3], g[:, 1:2]))
            link(dve.tensor_scalar(srow[:, 0, :], K.srow[:, 0, :], g[:, 1:2], None, ALU.mult))
            dve.wait_ge(s_c, PRE + 3)

            def stat(src, p, n):
                for t in range(NT):
                    dve.bn_stats(stats[p][:, t, :], src[:, t, :]).then_inc(s_bs[p], 1)
                dve.wait_ge(s_bs[p], 6 * i + 2 * n + 2)
                dve.memset(idle[p][:, :], 0.0)
                for t in range(NT):
                    dve.bn_aggr(mv[p][:, t, :], stats[p][:, t, :]).then_inc(s_mv[p], 1)

            def normed(src, p, n):
                for t in range(NT):
                    dve.wait_ge(s_rs[p], 3 * i + n + 1)
                    dve.tensor_scalar(xn[p][:, t, :], src[:, t, :], mv[p][:, t, 0:1], rstd[p][:, t:t + 1],
                                      ALU.subtract, ALU.mult).then_inc(s_xn[p], 1)

            SMALL = HD - KEEP
            with dve.Fori(0, PAIRS) as i:
                for p in range(2):
                    dve.wait_ge(s_h[p], 16 * i + 16)
                    dve.tensor_scalar(h[p][:, :, :], h[p][:, :, :], g[:, 2:3], QMAX, ALU.mult,
                                      ALU.min).then_inc(s_h1[p], 1)
                for p in range(2):
                    dve.wait_ge(s_h1[p], i + 1)
                    dve.tensor_scalar(h[p][:, :, :], h[p][:, :, :], -QMAX - 1.0, MAGIC, ALU.max,
                                      ALU.add).then_inc(s_h2[p], 1)
                for p in range(2):
                    dve.wait_ge(s_kvc[p], i + 1)
                    dve.scalar_tensor_tensor(kl[p][:, 0, :], kvc[p][:, 0:D], -0.01, kvc[p][:, 0:D],
                                             ALU.mult, ALU.max, accum_out=ks[p][:, 0:1]).then_inc(s_kf[p], 1)
                for p in range(2):
                    dve.wait_ge(s_dn[p], i + 1)
                    dve.tensor_tensor(x3[p][:, :, :], m0[p][:, :].rearrange("p (t d) -> p t d", t=NT),
                                      srow[:, :, :].to_broadcast([P, NT, D]), ALU.mult).then_inc(s_xs[p], 1)
                    dve.wait_ge(s_xs[p], i + 1)
                    dve.wait_ge(s_x[p], 16 * i + 16)
                    dve.tensor_tensor(x3[p][:, :, :], x3[p][:, :, :], x[p][:, :, :], ALU.add).then_inc(s_x3[p], 1)
                    dve.wait_ge(s_x3[p], i + 1)
                    stat(x3[p], p, 0)
                for p in range(2):
                    normed(x3[p], p, 0)
                for p in range(2):
                    dve.wait_ge(s_kln[p], i + 1)
                    dve.tensor_scalar(kl[p][:, 0, :], kl[p][:, 0, :], K.focus[0:V, :], None,
                                      ALU.mult).then_inc(s_kf[p], 1)
                    dve.wait_ge(s_kf[p], 7 * i + 2)
                    dve.tensor_reduce(ks[p][:, 1:2], kl[p][:, 0, :], axis=AX_X, op=ALU.max,
                                      negate=True).then_inc(s_kf[p], 1)
                for p in range(2):
                    dve.wait_ge(s_vp[p], i + 1)
                    dve.tensor_tensor(vs[p][:, :, :, 0:HD],
                                      m0[p][:, :].rearrange("p (t h e) -> p t h e", t=NT, h=H),
                                      K.bv[:, :, :].rearrange("p o (h e) -> p o h e", h=H)
                                      .to_broadcast([P, NT, H, HD]), ALU.add).then_inc(s_vs[p], 1)
                def biased(p, n, bank, product, bias):
                    dve.wait_ge(product[p], i + 1)
                    dve.tensor_tensor(qf[p][:, :, :], bank[p][:, :].rearrange("p (t d) -> p t d", t=NT),
                                      bias[:, :, :].to_broadcast([P, NT, D]), ALU.add).then_inc(s_qb[p], 1)

                def copies(p, n, stack, twice, one):
                    sl = stack[:, :, :, 0:MR].rearrange("p t h (s e) -> p (t h) s e", e=HD)
                    if n:
                        dve.wait_ge(s_p1[p], 2 * i + 2)
                    else:
                        dve.wait_ge(s_p1[p], 2 * i + 1)
                    dve.tensor_copy(sl[:, :, twice, :], sl[:, :, 0:1, :].to_broadcast([P, NT * H, 2, HD])).then_inc(s_sk[p], 1)
                    dve.wait_ge(s_p2[p], 2 * i + n + 1)
                    dve.tensor_copy(sl[:, :, one[0], :], sl[:, :, one[1], :]).then_inc(s_sk[p], 1)

                def stack_out(p, n, dst):
                    for c in (0, 2):
                        dve.wait_ge(s_st[p], 8 * i + 4 * n + c + 1)
                        dve.tensor_copy(dst[p][:, 4 * c:4 * c + 4, :], m0[p][:, :].bitcast(BF16)).then_inc(s_qe0[p], 1)

                for p in range(2):
                    biased(p, 0, m1, s_qp, K.bq)
                for p in range(2):
                    copies(p, 0, Qs[p], slice(1, 3), (4, 3))
                dve.wait_ge(s_p3[0], 2 * i + 1)
                biased(0, 1, m0, s_kp, K.bk)
                stack_out(0, 0, QS)
                copies(0, 1, Ks, slice(3, 6, 2), (4, 1))
                dve.wait_ge(s_p3[1], 2 * i + 1)
                biased(1, 1, m0, s_kp, K.bk)
                stack_out(1, 0, QS)
                stack_out(0, 1, KS)
                copies(1, 1, Ks, slice(3, 6, 2), (4, 1))
                stack_out(1, 1, KS)
                for p in range(2):
                    dve.wait_ge(s_ke[p], i + 1)
                    dve.scalar_tensor_tensor(kk[p][:, :, :], ke[p][:, :, :].bitcast(I32), -16,
                                             K.rank[0:V, :, :], ALU.bitwise_and,
                                             ALU.bitwise_or).then_inc(s_kf[p], 1)
                    dve.reciprocal(ks[p][:, 2:3], ks[p][:, 2:3]).then_inc(s_kf[p], 1)
                    dve.tensor_scalar(ks[p][:, 0:1], ks[p][:, 0:1], 1.0 / D, EPS, ALU.mult,
                                      ALU.add).then_inc(s_kf[p], 1)
                for p in range(2):
                    dve.wait_ge(s_kf[p], 7 * i + 6)
                    dve.memset(idle[p][:, :], 0.0)
                    for hh in range(H):
                        last = dve.max(kt[p][:, hh, :], kk[p][:, 0, hh * HD:(hh + 1) * HD].bitcast(F32))
                    last.then_inc(s_kf[p], 1)
                for p in range(2):
                    dve.wait_ge(s_kf[p], 7 * i + 7)
                    dve.tensor_tensor(kl[p][:, 0, :].rearrange("p (h e) -> p h e", h=H),
                                      kk[p][:, 0, :].bitcast(F32).rearrange("p (h e) -> p h e", h=H),
                                      kt[p][:, :, SMALL - 1:SMALL].to_broadcast([V, H, HD]),
                                      ALU.is_lt).then_inc(s_KV[p], 1)
                    dve.tensor_scalar(ks[p][:, 3:4], ks[p][:, 2:3], ks[p][:, 0:1], None, ALU.mult).then_inc(s_KV[p], 1)
                for p in range(2):
                    dve.wait_ge(s_KV[p], 5 * i + 2)
                    dve.scalar_tensor_tensor(ke[p][:, 0, :], kl[p][:, 0, :], ks[p][:, 3:4], ke[p][:, 0, :],
                                             ALU.mult, ALU.mult).then_inc(s_KV[p], 1)
                for p in range(2):
                    for u in range(STEPS):
                        n = p * STEPS + u
                        dve.wait_ge(s_s1[u % 2], STEPS * i + n // 2 + 1)
                        dve.tensor_reduce(mr[p][:, :, 2 * u:2 * u + 2].rearrange("p t h -> p h t"),
                                          S[u % 2][:, :].rearrange("p (h t s) -> p h t s", h=2, t=NT),
                                          axis=AX_X, op=ALU.max, negate=True).then_inc(s_mx[u % 2], 1)
                    for r in range(2):
                        dve.wait_ge(s_mx[r], STEPS * i + 4 * p + 4)
                    mcol = [Qs[p][:, :, :, MR + a] for a in range(3)]
                    dve.tensor_copy(mcol[0], mr[p][:, :, :]).then_inc(s_mr[p], 1)
                    dve.wait_ge(s_mr[p], 5 * i + 1)
                    dve.tensor_tensor(mr[p][:, :, :], mr[p][:, :, :], mcol[0], ALU.subtract).then_inc(s_mr[p], 1)
                    dve.wait_ge(s_mr[p], 5 * i + 2)
                    dve.tensor_copy(mcol[1], mr[p][:, :, :]).then_inc(s_mr[p], 1)
                    dve.wait_ge(s_mr[p], 5 * i + 3)
                    dve.tensor_tensor(mr[p][:, :, :], mr[p][:, :, :], mcol[1], ALU.subtract).then_inc(s_mr[p], 1)
                    dve.wait_ge(s_mr[p], 5 * i + 4)
                    dve.tensor_copy(mcol[2], mr[p][:, :, :]).then_inc(s_mr[p], 1)
                for p in range(2):
                    dve.wait_ge(s_ob[p], i + 1)
                    ob = [b[p][:, :].rearrange("p (h r) -> p h r", r=32) for b in (m0, m1)]
                    for t in range(NT):
                        dve.reciprocal(ro[p][:, t, :], ob[t][:, :, HD]).then_inc(s_ro[p], 1)
                    dve.wait_ge(s_ro[p], 2 * i + 2)
                    for t in range(NT):
                        dve.tensor_tensor(o[p][:, t, :].rearrange("p (h e) -> p h e", h=H), ob[t][:, :, 0:HD],
                                          ro[p][:, t, :].unsqueeze(2).to_broadcast([P, H, HD]),
                                          ALU.mult).then_inc(s_o[p], 1)
                for p in range(2):
                    dve.wait_ge(s_pr[p], 3 * i + 1)
                    dve.wait_ge(s_xb[p], 2 * i + 1)
                    dve.tensor_tensor(x4[p][:, :, :], m1[p][:, :].rearrange("p (t d) -> p t d", t=NT),
                                      xb[p][:, :, :], ALU.add).then_inc(s_x4[p], 1)
                    dve.wait_ge(s_x4[p], i + 1)
                    stat(x4[p], p, 1)
                for p in range(2):
                    normed(x4[p], p, 1)
                for p in range(2):
                    dve.wait_ge(s_qe[p], 3 * i + 1)
                    for t in range(NT):
                        dve.scalar_tensor_tensor(o[p][:, t, :], qe[p][:, t, :], -0.01, qe[p][:, t, :],
                                                 ALU.mult, ALU.max, accum_out=qs[p][:, 0, t:t + 1]).then_inc(s_qf[p], 1)
                for p in range(2):
                    dve.wait_ge(s_kv[p], i + 1)
                    for k in range(ND):
                        dve.tensor_tensor(KV[p][:, k, 0:P].rearrange("p (h e) -> p h e", e=HD),
                                          m0[p][:, k * 256:k * 256 + P].rearrange("p (h e) -> p h e", e=HD),
                                          K.blocks[:, :, :], ALU.mult)
                        last = dve.tensor_tensor(KV[p][:, k, P:KW],
                                                 m0[p][:, k * 256 + P:k * 256 + P + 1].to_broadcast([P, P // HD]),
                                                 K.heads[:, :, 0], ALU.mult)
                    last.then_inc(s_KV[p], 2)
                for p in range(2):
                    dve.wait_ge(s_qln[p], i + 1)
                    dve.tensor_scalar(o[p][:, :, :], o[p][:, :, :], K.focus[:, :], None, ALU.mult).then_inc(s_qf[p], 1)
                    dve.wait_ge(s_qf[p], 9 * i + 3)
                    dve.tensor_reduce(qs[p][:, 1, :], o[p][:, :, :], axis=AX_X, op=ALU.max,
                                      negate=True).then_inc(s_qf[p], 1)
                for p in range(2):
                    dve.wait_ge(s_qe[p], 3 * i + 3)
                    dve.scalar_tensor_tensor(qk[p][:, :, :], qe[p][:, :, :].bitcast(I32), -16,
                                             K.rank[:, :, :].to_broadcast([P, NT, D]), ALU.bitwise_and,
                                             ALU.bitwise_or).then_inc(s_qf[p], 1)
                    dve.reciprocal(qs[p][:, 2, :], qs[p][:, 2, :]).then_inc(s_qf[p], 1)
                    dve.tensor_scalar(qs[p][:, 0, :], qs[p][:, 0, :], 1.0 / D, EPS, ALU.mult,
                                      ALU.add).then_inc(s_qf[p], 1)
                for p in range(2):
                    dve.wait_ge(s_qf[p], 9 * i + 7)
                    dve.memset(idle[p][:, :], 0.0)
                    for t in range(NT):
                        for hh in range(H):
                            dve.max(qt[p][:, t * H + hh, :], qk[p][:, t, hh * HD:(hh + 1) * HD].bitcast(F32))
                    dve.tensor_tensor(qs[p][:, 3, :], qs[p][:, 2, :], qs[p][:, 0, :], ALU.mult).then_inc(s_qf[p], 1)
                for p in range(2):
                    dve.wait_ge(s_qf[p], 9 * i + 8)
                    dve.tensor_tensor(o[p][:, :, :].rearrange("p t (h e) -> p (t h) e", h=H),
                                      qk[p][:, :, :].bitcast(F32).rearrange("p t (h e) -> p (t h) e", h=H),
                                      qt[p][:, :, SMALL - 1:SMALL].to_broadcast([P, NT * H, HD]),
                                      ALU.is_lt).then_inc(s_qf[p], 1)
                    dve.wait_ge(s_qf[p], 9 * i + 9)
                    for t in range(NT):
                        dve.scalar_tensor_tensor(qe[p][:, t, :], o[p][:, t, :], qs[p][:, 3, t:t + 1],
                                                 qe[p][:, t, :], ALU.mult, ALU.mult).then_inc(s_o[p], 1)
                for p in range(2):
                    dve.wait_ge(s_y[p], i + 1)
                    yb = [b[p][:, :].rearrange("p (k c) -> p k c", k=ND) for b in (m1, m0)]
                    for t in range(NT):
                        dve.tensor_scalar(rz[p][:, t, :, :], yb[t][:, :, P:KW], EPS, None,
                                          ALU.add).then_inc(s_z[p], 1)
                    dve.wait_ge(s_z[p], 3 * i + 2)
                    dve.reciprocal(rz[p][:, :, :, :], rz[p][:, :, :, :]).then_inc(s_z[p], 1)
                    dve.wait_ge(s_z[p], 3 * i + 3)
                    for t in range(NT):
                        dve.tensor_tensor(o[p][:, t, :].rearrange("p (k h e) -> p k h e", k=ND, e=HD),
                                          yb[t][:, :, 0:P].rearrange("p k (h e) -> p k h e", e=HD),
                                          rz[p][:, t, :, :].unsqueeze(3).to_broadcast([P, ND, P // HD, HD]),
                                          ALU.mult).then_inc(s_yn[p], 1)
                for p in range(2):
                    dve.wait_ge(s_pr[p], 3 * i + 2)
                    dve.wait_ge(s_xb[p], 2 * i + 1)
                    dve.tensor_tensor(x3[p][:, :, :], m1[p][:, :].rearrange("p (t d) -> p t d", t=NT),
                                      x4[p][:, :, :], ALU.add).then_inc(s_x5[p], 1)
                    dve.wait_ge(s_x5[p], i + 1)
                    stat(x3[p], p, 2)
                for p in range(2):
                    normed(x3[p], p, 2)
                for p in range(2):
                    dve.wait_ge(s_pr[p], 3 * i + 3)
                    dve.wait_ge(s_xb[p], 2 * i + 2)
                    dve.wait_ge(s_out[p], 16 * i)
                    dve.tensor_tensor(xo[p][:, :, :], m1[p][:, :].rearrange("p (t d) -> p t d", t=NT),
                                      xb[p][:, :, :], ALU.add).then_inc(s_x6[p], 1)

        @block.tensor
        def _(pe):
            def turn(p, bank, src):
                for k in range(ND):
                    for t in range(NT):
                        last = pe.transpose(bank[p][:, k * T + t * P:k * T + (t + 1) * P],
                                            src[p][:, t, k * P:(k + 1) * P], K.ident[:, :])
                last.then_inc(s_tr[p], 1)

            def project(bank, p, w):
                for t in range(NT):
                    for k in range(ND):
                        last = pe.matmul(bank[p][:, t * D:(t + 1) * D], xT[p][:, k, t * P:(t + 1) * P],
                                         w[:, k, :], start=k == 0, stop=k == ND - 1)
                return last

            def turn_stack(p, n, stack):
                for c in range(4):
                    if c >= 2:
                        pe.wait_ge((s_qe0, s_qe1)[c % 2][p], 4 * i + 2 * n + 1)
                    for hh in range(4):
                        for t in range(NT):
                            last = pe.transpose((m0, m1)[c % 2][p][:, :].bitcast(BF16)
                                                [:, hh * T + t * P:hh * T + (t + 1) * P],
                                                stack[:, t, 4 * c + hh, :], K.identb[:, :])
                    last.then_inc(s_st[p], 1)

            with pe.Fori(0, PAIRS) as i:
                for p in range(2):
                    pe.wait_ge(s_cx[p], 16 * i + 16)
                    pe.wait_ge(s_x6[p], i)
                    for k in range(ND):
                        last = pe.transpose(m1[p][:, k * V:(k + 1) * V], cx[p][:, k * P:(k + 1) * P],
                                            K.ident[0:V, 0:V])
                    last.then_inc(s_ctr[p], 1)
                for p in range(2):
                    pe.wait_ge(s_cT[p], i + 1)
                    for k in range(ND):
                        last = pe.matmul(m1[p][0:V, :], cT[p][:, k, :], K.Xkv[:, k, :], start=k == 0,
                                         stop=k == ND - 1)
                    last.then_inc(s_ckv[p], 1)
                for p in range(2):
                    pe.wait_ge(s_hq[p], i + 1)
                    for t in range(NT):
                        for j in range(NI):
                            last = pe.matmul(m0[p][:, t * D:(t + 1) * D], hq[p][:, j, t * P:(t + 1) * P],
                                             K.wd[:, j, :], start=j == 0, stop=j == NI - 1)
                    last.then_inc(s_dn[p], 1)
                for p in range(2):
                    pe.wait_ge(s_xn[p], 6 * i + 2)
                    pe.wait_ge(s_kvc[p], i + 1)
                    turn(p, m1, xn)
                for p in range(2):
                    pe.wait_ge(s_xT[p], TURNS * i + 1)
                    project(m0, p, K.Wv).then_inc(s_vp[p], 1)
                    project(m1, p, K.Wq).then_inc(s_qp[p], 1)
                for p in range(2):
                    pe.wait_ge(s_vs[p], i + 1)
                    project(m0, p, K.Wk).then_inc(s_kp[p], 1)
                for p in range(2):
                    pe.wait_ge(s_qb[p], 2 * i + 2)
                    pe.wait_ge(s_p3[p], 2 * i + 1)
                    pe.wait_ge(s_sk[p], 4 * i + 2)
                    turn_stack(p, 0, Qs[p])
                for p in range(2):
                    pe.wait_ge(s_p3[p], 2 * i + 2)
                    pe.wait_ge(s_sk[p], 4 * i + 4)
                    pe.wait_ge(s_qe0[p], 4 * i + 2)
                    pe.wait_ge(s_qe1[p], 4 * i + 2)
                    turn_stack(p, 1, Ks)
                for p in range(2):
                    pe.wait_ge(s_qe0[p], 4 * i + 4)
                    pe.wait_ge(s_qe1[p], 4 * i + 4)
                    for u in range(STEPS):
                        n = p * STEPS + u
                        gg, r = u // 2, u % 2
                        if n < 2:
                            pe.wait_ge(s_ex[r], STEPS * i)
                        else:
                            pe.wait_ge(s_mx[r], STEPS * i + n // 2)
                        for a in range(2):
                            for t in range(NT):
                                last = pe.matmul(S[r][:, a * 512 + t * T:a * 512 + (t + 1) * T],
                                                 QS[p][:, 2 * u + a, t * P:(t + 1) * P], KS[p][:, 2 * u + a, :],
                                                 start=True, stop=True)
                        last.then_inc(s_s1[r], 1)
                for p in range(2):
                    pe.wait_ge(s_mr[p], 5 * i + 5)
                    for c in range(4):
                        if c >= 2:
                            pe.wait_ge(s_qm[p], 4 * i + c - 1)
                        for hh in range(4):
                            for t in range(NT):
                                last = pe.transpose((m0, m1)[c % 2][p][MR:P, :].bitcast(BF16)
                                                    [:, hh * T + t * P:hh * T + (t + 1) * P],
                                                    Qs[p][:, t, 4 * c + hh, MR:P], K.identb[:, :])
                        last.then_inc(s_mt[p], 1)

                def weigh(n):
                    p, u = n // STEPS, n % STEPS
                    gg, r = u // 2, u % 2
                    pe.wait_ge(s_ex[r], STEPS * i + n // 2 + 1)
                    for a in range(2):
                        j = 2 * r + a
                        for t in range(NT):
                            last = pe.matmul((m0, m1)[gg // 2][p][32 * j:32 * j + 32, (gg % 2) * T:(gg % 2 + 1) * T],
                                             vs[p][:, t, 4 * gg + j, :], E[n % NE][:, a, t, :],
                                             start=t == 0, stop=t == NT - 1, skip_group_check=True)
                    last.then_inc(s_av[n % NE], 1)
                    if u == STEPS - 1:
                        pe.wait_ge(s_av[n % NE], 4 * i + n // NE + 1)
                        pe.nop().then_inc(s_ao[p], 1)

                for n in range(2 * STEPS + 1):
                    if n < 2 * STEPS:
                        p, u = n // STEPS, n % STEPS
                        gg, r = u // 2, u % 2
                        if u == 0:
                            pe.wait_ge(s_qm[p], 4 * i + 4)
                        if n < 2:
                            pe.wait_ge(s_mx[r], STEPS * i + STEPS)
                        else:
                            pe.wait_ge(s_ex[r], STEPS * i + n // 2)
                        for a in range(2):
                            for t in range(NT):
                                last = pe.matmul(S[r][:, a * 512 + t * T:a * 512 + (t + 1) * T],
                                                 KS[p][:, 2 * u + a, t * P:(t + 1) * P], QS[p][:, 2 * u + a, :],
                                                 start=True, stop=True)
                        last.then_inc(s_s2[r], 1)
                    if n >= 1:
                        weigh(n - 1)
                for p in range(2):
                    pe.wait_ge(s_oT[p], 2 * i + 2)
                    for t in range(NT):
                        for gg in range(4):
                            last = pe.transpose((m0, m1)[t][p][:, gg * P:(gg + 1) * P],
                                                oT[p][:, gg, t * P:(t + 1) * P], K.ident[:, :])
                    last.then_inc(s_ob[p], 1)
                for p in range(2):
                    pe.wait_ge(s_o[p], 4 * i + 2)
                    turn(p, m0, o)
                for p in range(2):
                    pe.wait_ge(s_xT[p], TURNS * i + 2)
                    project(m1, p, K.Wp).then_inc(s_pr[p], 1)
                for p in range(2):
                    pe.wait_ge(s_xn[p], 6 * i + 4)
                    turn(p, m0, xn)
                for p in range(2):
                    pe.wait_ge(s_xT[p], TURNS * i + 3)
                    project(m1, p, K.Xq).then_inc(s_xq[p], 1)
                    pe.wait_ge(s_KV[p], 5 * i + 3)
                    for k in range(ND):
                        pe.matmul(m0[p][:, k * 256:k * 256 + P], ke[p][:, 0, k * P:(k + 1) * P],
                                  kvc[p][:, D + k * P:D + (k + 1) * P], start=True, stop=True)
                        last = pe.matmul(m0[p][:, k * 256 + P:k * 256 + P + 1], ke[p][:, 0, k * P:(k + 1) * P],
                                         K.one77[0:V, :], start=True, stop=True)
                    last.then_inc(s_kv[p], 1)
                for p in range(2):
                    pe.wait_ge(s_o[p], 4 * i + 4)
                    pe.wait_ge(s_KV[p], 5 * i + 5)
                    turn(p, m0, qe)
                for p in range(2):
                    pe.wait_ge(s_xT[p], TURNS * i + 4)
                    for t in range(NT):
                        for k in range(ND):
                            last = pe.matmul((m1, m0)[t][p][:, k * 256:k * 256 + KW],
                                             xT[p][:, k, t * P:(t + 1) * P], KV[p][:, k, :], start=True, stop=True)
                    last.then_inc(s_y[p], 1)
                for p in range(2):
                    pe.wait_ge(s_yn[p], 2 * i + 2)
                    turn(p, m0, o)
                for p in range(2):
                    pe.wait_ge(s_xT[p], TURNS * i + 5)
                    project(m1, p, K.Xp).then_inc(s_pr[p], 1)
                for p in range(2):
                    pe.wait_ge(s_xn[p], 6 * i + 6)
                    turn(p, m0, xn)
                for p in range(2):
                    pe.wait_ge(s_xT[p], TURNS * i + 6)
                    project(m1, p, K.M).then_inc(s_pr[p], 1)


def clear_semaphores(nc, numbers):
    with nc.Block() as block:
        @block.gpsimd
        def _(pool):
            pool.sem_clear(numbers)


class Kept:
    pass


def keep_weights(sb, K):
    K.hpeak = sb("hpeak", [P, 1])
    K.Wq = sb("Wq", [P, ND, D])
    K.Wk = sb("Wk", [P, ND, D])
    K.Wv = sb("Wv", [P, ND, D])
    K.Wp = sb("Wp", [P, ND, D])
    K.bq = sb("bq", [P, 1, D])
    K.bk = sb("bk", [P, 1, D])
    K.bv = sb("bv", [P, 1, D])
    K.bp = sb("bp", [P, 1, D])
    K.bf = sb("bf", [P, 1, D])
    K.Xq = sb("Xq", [P, ND, D])
    K.Xkv = sb("Xkv", [P, ND, 2 * D])
    K.Xp = sb("Xp", [P, ND, D])
    K.M = sb("M", [P, ND, D])
    K.wg = sb("wg", [P, ND, I], BF16)
    K.wu = sb("wu", [P, ND, I], BF16)
    K.wd = sb("wd", [P, NI, D], BF16)
    K.sgate = sb("sgate", [P, NI])
    K.sup = sb("sup", [P, NI])
    K.sdown = sb("sdown", [P, ND])
    K.srep = sb("srep", [P, ND, P])
    K.srow = sb("srow", [P, 1, D])
    K.clip = sb("clip", [P, 2])
    K.cexp = sb("cexp", [P, 2])
    K.csig = sb("csig", [P, 2])
    K.focus = sb("focus", [P, 1])
    K.rank = sb("rank", [P, 1, D], I32)
    K.magic = sb("magic", [P, 1])
    K.eps = sb("eps", [P, 1])
    K.one77 = sb("one77", [P, 1])
    K.heads = sb("heads", [P, P // HD, 1])
    K.blocks = sb("blocks", [P, P // HD, HD])


def build(nc, A, out):
    x2 = nc.dram_tensor("x2_scratch", (B, T, D), F32, kind="Internal").ap()
    xn3 = nc.dram_tensor("xn3_scratch", (B, T, D), F32, kind="Internal").ap()
    hs = nc.dram_tensor("h_scratch", (B, P, NI * T), F32, kind="Internal").ap()
    numbers = range(min(nc.free_semaphores), max(nc.free_semaphores) + 1)
    with ExitStack() as ctx:
        def sb(name, shape, dt=F32):
            return ctx.enter_context(nc.sbuf_tensor("k_" + name, shape, dt))

        K = Kept()
        K.ident = sb("ident", [P, P])
        K.identb = sb("identb", [P, P], BF16)
        K.peak = sb("peak", [P, 1])
        with nc.semaphore("ident_made") as s_id, nc.Block() as block:
            @block.gpsimd
            def _(pool):
                pool.memset(K.ident[:, :], 0.0).then_inc(s_id, 1)
                pool.wait_ge(s_id, 1)
                pool.affine_select(out=K.ident[:, :], in_=K.ident[:, :], compare_op=ALU.not_equal, fill=1.0,
                                   base=0, pattern=[[-1, P]], channel_multiplier=1).then_inc(s_id, 1)
                pool.wait_ge(s_id, 2)
                pool.tensor_copy(K.identb[:, :], K.ident[:, :]).then_inc(s_id, 1)
                pool.wait_ge(s_id, 3)
        clear_semaphores(nc, numbers)
        phase_attention(nc, A, x2, xn3, K.ident, K.peak)
        keep_weights(sb, K)
        clear_semaphores(nc, numbers)
        phase_weights(nc, A, K)
        clear_semaphores(nc, numbers)
        phase_gate_up(nc, K, xn3, hs)
        clear_semaphores(nc, numbers)
        phase_tail(nc, A, K, x2, hs, out)


def kernel(**inputs):
    import numpy as np
    import concourse.bacc as bacc
    from concourse.bass_utils import run_bass_kernel_spmd

    nc = bacc.Bacc("TRN2", target_bir_lowering=False, num_devices=1)
    arrays, A = {}, {}
    for name, a in inputs.items():
        a = np.ascontiguousarray(a)
        if a.ndim == 0:
            a = a.reshape(1)
        arrays["in_" + name] = a
        A[name] = nc.dram_tensor("in_" + name, a.shape, mybir.dt.from_np(a.dtype), kind="ExternalInput").ap()
    turns = np.outer(np.arange(D), np.arange(D)) % D * (2 * np.pi / D)
    arrays["in_dft"] = np.stack([np.cos(turns), np.sin(turns), -np.sin(turns)]).astype(np.float32)
    A["dft"] = nc.dram_tensor("in_dft", (3, D, D), F32, kind="ExternalInput").ap()
    rank = (HD - 1 - np.arange(D) % HD).astype(np.int64) - 2 ** 31
    arrays["in_rank"] = rank.astype(np.int32)
    A["rank"] = nc.dram_tensor("in_rank", (D,), I32, kind="ExternalInput").ap()
    out = nc.dram_tensor("out_0", (B, T, D), F32, kind="ExternalOutput").ap()
    build(nc, A, out)
    r = run_bass_kernel_spmd(nc, [arrays], core_ids=[0])
    return r.results[0]["out_0"]
```
